# Optimizing a Trainium2 kernel written in Bass

```python
import numpy as np
import jax
import jax.numpy as jnp

def _softmax(x, axis=-1):
    return jax.nn.softmax(x, axis=axis)

def _gelu(x):
    return jax.nn.gelu(x, approximate=True)

def _silu(x):
    return jax.nn.silu(x)

def _sigmoid(x):
    return jax.nn.sigmoid(x)

def _layernorm(x, axis=-1, eps=1e-05):
    m = jnp.mean(x, axis=axis, keepdims=True)
    v = jnp.var(x, axis=axis, keepdims=True)
    return (x - m) / jnp.sqrt(v + eps)

def _scatter_add(tgt, idx, src, axis=0):
    return tgt.at[idx].add(src)

def _segment_sum(src, seg, n):
    return jax.ops.segment_sum(src, seg, n)
kernel_name = 'mk_gnn_resnorm_d4_gnn_r64_fa9f28'

def setup_inputs(seed: int=0):
    np.random.seed(seed)
    _w = jnp.asarray

    def _rec_inputs():
        import jax
        import jax.numpy as jnp
        _gk = jax.random.key(seed)
        x = -0.0005121 + 1.001 * jax.random.normal(jax.random.fold_in(_gk, 1), (100000, 64), jnp.float32)
        src = jax.random.randint(jax.random.fold_in(_gk, 2), (50000,), 0, 100000, jnp.int32)
        dst = jax.random.randint(jax.random.fold_in(_gk, 3), (50000,), 0, 100000, jnp.int32)
        _o = jnp.argsort(dst, stable=True)
        src = src[_o]
        dst = dst[_o]
        return (x, src, dst)
    x, src, dst = _rec_inputs()

    def _L0_gnn_setup():
        import jax, jax.numpy as jnp
        import numpy as np
        N = 50000
        D = 64
        E = 12500
        key = jax.random.key(seed)
        k1, k2, k3, k4 = jax.random.split(key, 4)
        f = jax.random.normal(k1, (N, D), dtype=jnp.float32)
        norm = jax.random.uniform(k2, (N, 1), dtype=jnp.float32)
        src = jax.random.randint(k3, (E,), 0, N, dtype=jnp.int64)
        dst = jax.random.randint(k4, (E,), 0, N, dtype=jnp.int64)
        return {'f': f, 'norm': norm, 'src': src, 'dst': dst, 'num_nodes': N}
    _L0_gnn_all = _L0_gnn_setup()
    _L0_gnn_in = {k: v for k, v in _L0_gnn_all.items() if k in ()}
    del _L0_gnn_all

    def _L1_gnn_setup():
        import jax, jax.numpy as jnp
        import numpy as np
        N_NODES = 100000
        key = jax.random.key(seed)
        ks = jax.random.split(key, 7)
        feat = jax.random.normal(ks[0], (N_NODES, 64), dtype=jnp.float32)
        W_lin = jax.random.normal(ks[1], (64, 64), dtype=jnp.float32) * 0.1
        b_lin = jax.random.normal(ks[2], (64,), dtype=jnp.float32) * 0.1
        W_rot = jax.random.normal(ks[3], (64, 64), dtype=jnp.float32) * 0.1
        b_rot = jax.random.normal(ks[4], (64,), dtype=jnp.float32) * 0.1
        src = jax.random.randint(ks[5], (15625,), 0, N_NODES, dtype=jnp.int64)
        dst = jax.random.randint(ks[6], (15625,), 0, N_NODES, dtype=jnp.int64)
        return {'feat': feat, 'W_lin': W_lin, 'b_lin': b_lin, 'W_rot': W_rot, 'b_rot': b_rot, 'src': src, 'dst': dst}
    _L1_gnn_all = _L1_gnn_setup()
    _L1_gnn_in = {k: v for k, v in _L1_gnn_all.items() if k in ('W_lin', 'b_lin', 'W_rot', 'b_rot')}
    del _L1_gnn_all

    def _L2_gnn_setup():
        import jax, jax.numpy as jnp
        import numpy as np
        N = 100000
        E = 15625
        D = 64
        H = 64
        O = 64

        def _lin_init(key, fan_in, fan_out):
            k1, k2 = jax.random.split(key)
            s = 1.0 / np.sqrt(fan_in)
            W = jax.random.uniform(k1, (fan_in, fan_out), jnp.float32, -s, s)
            b = jax.random.uniform(k2, (fan_out,), jnp.float32, -s, s)
            return (W, b)

        def _graphconv_left(x, s, d, n):
            deg = jax.ops.segment_sum(jnp.ones_like(s, x.dtype), s, num_segments=n)
            deg = jnp.maximum(deg, 1.0)
            msg = (x / deg[:, None])[s]
            return jax.ops.segment_sum(msg, d, num_segments=n)

        def _sage_layer(x, s, d, n, W, b, use_activation):
            agg = _graphconv_left(x, s, d, n)
            h = jnp.concatenate([x, agg], axis=1) @ W + b
            return jax.nn.relu(h) if use_activation else h
        key = jax.random.key(seed)
        ks = jax.random.split(key, 6)
        x = jax.random.normal(ks[0], (N, D), jnp.float32)
        src = jax.random.randint(ks[1], (E,), 0, N)
        dst = jax.random.randint(ks[2], (E,), 0, N)
        W1, b1 = _lin_init(ks[3], 2 * D, H)
        W2, b2 = _lin_init(ks[4], 2 * H, H)
        W3, b3 = _lin_init(ks[5], 2 * H, O)
        return {'x': x, 'src': src, 'dst': dst, 'W1': W1, 'b1': b1, 'W2': W2, 'b2': b2, 'W3': W3, 'b3': b3}
    _L2_gnn_all = _L2_gnn_setup()
    _L2_gnn_in = {k: v for k, v in _L2_gnn_all.items() if k in ('W1', 'b1', 'W2', 'b2', 'W3', 'b3')}
    del _L2_gnn_all

    def _L3_gnn_setup():
        import jax, jax.numpy as jnp
        import numpy as np
        N_NODES, N_EDGES, D = (50000, 1250000, 64)
        N_LAYERS = 3
        key = jax.random.key(seed)
        ks = jax.random.split(key, 6)
        sc = 1.0 / np.sqrt(D)
        return {'in_feat': jax.random.normal(ks[0], (N_NODES, D), jnp.float32), 'src': jax.random.randint(ks[1], (N_EDGES,), 0, N_NODES, dtype=jnp.int32), 'dst': jax.random.randint(ks[2], (N_EDGES,), 0, N_NODES, dtype=jnp.int32), 'W_pool': jax.random.normal(ks[3], (N_LAYERS, D, D), jnp.float32) * sc, 'b_pool': jnp.zeros((N_LAYERS, D), jnp.float32), 'W_self': jax.random.normal(ks[4], (N_LAYERS, D, D), jnp.float32) * sc, 'W_neigh': jax.random.normal(ks[5], (N_LAYERS, D, D), jnp.float32) * sc, 'bias': jnp.zeros((N_LAYERS, D), jnp.float32)}
    _L3_gnn_all = _L3_gnn_setup()
    _L3_gnn_in = {k: v for k, v in _L3_gnn_all.items() if k in ('W_pool', 'b_pool', 'W_self', 'W_neigh', 'bias')}
    del _L3_gnn_all
    return {'x': x, 'src': src, 'dst': dst, 'L1_gnn_W_lin': _L1_gnn_in['W_lin'], 'L1_gnn_b_lin': _L1_gnn_in['b_lin'], 'L1_gnn_W_rot': _L1_gnn_in['W_rot'], 'L1_gnn_b_rot': _L1_gnn_in['b_rot'], 'L2_gnn_W1': _L2_gnn_in['W1'], 'L2_gnn_b1': _L2_gnn_in['b1'], 'L2_gnn_W2': _L2_gnn_in['W2'], 'L2_gnn_b2': _L2_gnn_in['b2'], 'L2_gnn_W3': _L2_gnn_in['W3'], 'L2_gnn_b3': _L2_gnn_in['b3'], 'L3_gnn_W_pool': _L3_gnn_in['W_pool'], 'L3_gnn_b_pool': _L3_gnn_in['b_pool'], 'L3_gnn_W_self': _L3_gnn_in['W_self'], 'L3_gnn_W_neigh': _L3_gnn_in['W_neigh'], 'L3_gnn_bias': _L3_gnn_in['bias']}

def reference(x, src, dst, L1_gnn_W_lin, L1_gnn_b_lin, L1_gnn_W_rot, L1_gnn_b_rot, L2_gnn_W1, L2_gnn_b1, L2_gnn_W2, L2_gnn_b2, L2_gnn_W3, L2_gnn_b3, L3_gnn_W_pool, L3_gnn_b_pool, L3_gnn_W_self, L3_gnn_W_neigh, L3_gnn_bias):
    import jax
    import jax.numpy as jnp

    def _L0_gnn_ref(f, norm, src, dst, num_nodes):
        import jax, jax.numpy as jnp
        import numpy as np
        N = 50000
        D = 64
        E = 12500
        w = norm[src] * norm[dst]
        h = f[src] * w
        s = jax.ops.segment_max(h, dst, num_segments=num_nodes)
        has_in = jax.ops.segment_sum(jnp.ones_like(dst, dtype=jnp.float32), dst, num_segments=num_nodes) > 0
        return jnp.where(has_in[:, None], s, 0.0)

    def _L1_gnn_ref(feat, W_lin, b_lin, W_rot, b_rot, src, dst):
        import jax, jax.numpy as jnp
        import numpy as np
        N_NODES = 100000
        agg = jax.ops.segment_sum(feat[src], dst, num_segments=feat.shape[0])
        rst = agg @ W_lin.T + b_lin
        rst = rst + (feat @ W_rot.T + b_rot)
        return rst

    def _L2_gnn_ref(x, src, dst, W1, b1, W2, b2, W3, b3):
        import jax, jax.numpy as jnp
        import numpy as np
        N = 100000
        E = 15625
        D = 64
        H = 64
        O = 64

        def _lin_init(key, fan_in, fan_out):
            k1, k2 = jax.random.split(key)
            s = 1.0 / np.sqrt(fan_in)
            W = jax.random.uniform(k1, (fan_in, fan_out), jnp.float32, -s, s)
            b = jax.random.uniform(k2, (fan_out,), jnp.float32, -s, s)
            return (W, b)

        def _graphconv_left(x, s, d, n):
            deg = jax.ops.segment_sum(jnp.ones_like(s, x.dtype), s, num_segments=n)
            deg = jnp.maximum(deg, 1.0)
            msg = (x / deg[:, None])[s]
            return jax.ops.segment_sum(msg, d, num_segments=n)

        def _sage_layer(x, s, d, n, W, b, use_activation):
            agg = _graphconv_left(x, s, d, n)
            h = jnp.concatenate([x, agg], axis=1) @ W + b
            return jax.nn.relu(h) if use_activation else h
        n = x.shape[0]
        usrc = jnp.concatenate([src, dst])
        udst = jnp.concatenate([dst, src])
        x = _sage_layer(x, src, dst, n, W1, b1, True)
        x = _sage_layer(x, dst, src, n, W2, b2, True)
        x = _sage_layer(x, usrc, udst, n, W3, b3, False)
        return x

    def _L3_gnn_ref(in_feat, src, dst, W_pool, b_pool, W_self, W_neigh, bias):
        import jax, jax.numpy as jnp
        import numpy as np
        N_NODES, N_EDGES, D = (50000, 1250000, 64)
        N_LAYERS = 3
        n = in_feat.shape[0]
        h = in_feat
        for l in range(N_LAYERS):
            m = jax.nn.relu(h[src] @ W_pool[l] + b_pool[l])
            agg = jax.ops.segment_max(m, dst, num_segments=n)
            agg = jnp.where(jnp.isfinite(agg), agg, 0.0)
            h = h @ W_self[l] + agg @ W_neigh[l] + bias[l]
            if l < N_LAYERS - 1:
                h = jax.nn.relu(h)
        return h
    deg = jnp.maximum(jax.ops.segment_sum(jnp.ones(dst.shape, jnp.float32), dst, num_segments=100000), 1.0)
    deg_isqrt = deg ** (-0.5)
    x = _layernorm(x + _L0_gnn_ref(x, deg_isqrt[:, None], src, dst, 100000), axis=-1)
    x = _layernorm(x + _L1_gnn_ref(x, L1_gnn_W_lin, L1_gnn_b_lin, L1_gnn_W_rot, L1_gnn_b_rot, src, dst), axis=-1)
    x = _layernorm(x + _L2_gnn_ref(x, src, dst, L2_gnn_W1, L2_gnn_b1, L2_gnn_W2, L2_gnn_b2, L2_gnn_W3, L2_gnn_b3), axis=-1)
    x = _layernorm(x + _L3_gnn_ref(x, src, dst, L3_gnn_W_pool, L3_gnn_b_pool, L3_gnn_W_self, L3_gnn_W_neigh, L3_gnn_bias), axis=-1)
    return x

_drawn_inputs = setup_inputs


def setup_inputs(seed=0):
    import zlib

    import numpy as np

    out = dict(_drawn_inputs(seed))
    spreads = {'L3_gnn_b_pool': (0.0, 0.1), 'L3_gnn_bias': (0.0, 0.1)}
    factors = {'L2_gnn_b1': 8.0, 'L2_gnn_b2': 3.545}
    for name, (base, spread) in spreads.items():
        noise = np.random.default_rng([zlib.crc32(name.encode()), seed]).standard_normal(out[name].shape)
        drawn = base * np.exp(spread * noise) if base else spread * noise
        out[name] = jnp.asarray(drawn.astype(out[name].dtype))
    for name, factor in factors.items():
        out[name] = (out[name] * factor).astype(out[name].dtype)
    return out
```

```python
import concourse.bass as bass
from concourse import mybir
from contextlib import ExitStack

P = 128
D = 64
NODES, EDGES = 100000, 50000
PAIRS = 49
GROUPS = 2 * PAIRS
ET, NT = 4, 8
EG, NG = ET * P, NT * P
EDGES_PAD = GROUPS * EG
NODES_PAD = GROUPS * NG
SPARE = NODES_PAD - P
COLS = GROUPS * ET
COLS_BUF = COLS + 2 * ET
HI = NODES_PAD // P
HALF = HI // 2
HT = HI // 7
INFO = 4
XW = D + INFO
EPS = 1e-5
FAR = -3.0e38
CREDIT = 2

F32, I32, U32, BF16, F16 = (mybir.dt.float32, mybir.dt.int32, mybir.dt.uint32, mybir.dt.bfloat16, mybir.dt.float16)
ALU, ACT, AX = mybir.AluOpType, mybir.ActivationFunctionType, mybir.AxisListType


class Phase:

    def __init__(self, name, fwd=None, fwd_idx=None, scale=None, rev=None, rev_scale=None, rev_sum=None, side=None,
                 msg=None, agg=None, keep=None, w_agg=None, w_self=None, bias=None, self_rows=None, resid=None,
                 after=None, out=None, nodes=None, node_self=None, node_q=None, node_w=None, node_wq=None,
                 node_bias=None, node_resid=None, node_after=None, node_out=None, scatter=False):
        self.name = name
        self.fwd, self.fwd_idx, self.scale = fwd, fwd_idx, scale
        self.rev, self.rev_scale, self.rev_sum = rev, rev_scale, rev_sum
        self.side = side
        self.msg = msg
        self.agg = agg
        self.keep = keep
        self.w_agg, self.w_self, self.bias = w_agg, w_self, bias
        self.self_rows, self.resid, self.after, self.out = self_rows, resid, after, out
        self.nodes, self.node_self, self.node_q, self.node_w, self.node_wq = nodes, node_self, node_q, node_w, node_wq
        self.node_bias, self.node_resid, self.node_after, self.node_out = node_bias, node_resid, node_after, node_out
        self.scatter = scatter


class Step:

    def __init__(self, sem, phases, more=0):
        self.sem, self.each, self.at = sem, GROUPS + more, {p: n for n, p in enumerate(phases)}

    def after(self, ph, g):
        return self.sem, CREDIT + self.at[ph] * self.each + g + 1


class Arrivals:

    def __init__(self, sems, phases, each=1, primed=False):
        self.sems, self.at, self.each, self.primed = sems, {p: n for n, p in enumerate(phases)}, each, primed

    def after(self, ph, i, b):
        return self.sems[b], 16 * self.each * (self.at[ph] * PAIRS + i + 1) + 16 * self.primed

    def before(self, ph, i, b):
        return self.sems[b], 16 * self.each * (self.at[ph] * PAIRS + i) + 16 * self.primed

    def all(self, ph):
        return [self.after(ph, PAIRS - 1, b) for b in range(2)]


def wait(eng, *pairs):
    for sem, value in pairs:
        eng.wait_ge(sem, value)


def settle(eng, pace):
    eng.sem_inc(pace, 1)


def paced(eng, pace, *pairs):
    for pair in pairs:
        wait(eng, pair)
        settle(eng, pace)


def skewed(eng, first, second, third=None):
    third = third or (lambda i, b: None)
    first(0, 0)
    third(0, 0)
    with eng.Fori(0, PAIRS - 1) as i:
        for nxt, now in (((i, 1), (i, 0)), ((i + 1, 0), (i, 1))):
            first(*nxt)
            second(*now)
            third(*nxt)
    first(PAIRS - 1, 1)
    second(PAIRS - 1, 0)
    third(PAIRS - 1, 1)
    second(PAIRS - 1, 1)


def graph_kernel(nc, x, src_e, dst_e, next_e, src_tiles, dst_rows, prev_rows, w_lin, b_lin, w_rot, b_rot,
                 w1, b1, w2, b2, w3, b3, w_pool, b_pool, w_self, w_neigh, bias, out):
    ctx = ExitStack()

    def dram(name, shape, dt=F32):
        return nc.dram_tensor(name, shape, dt).ap()

    STATES = ["T1", "T2", "H1", "H2", "T3", "G1", "G2"]
    table = {n: dram(n, [NODES_PAD + EDGES_PAD, D]) for n in STATES}
    table["XH"] = dram("XH", [NODES_PAD, XW])
    table["XA"] = dram("XA", [EDGES_PAD, D])
    table["FA"] = dram("FA", [EDGES_PAD, D])
    table["S1"] = dram("S1", [NODES_PAD, D])
    table["S2"] = dram("S2", [NODES_PAD, D])
    F3 = dram("F3", [GROUPS, D, EG])
    info_d = dram("info_d", [NODES_PAD, INFO])
    same_d = dram("same_d", [GROUPS, EG])
    far_d = dram("far_d", [GROUPS, EG])
    prime_d = dram("prime_d", [16, 16])
    side_of = {"same": same_d, "far": far_d}

    def edge_rows(name):
        t = table[name]
        if name in STATES:
            t = t[NODES_PAD:NODES_PAD + EDGES_PAD, :]
        return t.rearrange("(g p j) d -> g p (j d)", p=P, j=ET)

    def node_rows(name):
        t = {"x": x, "out": out}.get(name)
        t = table[name][0:NODES_PAD, :] if t is None else t
        return t.rearrange("(g p j) d -> g p (j d)", p=P, j=NT)

    LN_PHASES = ("l0", "l1", "l2c", "l3c")
    PHASES = [
        Phase("own", fwd="XH", fwd_idx="dst", after="copy", out="XA", nodes="ln", node_self="x", node_out="T1"),
        Phase("l0", fwd="XH", fwd_idx="src", scale="norm", side="far", agg=(ALU.add, ALU.max), w_agg="eye",
              resid="XA", after="norm_ln", out="T1", nodes="mm", node_self="T1", node_w="rot", node_bias="l1",
              node_resid="self", node_after="ln", node_out="T2"),
        Phase("l1", fwd="T1", fwd_idx="src_own", side="same", agg=(ALU.mult, ALU.add), w_agg="lin", w_self="rot",
              self_rows="T1", resid="self", bias="l1", after="ln", out="T2", nodes="mm", node_self="T2", node_w="w1a",
              node_bias="b1", node_after="relu", node_out="H1"),
        Phase("l2a", fwd="T2", fwd_idx="src_own", scale="inv_out", side="same", agg=(ALU.mult, ALU.add), w_agg="w1b",
              w_self="w1a", self_rows="T2", bias="b1", after="relu", out="H1"),
        Phase("sum1", rev="H1", rev_scale="inv_in", rev_sum="S1"),
        Phase("l2b", fwd="S1", fwd_idx="dst", agg="pass", w_agg="w2b", w_self="w2a", self_rows="H1", bias="b2",
              after="relu", out="H2", nodes="mm", node_self="H1", node_q="S1", node_w="w2a", node_wq="w2b",
              node_bias="b2", node_after="relu", node_out="H2"),
        Phase("sum2", fwd="H2", fwd_idx="src_own", scale="inv_all", side="same", agg=(ALU.mult, ALU.add), keep="F3",
              rev="H2", rev_scale="inv_all_dst", rev_sum="S2"),
        Phase("l2c", fwd="S2", fwd_idx="dst", side="F3", agg="add", w_agg="w3b", w_self="w3a", self_rows="H2",
              resid="T2", bias="b3", after="ln", out="T3", nodes="mm", node_self="H2", node_q="S2", node_w="w3a",
              node_wq="w3b", node_bias="b3", node_resid="T2", node_after="ln", node_out="T3"),
    ]
    for n, (before, name) in enumerate((("T3", "G1"), ("G1", "G2"), ("G2", "FA"))):
        last = n == 2
        PHASES.append(Phase(
            "l3" + "abc"[n], fwd=before, fwd_idx="src_own", side="same", msg=n, agg=(ALU.mult, ALU.max),
            w_agg=f"neigh{n}", w_self=f"self{n}", self_rows=before, resid="T3" if last else None, bias=f"bias{n}",
            after="ln" if last else "relu", out=name, nodes="mm", node_self=before, node_w=f"self{n}",
            node_bias=f"bias{n}", node_resid="T3" if last else None, node_after="ln" if last else "relu",
            node_out="out" if last else name))
    PHASES.append(Phase("scatter", scatter=True))
    assert LN_PHASES == tuple(p.name for p in PHASES if p.after in ("ln", "norm_ln"))

    def which(test):
        return [p.name for p in PHASES if test(p)]

    with ctx:
        def sb(name, shape, dt=F32):
            return ctx.enter_context(nc.sbuf_tensor(name, shape, dt))

        def sem(name):
            return ctx.enter_context(nc.semaphore(name))

        bank = [ctx.enter_context(nc.psum_tensor(f"bank{n}", [P, 512], F32)) for n in range(8)]

        eye = sb("eye", [P, P])
        tri = sb("tri", [P, P])
        ones = sb("ones", [P, P])
        earlier = sb("earlier", [P, P])
        idx_all = {n: sb(f"idx_{n}", [P, COLS_BUF], U32) for n in ("dst", "src", "src_own", "dst_own", "sum", "out")}
        src_f = sb("src_f", [P, COLS_BUF])
        info_src = sb("info_src", [P, GROUPS, ET, INFO])
        info_dst = sb("info_dst", [P, GROUPS, ET, INFO])
        inv_in = sb("inv_in", [P, GROUPS, ET])
        spare = sb("spare", [P, 1])
        eps = sb("eps", [P, 1])
        zero = sb("zero", [P, 1024])

        W_SMALL = {"lin": w_lin, "w1b": w1[D:2 * D, :], "w2b": w2[D:2 * D, :], "w3b": w3[D:2 * D, :]}
        W_PAIR = {"rot": w_rot, "w1a": w1[0:D, :], "w2a": w2[0:D, :], "w2b": w2[D:2 * D, :], "w3a": w3[0:D, :],
                  "w3b": w3[D:2 * D, :]}
        for n in range(3):
            W_SMALL[f"neigh{n}"] = w_neigh[n]
            W_SMALL[f"pool{n}"] = w_pool[n]
            W_PAIR[f"self{n}"] = w_self[n]
        small = {n: sb(f"small_{n}", [D, D]) for n in W_SMALL}
        pair = {n: sb(f"pair_{n}", [P, P]) for n in W_PAIR}
        B_ROWS = {"l1": b_lin, "rot": b_rot, "b1": b1, "b2": b2, "b3": b3}
        for n in range(3):
            B_ROWS[f"bias{n}"] = bias[n:n + 1, :]
        brow = {n: sb(f"brow_{n}", [P, D]) for n in B_ROWS}
        b_pool_col = sb("b_pool_col", [D, 3])

        two = range(2)
        ib = [sb(f"ib{b}", [P, ET], U32) for b in two]
        ib2 = [sb(f"ib2{b}", [P, ET], U32) for b in two]
        ib3 = [sb(f"ib3{b}", [P, ET], U32) for b in two]
        got = [sb(f"got{b}", [P, ET, XW]) for b in two]
        scaled = [sb(f"scaled{b}", [P, ET, D]) for b in two]
        got2 = [sb(f"got2{b}", [P, ET, D]) for b in two]
        scaled2 = [sb(f"scaled2{b}", [P, ET, D]) for b in two]
        src_row = [sb(f"src_row{b}", [P, ET, P], I32) for b in two]
        equal = [sb(f"equal{b}", [P, ET, P]) for b in two]
        summed = [sb(f"summed{b}", [P, ET, D]) for b in two]
        side = [sb(f"side{b}", [D, EG]) for b in two]
        got_t = [sb(f"got_t{b}", [D, EG]) for b in two]
        msg_t = [sb(f"msg_t{b}", [D, EG]) for b in two]
        agg_t = [sb(f"agg_t{b}", [D, EG]) for b in two]
        rows = [sb(f"rows{b}", [P, ET, D]) for b in two]
        resid = [sb(f"resid{b}", [P, ET, D]) for b in two]
        rows_t = [sb(f"rows_t{b}", [P, 2 * P]) for b in two]
        res = [sb(f"res{b}", [P, ET, D]) for b in two]
        nrows = [sb(f"nrows{b}", [P, NT, D]) for b in two]
        nq = [sb(f"nq{b}", [P, NT, D]) for b in two]
        nresid = [sb(f"nresid{b}", [P, NT, D]) for b in two]
        nrows_t = [sb(f"nrows_t{b}", [P, 4 * P]) for b in two]
        nq_t = [sb(f"nq_t{b}", [P, 4 * P]) for b in two]
        nres = [sb(f"nres{b}", [P, NT, D]) for b in two]
        sq = sb("sq", [P, ET, D])
        nsq = sb("nsq", [P, NT, D])
        stat = {k: sb(f"stat_{k}", [P, ET]) for k in ("mean", "neg", "var", "std", "rstd")}
        nstat = {k: sb(f"nstat_{k}", [P, NT]) for k in ("mean", "neg", "var", "std", "rstd")}

        fwd_ph = which(lambda p: p.fwd)
        rev_ph = which(lambda p: p.rev)
        scat_ph = which(lambda p: p.scatter)
        edge_ph = which(lambda p: p.after and p.after != "copy")
        out_ph = which(lambda p: p.after)
        self_ph = which(lambda p: p.self_rows)
        node_ph = which(lambda p: p.nodes)
        nmm_ph = which(lambda p: p.nodes == "mm")
        nq_ph = which(lambda p: p.node_q)
        ln_ph = which(lambda p: p.after in ("ln", "norm_ln"))
        nln_ph = which(lambda p: p.nodes and (p.nodes == "ln" or p.node_after == "ln"))
        t_ph = which(lambda p: p.agg)
        a_loaded_ph = which(lambda p: p.self_rows or p.resid)
        steps = {}

        def step(name, phases):
            steps[name] = Step(sem(name), phases, 2 if name in ("idx_ready", "idx2_ready") else 0)

        every = [p.name for p in PHASES]
        for name, phases in (
                ("idx_ready", fwd_ph + scat_ph), ("idx2_ready", rev_ph), ("idx3_ready", rev_ph),
                ("got_used", which(lambda p: p.scale or p.after == "copy")), ("got2_used", rev_ph),
                ("equal_ready", rev_ph), ("counted", ["l2a"]), ("eq_l2a", ["l2a"]), ("dup_l2a", ["l2a"]),
                ("dup1_l2a", ["l2a"]), ("spread_l2a", ["l2a"]),
                ("got_turned", t_ph), ("rows_turned", self_ph), ("nrows_turned", nmm_ph), ("nq_turned", nq_ph),
                ("msg_summed", which(lambda p: p.msg is not None)), ("deduped", rev_ph),
                ("out_summed", edge_ph), ("nout_summed", nmm_ph),
                ("got_t_ready", t_ph), ("rows_t_ready", self_ph), ("nrows_t_ready", nmm_ph), ("nq_t_ready", nq_ph),
                ("msg_ready", which(lambda p: p.msg is not None)), ("summed_ready", rev_ph),
                ("std_ready", ln_ph), ("nstd_ready", nln_ph), ("agg_ready", which(lambda p: p.agg and p.agg != "pass")),
                ("psum_out_used", edge_ph), ("psum_nout_used", nmm_ph),
                ("resid_added", which(lambda p: p.resid)), ("nresid_added", which(lambda p: p.nodes == "mm" and p.node_resid)),
                ("mean_sum", ln_ph), ("mean_ready", ln_ph), ("centred", ln_ph), ("squared", ln_ph), ("var_ready", ln_ph),
                ("rstd_ready", ln_ph), ("res_ready", out_ph),
                ("nmean_sum", nln_ph), ("nmean_ready", nln_ph), ("ncentred", nln_ph), ("nsquared", nln_ph),
                ("nvar_ready", nln_ph), ("nrstd_ready", nln_ph), ("nres_ready", node_ph)):
            step(name, phases)
        s = steps

        def pairof(name):
            return [sem(f"{name}{b}") for b in two]

        early, late = every[:6], every[6:]
        gathered_1 = Arrivals(pairof("gathered_a"), [p for p in fwd_ph if p in early], ET)
        gathered_2 = Arrivals(pairof("gathered_b"), [p for p in fwd_ph if p in late], ET)

        def gathered(ph):
            return gathered_1 if ph in early else gathered_2

        gathered_rev = Arrivals(pairof("gathered_rev"), rev_ph, ET)
        scattered = Arrivals(pairof("scattered"), scat_ph, ET)
        side_in = Arrivals(pairof("side_in"), which(lambda p: p.side))
        srow_in = Arrivals(pairof("srow_in"), which(lambda p: p.rev or p.name == "l2a"))
        rows_in = Arrivals(pairof("rows_in"), self_ph)
        resid_in = Arrivals(pairof("resid_in"), which(lambda p: p.resid and p.resid != "self" or p.scatter))
        nrows_in = Arrivals(pairof("nrows_in"), node_ph)
        nq_in = Arrivals(pairof("nq_in"), nq_ph)
        nresid_in = Arrivals(pairof("nresid_in"), which(lambda p: p.nodes == "mm" and p.node_resid not in (None, "self")))
        stored = Arrivals(pairof("stored"), which(lambda p: p.out or p.keep), primed=True)
        nstored = Arrivals(pairof("nstored"), node_ph, primed=True)
        added = sem("added")
        consts_in, zeroed, prep_in = sem("consts_in"), sem("zeroed"), sem("prep_in")
        pool_built, dve_chain, act_chain, pe_chain = sem("pool_built"), sem("dve_chain"), sem("act_chain"), sem("pe_chain")
        hot_ready, hot_used = sem("hot_ready"), sem("hot_used")
        info_out, xh_in, xh_ready, xh_out = sem("info_out"), pairof("xh_in"), sem("xh_ready"), pairof("xh_out")
        masks_out, masks_ready, info_ready = sem("masks_out"), sem("masks_ready"), sem("info_ready")

        def barrier(eng, n):
            if n == 0:
                wait(eng, (xh_out[0], 16 * PAIRS), (xh_out[1], 16 * PAIRS), (masks_out, 32), (zeroed, 32 * GROUPS))
                return
            before = PHASES[n - 1]
            if before.name in stored.at:
                wait(eng, *stored.all(before.name))
            if before.nodes:
                wait(eng, *nstored.all(before.name))
            if before.rev:
                wait(eng, (added, 16 * COLS * (rev_ph.index(before.name) + 1)))

        hot_lo = [[sb(f"hot_lo{k}{b}", [P, P], BF16) for b in two] for k in two]
        hot_hi = [[sb(f"hot_hi{k}{b}", [P, HI], BF16) for b in two] for k in two]
        count_up = sb("count_up", [P, HI], F16)
        count_i = sb("count_i", [P, HI], I32)
        node_i = sb("node_i", [P, HI], I32)
        edge_i = [sb(f"edge_i{k}", [P, COLS], I32) for k in range(3)]
        part_i = sb("part_i", [P, 1], I32)
        lo_f = [sb(f"lo_f{k}", [P, COLS]) for k in two]
        hi_f = [sb(f"hi_f{k}", [P, COLS]) for k in two]
        deg = [sb(f"deg{k}", [P, HI]) for k in two]
        field = [sb(f"field{k}", [P, HI]) for k in range(INFO)]
        tmp = sb("tmp", [P, HI])
        info_t = sb("info_t", [HT, 7, P, INFO])
        xh = [sb(f"xh{b}", [P, NT, XW]) for b in two]
        xh_info = [sb(f"xh_info{b}", [P, NT * INFO]) for b in two]
        drow = sb("drow", [GROUPS, EG], I32)
        prow = sb("prow", [GROUPS, EG], I32)
        same = sb("same", [GROUPS, EG])
        far = sb("far", [GROUPS, EG])
        last_f = sb("last_f", [P, COLS])
        dst_f = sb("dst_f", [P, COLS])
        shifted = sb("shifted", [P, COLS], I32)
        prefix = sb("prefix", [P, HI])
        dup = sb("dup", [P, 3, ET])
        links, sp_pace, pool_pace, pe_pace = sem("links"), sem("sp_pace"), sem("pool_pace"), sem("pe_pace")

        block = ctx.enter_context(nc.Block())
        N_CONSTS = len(W_SMALL) + 2 * len(W_PAIR) + len(B_ROWS) + 1

        def scale_of(p, kind, g):
            ap = {"norm": info_src[:, g, :, 0], "inv_out": info_src[:, g, :, 1], "inv_all": info_src[:, g, :, 2],
                  "inv_all_dst": info_dst[:, g, :, 2], "inv_in": inv_in[:, g, :]}[kind]
            return ap.unsqueeze(2).to_broadcast([P, ET, D])

        @block.sync
        def _(sp):
            for name in steps:
                sp.sem_inc(steps[name].sem, CREDIT)
            for k, a in enumerate((src_e, dst_e, next_e)):
                sp.dma_start(edge_i[k][:, :], a).then_inc(prep_in, 16)
            sp.dma_start(drow[:, :], dst_rows).then_inc(prep_in, 16)
            sp.dma_start(prow[:, :], prev_rows).then_inc(prep_in, 16)
            paced(sp, sp_pace, (pool_built, 2))
            for name, w in W_SMALL.items():
                sp.dma_start(small[name][:, :], w).then_inc(consts_in, 16)
            for name, w in W_PAIR.items():
                for k in two:
                    sp.dma_start(pair[name][D * k:D * (k + 1), D * k:D * (k + 1)], w).then_inc(consts_in, 16)
            for name, v in B_ROWS.items():
                sp.dma_start(brow[name][:, :], v.to_broadcast([P, D])).then_inc(consts_in, 16)
            sp.dma_start(b_pool_col[:, :], b_pool).then_inc(consts_in, 16)
            for n, sm in enumerate(stored.sems + nstored.sems):
                sp.dma_start(prime_d[n:n + 1, :], zero[0:1, 0:16]).then_inc(sm, 16)
            with sp.Fori(0, GROUPS) as g:
                for name in ("S1", "S2"):
                    sp.dma_start(node_rows(name)[g], zero[:, 0:NT * D]).then_inc(zeroed, 16)
            paced(sp, sp_pace, (masks_ready, 1))
            sp.dma_start(same_d, same[:, :]).then_inc(masks_out, 16)
            sp.dma_start(far_d, far[:, :]).then_inc(masks_out, 16)
            paced(sp, sp_pace, (info_ready, 7))
            info_rows = info_d.rearrange("(k h l) f -> k h (l f)", k=7, l=P)
            for k in range(7):
                sp.dma_start(info_rows[k], info_t[:, k, :, :].rearrange("h l f -> h (l f)")).then_inc(info_out, 16)
            paced(sp, sp_pace, (info_out, 16 * 7))
            x_rows, xh_rows = node_rows("x"), node_rows("XH")
            info_in = info_d.rearrange("(g p j) f -> g p (j f)", p=P, j=NT)

            def load_xh(i, b):
                g = 2 * i + b
                if not isinstance(i, int) or i > 0:
                    paced(sp, sp_pace, (xh_out[b], 16 * i))
                sp.dma_start(xh[b][:, :, 0:D], x_rows[g].rearrange("p (j d) -> p j d", d=D)).then_inc(xh_in[b], 16)
                sp.dma_start(xh_info[b][:, :], info_in[g]).then_inc(xh_in[b], 16)

            def store_xh(i, b):
                g = 2 * i + b
                paced(sp, sp_pace, (xh_ready, g + 1))
                sp.dma_start(xh_rows[g], xh[b][:, :, :].rearrange("p j w -> p (j w)")).then_inc(xh_out[b], 16)

            load_xh(0, 0)
            load_xh(0, 1)
            store_xh(0, 0)
            with sp.Fori(1, PAIRS) as i:
                load_xh(i, 0)
                store_xh(i - 1, 1)
                load_xh(i, 1)
                store_xh(i, 0)
            store_xh(PAIRS - 1, 1)

            for n, p in enumerate(PHASES):
                ph = p.name
                barrier(sp, n)

                def load(i, b, p=p, ph=ph):
                    g = 2 * i + b
                    if p.scatter:
                        paced(sp, sp_pace, scattered.before(ph, i, b)) if not isinstance(i, int) or i > 0 else None
                        return
                    if p.rev or ph == "l2a":
                        paced(sp, sp_pace, s["equal_ready" if p.rev else "eq_l2a"].after(ph, g - 2))
                        sp.dma_start(src_row[b][:, :, :].rearrange("p j q -> p (j q)"),
                                     src_tiles[g].to_broadcast([P, EG])).then_inc(srow_in.sems[b], 16)
                    if p.side:
                        paced(sp, sp_pace, s["agg_ready"].after(ph, g - 2))
                        a = F3[g] if p.side == "F3" else side_of[p.side][bass.ds(g, 1), :].to_broadcast([D, EG])
                        sp.dma_start(side[b][:, :], a).then_inc(side_in.sems[b], 16)
                    if p.self_rows:
                        paced(sp, sp_pace, s["rows_turned"].after(ph, g - 2))
                        if p.resid == "self":
                            paced(sp, sp_pace, s["resid_added"].after(ph, g - 2))
                        sp.dma_start(rows[b][:, :, :].rearrange("p j d -> p (j d)"),
                                     edge_rows(p.self_rows)[g]).then_inc(rows_in.sems[b], 16)
                    if p.resid and p.resid != "self":
                        paced(sp, sp_pace, s["resid_added"].after(ph, g - 2))
                        sp.dma_start(resid[b][:, :, :].rearrange("p j d -> p (j d)"),
                                     edge_rows(p.resid)[g]).then_inc(resid_in.sems[b], 16)
                    if p.nodes:
                        if p.nodes == "mm":
                            paced(sp, sp_pace, s["nrows_turned"].after(ph, g - 2))
                            if p.node_resid == "self":
                                paced(sp, sp_pace, s["nresid_added"].after(ph, g - 2))
                        else:
                            paced(sp, sp_pace, s["ncentred"].after(ph, g - 2))
                        sp.dma_start(nrows[b][:, :, :].rearrange("p j d -> p (j d)"),
                                     node_rows(p.node_self)[g]).then_inc(nrows_in.sems[b], 16)
                        if p.node_q:
                            paced(sp, sp_pace, s["nq_turned"].after(ph, g - 2))
                            sp.dma_start(nq[b][:, :, :].rearrange("p j d -> p (j d)"),
                                         node_rows(p.node_q)[g]).then_inc(nq_in.sems[b], 16)
                        if p.node_resid not in (None, "self"):
                            paced(sp, sp_pace, s["nresid_added"].after(ph, g - 2))
                            sp.dma_start(nresid[b][:, :, :].rearrange("p j d -> p (j d)"),
                                         node_rows(p.node_resid)[g]).then_inc(nresid_in.sems[b], 16)

                def store(i, b, p=p, ph=ph):
                    g = 2 * i + b
                    if p.out:
                        paced(sp, sp_pace, s["res_ready"].after(ph, g))
                        sp.dma_start(edge_rows(p.out)[g], res[b][:, :, :].rearrange("p j d -> p (j d)")).then_inc(
                            stored.sems[b], 16)
                    if p.keep:
                        paced(sp, sp_pace, s["agg_ready"].after(ph, g))
                        sp.dma_start(F3[g], agg_t[b][:, :]).then_inc(stored.sems[b], 16)
                    if p.nodes:
                        paced(sp, sp_pace, s["nres_ready"].after(ph, g))
                        sp.dma_start(node_rows(p.node_out)[g],
                                     nres[b][:, :, :].rearrange("p j d -> p (j d)")).then_inc(nstored.sems[b], 16)

                if not p.scatter:
                    skewed(sp, load, store)
                else:
                    def load_res(i, b, ph=ph):
                        if not isinstance(i, int) or i > 0:
                            paced(sp, sp_pace, scattered.before(ph, i, b))
                        sp.dma_start(res[b][:, :, :].rearrange("p j d -> p (j d)"),
                                     edge_rows("FA")[2 * i + b]).then_inc(resid_in.sems[b], 16)
                    for b in two:
                        load_res(0, b)
                    with sp.Fori(1, PAIRS) as i:
                        for b in two:
                            load_res(i, b)
            paced(sp, sp_pace, *scattered.all("scatter"))

        @block.gpsimd
        def _(pool):
            nc.gpsimd.memset(zero[:, :], 0.0)
            nc.gpsimd.memset(ones[:, :], 1.0)
            for name in pair:
                nc.gpsimd.memset(pair[name][:, :], 0.0)
            nc.gpsimd.memset(eye[:, :], 0.0)
            nc.gpsimd.memset(agg_t[0][:, :], 0.0)
            nc.gpsimd.memset(agg_t[1][:, :], 0.0)
            nc.gpsimd.memset(eps[:, :], EPS).then_inc(pool_built, 1)
            pool.wait_ge(pool_built, 1)
            nc.gpsimd.affine_select(out=eye[:, :], in_=eye[:, :], compare_op=ALU.not_equal, fill=1.0, base=0,
                                    pattern=[[-1, P]], channel_multiplier=1)
            nc.gpsimd.affine_select(out=tri[:, :], in_=ones[:, :], compare_op=ALU.is_ge, fill=0.0, base=0,
                                    pattern=[[1, P]], channel_multiplier=-1)
            nc.gpsimd.affine_select(out=earlier[:, :], in_=ones[:, :], compare_op=ALU.is_gt, fill=0.0, base=0,
                                    pattern=[[-1, P]], channel_multiplier=1)
            nc.gpsimd.iota(count_i[:, :], pattern=[[1, HI]], base=0, channel_multiplier=0)
            nc.gpsimd.iota(node_i[:, :], pattern=[[P, HI]], base=0, channel_multiplier=1)
            nc.gpsimd.iota(part_i[:, :], pattern=[[0, 1]], base=SPARE, channel_multiplier=1).then_inc(pool_built, 1)

            for n, p in enumerate(PHASES):
                ph = p.name
                barrier(pool, n)

                def gather(i, b, p=p, ph=ph):
                    g = 2 * i + b
                    if p.fwd:
                        wait(pool, s["idx_ready"].after(ph, g))
                        if ph in s["got_used"].at:
                            wait(pool, s["got_used"].after(ph, g - 2))
                        else:
                            wait(pool, s["got_turned"].after(ph, g - 2))
                    if p.rev:
                        wait(pool, s["idx2_ready"].after(ph, g), s["got2_used"].after(ph, g - 2))
                    settle(pool, pool_pace)
                    width = XW if p.fwd == "XH" else D
                    for j in range(ET):
                        if p.fwd:
                            pool.indirect_dma_start(
                                got[b][:, j, 0:width], None, table[p.fwd],
                                bass.IndirectOffsetOnAxis(ib[b][:, j:j + 1], 0)).then_inc(gathered(ph).sems[b], 16)
                        if p.rev:
                            pool.indirect_dma_start(
                                got2[b][:, j, :], None, table[p.rev],
                                bass.IndirectOffsetOnAxis(ib2[b][:, j:j + 1], 0)).then_inc(gathered_rev.sems[b], 16)

                def put(i, b, p=p, ph=ph):
                    g = 2 * i + b
                    if p.rev:
                        wait(pool, s["summed_ready"].after(ph, g), s["idx3_ready"].after(ph, g))
                        for j in range(ET):
                            done = 16 * (COLS * rev_ph.index(ph) + ET * g + j)
                            if not isinstance(done, int) or done > 0:
                                pool.wait_ge(added, done)
                            settle(pool, pool_pace)
                            pool.indirect_dma_start(
                                table[p.rev_sum], bass.IndirectOffsetOnAxis(ib3[b][:, j:j + 1], 0),
                                summed[b][:, j, :], None, compute_op=ALU.add).then_inc(added, 16)

                if p.scatter:
                    def scatter(i, b, ph=ph):
                        g = 2 * i + b
                        wait(pool, s["idx_ready"].after(ph, g), resid_in.after(ph, i, b))
                        settle(pool, pool_pace)
                        for j in range(ET):
                            pool.indirect_dma_start(
                                out, bass.IndirectOffsetOnAxis(ib[b][:, j:j + 1], 0),
                                res[b][:, j, :], None, bounds_check=NODES_PAD - 1,
                                oob_is_err=False).then_inc(scattered.sems[b], 16)
                    with pool.Fori(0, PAIRS) as i:
                        for b in two:
                            scatter(i, b)
                elif p.rev:
                    gather(0, 0)
                    gather(0, 1)
                    put(0, 0)
                    with pool.Fori(1, PAIRS) as i:
                        gather(i, 0)
                        put(i - 1, 1)
                        gather(i, 1)
                        put(i, 0)
                    put(PAIRS - 1, 1)
                else:
                    with pool.Fori(0, PAIRS) as i:
                        for b in two:
                            gather(i, b)

        @block.tensor
        def _(pe):
            T = nc.tensor
            pe.wait_ge(pool_built, 2)
            wait(pe, (dve_chain, 1))
            for k in range(4):
                T.matmul(bank[k][:, 0:HALF], hot_lo[0][0][:, :], hot_hi[0][0][:, 0:HALF], start=True, stop=False,
                         skip_group_check=True)
            T.matmul(bank[4][:, 0:P], hot_lo[0][0][:, :], hot_lo[0][0][:, :], start=True,
                     stop=True).then_inc(hot_used, 2)
            with pe.Fori(0, COLS // 2) as i:
                for b in two:
                    pe.wait_ge(hot_ready, 2 * i + b + 1)
                    for k in two:
                        for h in two:
                            last = T.matmul(bank[2 * k + h][:, 0:HALF], hot_lo[k][b][:, :],
                                            hot_hi[k][b][:, h * HALF:(h + 1) * HALF], start=False, stop=False,
                                            skip_group_check=True)
                    last.then_inc(hot_used, 1)
            pe.wait_ge(hot_ready, COLS + 1)
            for k in range(4):
                last = T.matmul(bank[k][:, 0:HALF], hot_lo[0][0][:, :], hot_hi[0][0][:, 0:HALF], start=False, stop=True,
                                skip_group_check=True)
            last.then_inc(pe_chain, 1)
            pe.wait_ge(act_chain, 1)
            for h in two:
                T.matmul(bank[4 + h][:, 0:HALF], tri[:, :], deg[1][:, h * HALF:(h + 1) * HALF], start=True, stop=True)
            for h in two:
                last = T.matmul(bank[6 + h][:, 0:HALF], ones[:, :], deg[1][:, h * HALF:(h + 1) * HALF], start=True,
                                stop=True)
            last.then_inc(pe_chain, 1)
            pe.wait_ge(act_chain, 3)
            for k in range(7):
                if k >= 2:
                    pe.wait_ge(info_ready, k - 1)
                for f in range(INFO):
                    last = T.transpose(bank[k % 2][0:HT, f * P:(f + 1) * P], field[f][:, k * HT:(k + 1) * HT], eye[:, :])
                last.then_inc(pe_chain, 1)

            pe.wait_ge(consts_in, 16 * N_CONSTS)
            for n, p in enumerate(PHASES):
                ph = p.name

                def turn(i, b, p=p, ph=ph):
                    g = 2 * i + b
                    if p.agg:
                        if p.scale:
                            wait(pe, s["got_used"].after(ph, g))
                            a = scaled[b]
                        else:
                            wait(pe, gathered(ph).after(ph, i, b))
                            a = got[b]
                        wait(pe, s["got_t_ready"].after(ph, g - 2))
                        settle(pe, pe_pace)
                        for j in range(ET):
                            last = T.transpose(bank[b][0:D, j * P:(j + 1) * P], a[:, j, 0:D], eye[:, :])
                        last.then_inc(s["got_turned"].sem, 1)
                    if p.self_rows:
                        wait(pe, rows_in.after(ph, i, b), s["rows_t_ready"].after(ph, g - 1))
                        settle(pe, pe_pace)
                        for j in range(ET // 2):
                            last = T.transpose(bank[3][:, j * P:(j + 1) * P],
                                               rows[b][:, 2 * j:2 * j + 2, :].rearrange("p j d -> p (j d)"), eye[:, :])
                        last.then_inc(s["rows_turned"].sem, 1)
                    if p.nodes == "mm":
                        wait(pe, nrows_in.after(ph, i, b), s["nrows_t_ready"].after(ph, g - 1))
                        settle(pe, pe_pace)
                        for j in range(NT // 2):
                            last = T.transpose(bank[5][:, j * P:(j + 1) * P],
                                               nrows[b][:, 2 * j:2 * j + 2, :].rearrange("p j d -> p (j d)"), eye[:, :])
                        last.then_inc(s["nrows_turned"].sem, 1)
                    if p.node_q:
                        wait(pe, nq_in.after(ph, i, b), s["nq_t_ready"].after(ph, g - 1))
                        settle(pe, pe_pace)
                        for j in range(NT // 2):
                            last = T.transpose(bank[6][:, j * P:(j + 1) * P],
                                               nq[b][:, 2 * j:2 * j + 2, :].rearrange("p j d -> p (j d)"), eye[:, :])
                        last.then_inc(s["nq_turned"].sem, 1)

                def combine(i, b, p=p, ph=ph):
                    g = 2 * i + b
                    if p.after and p.after != "copy":
                        if p.agg == "pass":
                            wait(pe, s["got_t_ready"].after(ph, g))
                            a = got_t[b]
                        else:
                            wait(pe, s["agg_ready"].after(ph, g))
                            a = agg_t[b]
                        if p.self_rows:
                            wait(pe, s["rows_t_ready"].after(ph, g))
                        wait(pe, s["psum_out_used"].after(ph, g - 1))
                        settle(pe, pe_pace)
                        w = eye[0:D, 0:D] if p.w_agg == "eye" else small[p.w_agg][:, :]
                        a = a[:, :].rearrange("c (q j) -> c q j", j=ET)
                        for j in range(ET // 2):
                            if p.self_rows:
                                T.matmul(bank[4][:, j * P:(j + 1) * P], rows_t[b][:, j * P:(j + 1) * P],
                                         pair[p.w_self][:, :], start=True, stop=False, skip_group_check=True)
                            for k in (2 * j, 2 * j + 1):
                                last = T.matmul(bank[4][:, k * D:(k + 1) * D], a[:, :, k], w,
                                                start=not p.self_rows, stop=True, skip_group_check=True)
                        last.then_inc(s["out_summed"].sem, 1)
                    if p.nodes == "mm":
                        wait(pe, s["nrows_t_ready"].after(ph, g), s["psum_nout_used"].after(ph, g - 1))
                        if p.node_q:
                            wait(pe, s["nq_t_ready"].after(ph, g))
                        settle(pe, pe_pace)
                        for j in range(NT // 2):
                            cols = slice(j * P, (j + 1) * P)
                            last = T.matmul(bank[7][:, cols], nrows_t[b][:, cols], pair[p.node_w][:, :], start=True,
                                            stop=not p.node_q)
                            if p.node_q:
                                last = T.matmul(bank[7][:, cols], nq_t[b][:, cols], pair[p.node_wq][:, :], start=False,
                                                stop=True)
                        last.then_inc(s["nout_summed"].sem, 1)

                def message(i, b, p=p, ph=ph):
                    g = 2 * i + b
                    if p.msg is not None:
                        wait(pe, s["got_t_ready"].after(ph, g), s["msg_ready"].after(ph, g - 1))
                        settle(pe, pe_pace)
                        T.matmul(bank[2][0:D, :], small[f"pool{p.msg}"][:, :], got_t[b][:, :], start=True,
                                 stop=True).then_inc(s["msg_summed"].sem, 1)
                    if p.rev:
                        wait(pe, s["equal_ready"].after(ph, g), s["got2_used"].after(ph, g),
                             s["summed_ready"].after(ph, g - 1))
                        settle(pe, pe_pace)
                        for j in range(ET):
                            last = T.matmul(bank[2][:, j * D:(j + 1) * D], equal[b][:, j, :], scaled2[b][:, j, :],
                                            start=True, stop=True)
                        last.then_inc(s["deduped"].sem, 1)

                if p.name not in ("own", "scatter"):
                    skewed(pe, turn, combine, message)

        @block.scalar
        def _(act):
            A = nc.scalar
            act.wait_ge(pe_chain, 1)
            for k in two:
                for h in two:
                    last = A.copy(deg[k][:, h * HALF:(h + 1) * HALF], bank[2 * k + h][:, 0:HALF])
            last.then_inc(act_chain, 1)
            act.wait_ge(dve_chain, 2)
            act.wait_ge(pool_built, 2)
            A.activation(tmp[:, :], field[0][:, :], ACT.Sqrt).then_inc(act_chain, 1)
            act.wait_ge(dve_chain, 3)
            A.copy(eps[0:1, :], eps[0:1, :]).then_inc(act_chain, 1)
            for k in range(7):
                act.wait_ge(pe_chain, 3 + k)
                A.copy(info_t[:, k, :, :].rearrange("h l f -> h f l"),
                       bank[k % 2][0:HT, :].rearrange("h (f l) -> h f l", f=INFO)).then_inc(info_ready, 1)

            for n, p in enumerate(PHASES):
                ph = p.name

                def evacuate(i, b, p=p, ph=ph):
                    g = 2 * i + b
                    if p.agg:
                        reader = "msg_summed" if p.msg is not None else "out_summed" if p.agg == "pass" else "agg_ready"
                        wait(act, s["got_turned"].after(ph, g), s[reader].after(ph, g - 2))
                        A.copy(got_t[b][:, :].rearrange("c (q j) -> c j q", j=ET),
                               bank[b][0:D, :].rearrange("c (j q) -> c j q", j=ET)).then_inc(s["got_t_ready"].sem, 1)
                    if p.self_rows:
                        wait(act, s["rows_turned"].after(ph, g), s["out_summed"].after(ph, g - 2))
                        A.copy(rows_t[b][:, :], bank[3][:, 0:2 * P]).then_inc(s["rows_t_ready"].sem, 1)
                    if p.nodes == "mm":
                        wait(act, s["nrows_turned"].after(ph, g), s["nout_summed"].after(ph, g - 2))
                        A.copy(nrows_t[b][:, :], bank[5][:, :]).then_inc(s["nrows_t_ready"].sem, 1)
                    if p.node_q:
                        wait(act, s["nq_turned"].after(ph, g), s["nout_summed"].after(ph, g - 2))
                        A.copy(nq_t[b][:, :], bank[6][:, :]).then_inc(s["nq_t_ready"].sem, 1)

                def roots(i, b, p=p, ph=ph):
                    g = 2 * i + b
                    if ph in s["std_ready"].at:
                        wait(act, s["var_ready"].after(ph, g), s["rstd_ready"].after(ph, g - 1))
                        A.activation(stat["std"][:, :], stat["var"][:, :], ACT.Sqrt, bias=eps[:, 0:1],
                                     scale=1.0 / D).then_inc(s["std_ready"].sem, 1)
                    if ph in s["nstd_ready"].at:
                        wait(act, s["nvar_ready"].after(ph, g), s["nrstd_ready"].after(ph, g - 1))
                        A.activation(nstat["std"][:, :], nstat["var"][:, :], ACT.Sqrt, bias=eps[:, 0:1],
                                     scale=1.0 / D).then_inc(s["nstd_ready"].sem, 1)

                def message(i, b, p=p, ph=ph):
                    g = 2 * i + b
                    if p.msg is not None:
                        wait(act, s["msg_summed"].after(ph, g), s["agg_ready"].after(ph, g - 2))
                        A.activation(msg_t[b][:, :], bank[2][0:D, :], ACT.Relu,
                                     bias=b_pool_col[:, p.msg:p.msg + 1]).then_inc(s["msg_ready"].sem, 1)
                    if p.rev:
                        wait(act, s["deduped"].after(ph, g))
                        if not isinstance(i, int) or i > 0:
                            act.wait_ge(added, 16 * (COLS * rev_ph.index(ph) + ET * (g - 1)))
                        A.copy(summed[b][:, :, :].rearrange("p j d -> p (j d)"),
                               bank[2][:, 0:ET * D]).then_inc(s["summed_ready"].sem, 1)

                if p.name != "scatter":
                    skewed(act, evacuate, roots, message)

        @block.vector
        def _(dve):
            V = nc.vector
            link_count = [0]

            def link(ins):
                link_count[0] += 1
                ins.then_inc(links, 1)
                dve.wait_ge(links, link_count[0])

            V.memset(hot_lo[0][0][:, :], 0.0)
            for name in idx_all:
                V.memset(idx_all[name][:, COLS:COLS_BUF], 0)
            V.memset(hot_hi[0][0][:, :], 0.0).then_inc(dve_chain, 1)
            wait(dve, (prep_in, 16 * 5), (pool_built, 2))
            link(V.tensor_copy(count_up[:, :], count_i[:, :]))
            for k in two:
                link(V.tensor_scalar(shifted[:, :], edge_i[k][:, :], P - 1, None, ALU.bitwise_and))
                link(V.tensor_copy(lo_f[k][:, :], shifted[:, :]))
                link(V.tensor_scalar(shifted[:, :], edge_i[k][:, :], 7, None, ALU.arith_shift_right))
                link(V.tensor_copy(hi_f[k][:, :], shifted[:, :]))
            with dve.Fori(0, COLS // 2) as i:
                for b in two:
                    c = 2 * i + b
                    dve.wait_ge(hot_used, c + 1)
                    for k in two:
                        V.tensor_scalar(hot_lo[k][b][:, :], count_up[:, 0:P], lo_f[k][:, bass.ds(c, 1)], None,
                                        ALU.is_equal)
                        last = V.tensor_scalar(hot_hi[k][b][:, :], count_up[:, :], hi_f[k][:, bass.ds(c, 1)], None,
                                               ALU.is_equal)
                    last.then_inc(hot_ready, 1)
            dve.wait_ge(hot_used, COLS + 2)
            V.memset(hot_lo[0][0][:, :], 0.0).then_inc(hot_ready, 1)

            link(V.tensor_copy(idx_all["src"][:, 0:COLS], edge_i[0][:, :]))
            link(V.tensor_copy(idx_all["dst"][:, 0:COLS], edge_i[1][:, :]))
            link(V.tensor_copy(src_f[:, 0:COLS], edge_i[0][:, :]))
            link(V.tensor_copy(dst_f[:, :], edge_i[1][:, :]))
            link(V.tensor_tensor(last_f[:, :], edge_i[1][:, :], edge_i[2][:, :], ALU.not_equal))
            link(V.tensor_scalar(dst_f[:, :], dst_f[:, :], float(NODES_PAD), None, ALU.subtract))
            link(V.tensor_tensor(dst_f[:, :], dst_f[:, :], last_f[:, :], ALU.mult))
            link(V.tensor_scalar(idx_all["out"][:, 0:COLS], dst_f[:, :], float(NODES_PAD), None, ALU.add))
            link(V.tensor_copy(spare[:, :], part_i[:, :]))
            link(V.tensor_tensor(same[:, :], drow[:, :], prow[:, :], ALU.is_equal))
            V.tensor_scalar(far[:, :], same[:, :], 1.0, -FAR, ALU.subtract, ALU.mult).then_inc(masks_ready, 1)

            dve.wait_ge(act_chain, 1)
            V.tensor_scalar(field[0][:, :], deg[1][:, :], 1.0, None, ALU.max).then_inc(dve_chain, 1)
            link(V.tensor_scalar(field[1][:, :], deg[0][:, :], 1.0, None, ALU.max))
            link(V.reciprocal(field[1][:, :], field[1][:, :]))
            link(V.tensor_tensor(field[2][:, :], deg[0][:, :], deg[1][:, :], ALU.add))
            link(V.tensor_scalar(field[2][:, :], field[2][:, :], 1.0, None, ALU.max))
            link(V.reciprocal(field[2][:, :], field[2][:, :]))
            dve.wait_ge(pe_chain, 2)
            for h in two:
                cols = slice(h * HALF, (h + 1) * HALF)
                link(V.tensor_copy(prefix[:, cols], bank[6 + h][:, 0:HALF]))
            link(V.tensor_tensor_scan(field[3][:, :], prefix[:, :], zero[:, 0:HI], 0.0, ALU.add, ALU.add))
            link(V.tensor_tensor(field[3][:, :], field[3][:, :], prefix[:, :], ALU.subtract))
            for h in two:
                cols = slice(h * HALF, (h + 1) * HALF)
                link(V.tensor_tensor(field[3][:, cols], field[3][:, cols], bank[4 + h][:, 0:HALF], ALU.add))
            link(V.tensor_copy(prefix[:, :], node_i[:, :]))
            link(V.tensor_scalar(field[3][:, :], field[3][:, :], float(NODES_PAD - 1), None, ALU.add))
            link(V.tensor_tensor(field[3][:, :], field[3][:, :], prefix[:, :], ALU.subtract))
            link(V.tensor_scalar(deg[1][:, :], deg[1][:, :], 1.0, None, ALU.min))
            link(V.tensor_tensor(field[3][:, :], field[3][:, :], deg[1][:, :], ALU.mult))
            link(V.tensor_tensor(field[3][:, :], field[3][:, :], prefix[:, :], ALU.add))
            dve.wait_ge(act_chain, 2)
            V.reciprocal(field[0][:, :], tmp[:, :]).then_inc(dve_chain, 1)
            dve.wait_ge(consts_in, 16 * N_CONSTS)
            link(V.tensor_tensor(brow["l1"][:, :], brow["l1"][:, :], brow["rot"][:, :], ALU.add))
            with dve.Fori(0, PAIRS) as i:
                for b in two:
                    dve.wait_ge(xh_in[b], 32 * (i + 1))
                    V.tensor_copy(xh[b][:, :, D:XW],
                                  xh_info[b][:, :].rearrange("p (j f) -> p j f", f=INFO)).then_inc(xh_ready, 1)

            def bc(ap, n):
                return ap.unsqueeze(2).to_broadcast([P, n, D])

            for n, p in enumerate(PHASES):
                ph = p.name

                def fetch_idx(g, b, p=p, ph=ph):
                    cols = bass.ds(g * ET, ET)
                    if p.fwd or p.scatter:
                        V.tensor_copy(ib[b][:, :], idx_all["out" if p.scatter else p.fwd_idx][:, cols]).then_inc(
                            s["idx_ready"].sem, 1)
                    if p.rev:
                        V.tensor_copy(ib2[b][:, :], idx_all["dst_own"][:, cols]).then_inc(s["idx2_ready"].sem, 1)

                def receive(i, b, p=p, ph=ph):
                    g = 2 * i + b
                    if p.scatter:
                        wait(dve, scattered.after(ph, i, b))
                        fetch_idx(g + 2, b)
                        return
                    if p.fwd:
                        wait(dve, gathered(ph).after(ph, i, b))
                    if p.rev:
                        wait(dve, gathered_rev.after(ph, i, b))
                    fetch_idx(g + 2, b)
                    cols = bass.ds(g * ET, ET)
                    if p.fwd == "XH":
                        keep = info_dst if ph == "own" else info_src
                        V.tensor_copy(keep[:, g, :, :], got[b][:, :, D:XW])
                        V.tensor_copy(idx_all["dst_own" if ph == "own" else "src_own"][:, cols],
                                      got[b][:, :, XW - 1])
                        if ph == "own":
                            V.tensor_tensor(inv_in[:, g, :], got[b][:, :, D], got[b][:, :, D], ALU.mult)
                            wait(dve, stored.before(ph, i, b))
                            V.tensor_copy(res[b][:, :, :], got[b][:, :, 0:D]).then_inc(s["got_used"].sem, 1)
                            s_res = s["res_ready"]
                            dve.wait_ge(*s["got_used"].after(ph, g))
                            dve.sem_inc(s_res.sem, 1)
                    if p.scale:
                        wait(dve, s["got_turned"].after(ph, g - 2))
                        if p.scale == "norm":
                            f = got[b][:, :, D].unsqueeze(2).to_broadcast([P, ET, D])
                        else:
                            f = scale_of(p, p.scale, g)
                        V.tensor_tensor(scaled[b][:, :, :], got[b][:, :, 0:D], f, ALU.mult).then_inc(
                            s["got_used"].sem, 1)
                    if p.rev:
                        wait(dve, s["deduped"].after(ph, g - 2))
                        V.tensor_tensor(scaled2[b][:, :, :], got2[b][:, :, :], scale_of(p, p.rev_scale, g),
                                        ALU.mult).then_inc(s["got2_used"].sem, 1)
                        wait(dve, srow_in.after(ph, i, b))
                        V.tensor_tensor(equal[b][:, :, :], src_row[b][:, :, :],
                                        src_f[:, cols].unsqueeze(2).to_broadcast([P, ET, P]),
                                        ALU.is_equal).then_inc(s["equal_ready"].sem, 1)
                        if not isinstance(i, int) or i > 0:
                            dve.wait_ge(added, 16 * (COLS * rev_ph.index(ph) + ET * (g - 1)))
                        V.tensor_copy(ib3[b][:, :], idx_all["sum"][:, cols]).then_inc(s["idx3_ready"].sem, 1)
                    if ph == "l2a":
                        wait(dve, srow_in.after(ph, i, b))
                        V.tensor_tensor(equal[b][:, :, :], src_row[b][:, :, :],
                                        src_f[:, cols].unsqueeze(2).to_broadcast([P, ET, P]),
                                        ALU.is_equal).then_inc(s["eq_l2a"].sem, 1)
                        wait(dve, s["eq_l2a"].after(ph, g))
                        V.tensor_tensor(equal[b][:, :, :], equal[b][:, :, :],
                                        earlier[:, :].unsqueeze(1).to_broadcast([P, ET, P]),
                                        ALU.mult).then_inc(s["dup_l2a"].sem, 1)
                        wait(dve, s["dup_l2a"].after(ph, g))
                        V.tensor_reduce(dup[:, 0, :], equal[b][:, :, :], AX.X, ALU.max).then_inc(s["counted"].sem, 1)
                        wait(dve, s["counted"].after(ph, g))
                        V.tensor_scalar(dup[:, 1, :], src_f[:, cols], spare[:, 0:1], -1.0, ALU.subtract,
                                        ALU.mult).then_inc(s["dup1_l2a"].sem, 1)
                        wait(dve, s["dup1_l2a"].after(ph, g))
                        V.tensor_tensor(dup[:, 2, :], dup[:, 0, :], dup[:, 1, :], ALU.mult).then_inc(
                            s["spread_l2a"].sem, 1)
                        wait(dve, s["spread_l2a"].after(ph, g))
                        V.tensor_tensor(idx_all["sum"][:, cols], dup[:, 2, :], src_f[:, cols], ALU.add)

                def finish(i, b, p=p, ph=ph):
                    g = 2 * i + b
                    edges = bool(p.after and p.after != "copy")
                    nodes = bool(p.nodes)
                    o, no = res[b][:, :, :], nres[b][:, :, :]
                    if edges:
                        wait(dve, s["out_summed"].after(ph, g), stored.before(ph, i, b))
                        po = bank[4][:, 0:ET * D].rearrange("p (j d) -> p j d", d=D)
                        if p.after == "norm_ln":
                            V.tensor_tensor(o, po, bc(info_dst[:, g, :, 0], ET), ALU.mult).then_inc(
                                s["psum_out_used"].sem, 1)
                        else:
                            V.tensor_tensor(o, po, brow[p.bias][:, :].unsqueeze(1).to_broadcast([P, ET, D]),
                                            ALU.add).then_inc(s["psum_out_used"].sem, 1)
                    if nodes:
                        wait(dve, nstored.before(ph, i, b))
                        if p.nodes == "mm":
                            wait(dve, s["nout_summed"].after(ph, g))
                            V.tensor_tensor(no, bank[7][:, :].rearrange("p (j d) -> p j d", d=D),
                                            brow[p.node_bias][:, :].unsqueeze(1).to_broadcast([P, NT, D]),
                                            ALU.add).then_inc(s["psum_nout_used"].sem, 1)
                    if edges:
                        wait(dve, s["psum_out_used"].after(ph, g))
                        if p.resid:
                            r = rows[b] if p.resid == "self" else resid[b]
                            wait(dve, (rows_in if p.resid == "self" else resid_in).after(ph, i, b))
                            V.tensor_tensor(o, o, r[:, :, :], ALU.add).then_inc(s["resid_added"].sem, 1)
                        if p.after == "relu":
                            V.tensor_scalar(o, o, 0.0, None, ALU.max).then_inc(s["res_ready"].sem, 1)
                    nsrc = no
                    if nodes and p.nodes == "mm":
                        wait(dve, s["psum_nout_used"].after(ph, g))
                        if p.node_resid:
                            r = nrows[b] if p.node_resid == "self" else nresid[b]
                            wait(dve, (nrows_in if p.node_resid == "self" else nresid_in).after(ph, i, b))
                            V.tensor_tensor(no, no, r[:, :, :], ALU.add).then_inc(s["nresid_added"].sem, 1)
                        if p.node_after == "relu":
                            V.tensor_scalar(no, no, 0.0, None, ALU.max).then_inc(s["nres_ready"].sem, 1)
                    elif nodes:
                        wait(dve, nrows_in.after(ph, i, b))
                        nsrc = nrows[b][:, :, :]
                    both = []
                    if ph in s["mean_sum"].at:
                        both.append(("", o, o, sq, stat, ET, "resid_added" if p.resid else "psum_out_used"))
                    if ph in s["nmean_sum"].at:
                        both.append(("n", nsrc, no, nsq, nstat, NT,
                                     ("nresid_added" if p.node_resid else "psum_nout_used") if p.nodes == "mm" else None))
                    for k, a, to, q, st, m, before in both:
                        if before:
                            wait(dve, s[before].after(ph, g))
                        V.tensor_reduce(st["mean"][:, :], a, AX.X, ALU.add).then_inc(s[k + "mean_sum"].sem, 1)
                    for k, a, to, q, st, m, _ in both:
                        wait(dve, s[k + "mean_sum"].after(ph, g))
                        V.tensor_scalar(st["neg"][:, :], st["mean"][:, :], -1.0 / D, None, ALU.mult).then_inc(
                            s[k + "mean_ready"].sem, 1)
                    for k, a, to, q, st, m, _ in both:
                        wait(dve, s[k + "mean_ready"].after(ph, g))
                        V.tensor_tensor(to, a, bc(st["neg"][:, :], m), ALU.add).then_inc(s[k + "centred"].sem, 1)
                    for k, a, to, q, st, m, _ in both:
                        wait(dve, s[k + "centred"].after(ph, g))
                        V.tensor_tensor(q[:, :, :], to, to, ALU.mult).then_inc(s[k + "squared"].sem, 1)
                    for k, a, to, q, st, m, _ in both:
                        wait(dve, s[k + "squared"].after(ph, g), s[k + "std_ready"].after(ph, g - 1))
                        V.tensor_reduce(st["var"][:, :], q[:, :, :], AX.X, ALU.add).then_inc(s[k + "var_ready"].sem, 1)
                    for k, a, to, q, st, m, _ in both:
                        wait(dve, s[k + "std_ready"].after(ph, g))
                        V.reciprocal(st["rstd"][:, :], st["std"][:, :]).then_inc(s[k + "rstd_ready"].sem, 1)
                    for k, a, to, q, st, m, _ in both:
                        wait(dve, s[k + "rstd_ready"].after(ph, g))
                        V.tensor_tensor(to, to, bc(st["rstd"][:, :], m), ALU.mult).then_inc(s[k + "res_ready"].sem, 1)

                def scan(i, b, p=p, ph=ph):
                    g = 2 * i + b
                    if ph in s["agg_ready"].at:
                        if p.msg is not None:
                            wait(dve, s["msg_ready"].after(ph, g))
                            a = msg_t[b]
                        else:
                            wait(dve, s["got_t_ready"].after(ph, g))
                            a = got_t[b]
                        wait(dve, side_in.after(ph, i, b))
                        if p.keep:
                            wait(dve, stored.before(ph, i, b))
                        else:
                            wait(dve, s["out_summed"].after(ph, g - 2))
                        wait(dve, s["agg_ready"].after(ph, g - 1))
                        if p.agg == "add":
                            last = V.tensor_tensor(agg_t[b][:, :], got_t[b][:, :], side[b][:, :], ALU.add)
                        else:
                            last = V.tensor_tensor_scan(agg_t[b][:, :], side[b][:, :], a[:, :],
                                                        agg_t[1 - b][:, EG - 1:EG], p.agg[0], p.agg[1])
                        last.then_inc(s["agg_ready"].sem, 1)

                if n:
                    barrier(dve, n)
                for b in two:
                    fetch_idx(b, b)
                if p.scatter:
                    with dve.Fori(0, PAIRS - 1) as i:
                        for b in two:
                            receive(i, b)
                else:
                    skewed(dve, receive, finish, scan)


def kernel(x, src, dst, L1_gnn_W_lin, L1_gnn_b_lin, L1_gnn_W_rot, L1_gnn_b_rot, L2_gnn_W1, L2_gnn_b1, L2_gnn_W2,
           L2_gnn_b2, L2_gnn_W3, L2_gnn_b3, L3_gnn_W_pool, L3_gnn_b_pool, L3_gnn_W_self, L3_gnn_W_neigh, L3_gnn_bias):
    import numpy as np
    import concourse.bacc as bacc
    from concourse.bass_utils import run_bass_kernel_spmd as run

    def edges(a, pad):
        return np.concatenate([np.asarray(a), np.full(pad, NODES, a.dtype)])

    def by_partition(e):
        return np.ascontiguousarray(e.reshape(GROUPS, P, ET).transpose(1, 0, 2).reshape(P, COLS))

    src, dst = np.asarray(src), np.asarray(dst)
    pad = EDGES_PAD - EDGES
    s, d = edges(src, pad), edges(dst, pad)
    nxt = np.concatenate([d[1:], np.full(1, -1, d.dtype)])
    prev = np.concatenate([np.full(1, -1, d.dtype), d[:-1]])
    xp = np.zeros((NODES_PAD, D), np.float32)
    xp[:NODES] = x
    row = lambda v: np.asarray(v).reshape(1, D)
    ins = {
        "x": xp, "src_e": by_partition(s), "dst_e": by_partition(d), "next_e": by_partition(nxt),
        "src_tiles": np.ascontiguousarray(s.reshape(GROUPS, P, ET).transpose(0, 2, 1).reshape(GROUPS, 1, EG)),
        "dst_rows": d.reshape(GROUPS, EG), "prev_rows": prev.reshape(GROUPS, EG),
        "w_lin": np.ascontiguousarray(np.asarray(L1_gnn_W_lin).T), "b_lin": row(L1_gnn_b_lin),
        "w_rot": np.ascontiguousarray(np.asarray(L1_gnn_W_rot).T), "b_rot": row(L1_gnn_b_rot),
        "w1": L2_gnn_W1, "b1": row(L2_gnn_b1), "w2": L2_gnn_W2, "b2": row(L2_gnn_b2), "w3": L2_gnn_W3,
        "b3": row(L2_gnn_b3), "w_pool": L3_gnn_W_pool, "b_pool": np.ascontiguousarray(np.asarray(L3_gnn_b_pool).T),
        "w_self": L3_gnn_W_self, "w_neigh": L3_gnn_W_neigh, "bias": L3_gnn_bias,
    }
    nc = bacc.Bacc("TRN2", target_bir_lowering=False, num_devices=1)
    arrays, args = {}, []
    for name, a in ins.items():
        a = np.ascontiguousarray(a)
        arrays[f"in_{name}"] = a
        args.append(nc.dram_tensor(f"in_{name}", a.shape, mybir.dt.from_np(a.dtype), kind="ExternalInput").ap())
    args.append(nc.dram_tensor("out_rows", (NODES_PAD, D), F32, kind="ExternalOutput").ap())
    graph_kernel(nc, *args)
    r = run(nc, [arrays], core_ids=[0])
    return r.results[0]["out_rows"][:NODES]
```

```python
import concourse.bass as bass
from concourse import mybir
from contextlib import ExitStack

P = 128
D = 64
NODES, EDGES = 100000, 50000
PAIRS = 49
GROUPS = 2 * PAIRS
ET, NT = 4, 8
EG, NG = ET * P, NT * P
EDGES_PAD = GROUPS * EG
NODES_PAD = GROUPS * NG
SPARES = EG
COLS = GROUPS * ET
COLS_BUF = COLS + 2 * ET
HI = NODES_PAD // P
HALF = HI // 2
HT = HI // 7
INFO = 4
XW = D + INFO
EPS = 1e-5
FAR = -3.0e38
CREDIT = 2

F32, I32, U32, BF16, F16 = (mybir.dt.float32, mybir.dt.int32, mybir.dt.uint32, mybir.dt.bfloat16, mybir.dt.float16)
ALU, ACT, AX = mybir.AluOpType, mybir.ActivationFunctionType, mybir.AxisListType


class Phase:

    def __init__(self, name, fwd=None, fwd_idx=None, scale=None, rev=None, rev_scale=None, rev_sum=None, side=None,
                 msg=None, agg=None, keep=None, w=None, bias=None, self_rows=None, resid=None,
                 after=None, out=None, nodes=False, node_self=None, node_q=None, node_w=None,
                 node_bias=None, node_resid=None, node_after=None, node_out=None, scatter=False):
        self.name = name
        self.fwd, self.fwd_idx, self.scale = fwd, fwd_idx, scale
        self.rev, self.rev_scale, self.rev_sum = rev, rev_scale, rev_sum
        self.side = side
        self.msg = msg
        self.agg = agg
        self.keep = keep
        self.w, self.bias = w, bias
        self.self_rows, self.resid, self.after, self.out = self_rows, resid, after, out
        self.nodes, self.node_self, self.node_q, self.node_w = nodes, node_self, node_q, node_w
        self.node_bias, self.node_resid, self.node_after, self.node_out = node_bias, node_resid, node_after, node_out
        self.scatter = scatter


class Step:

    def __init__(self, sem, phases, more=0):
        self.sem, self.each, self.at = sem, GROUPS + more, {p: n for n, p in enumerate(phases)}

    def after(self, ph, g):
        return self.sem, CREDIT + self.at[ph] * self.each + g + 1


class Arrivals:

    def __init__(self, sems, phases, each=1, primed=False):
        self.sems, self.at, self.each, self.primed = sems, {p: n for n, p in enumerate(phases)}, each, primed

    def after(self, ph, i, b):
        return self.sems[b], 16 * self.each * (self.at[ph] * PAIRS + i + 1) + 16 * self.primed

    def before(self, ph, i, b):
        return self.sems[b], 16 * self.each * (self.at[ph] * PAIRS + i) + 16 * self.primed

    def all(self, ph):
        return [self.after(ph, PAIRS - 1, b) for b in range(2)]


def wait(eng, *pairs):
    for sem, value in pairs:
        eng.wait_ge(sem, value)


def settle(eng, pace):
    eng.sem_inc(pace, 1)


def paced(eng, pace, *pairs):
    for pair in pairs:
        wait(eng, pair)
        settle(eng, pace)


def skewed(steps):
    def trip(cur, nxt):
        for ahead, do in steps:
            if ahead and nxt:
                do(*nxt)
            elif not ahead and cur:
                do(*cur)
    return trip


def run_skewed(eng, steps):
    trip = skewed(steps)
    trip(None, (0, 0))
    with eng.Fori(0, PAIRS - 1) as i:
        trip((i, 0), (i, 1))
        trip((i, 1), (i + 1, 0))
    trip((PAIRS - 1, 0), (PAIRS - 1, 1))
    trip((PAIRS - 1, 1), None)


def graph_kernel(nc, x, src_e, dst_e, next_e, src_tiles, dst_rows, prev_rows, w_lin, b_lin, w_rot, b_rot,
                 w1, b1, w2, b2, w3, b3, w_pool, b_pool, w_self, w_neigh, bias, out):
    ctx = ExitStack()

    def dram(name, shape, dt=F32):
        return nc.dram_tensor(name, shape, dt).ap()

    STATES = ["T1", "T2", "H1", "H2", "T3", "G1", "G2"]
    table = {n: dram(n, [NODES_PAD + EDGES_PAD, D]) for n in STATES}
    table["XH"] = dram("XH", [NODES_PAD, XW])
    table["XA"] = dram("XA", [EDGES_PAD, D])
    table["FA"] = dram("FA", [EDGES_PAD, D])
    table["S1"] = dram("S1", [NODES_PAD + SPARES, D])
    table["S2"] = dram("S2", [NODES_PAD + SPARES, D])
    F3 = dram("F3", [GROUPS, D, EG])
    info_d = dram("info_d", [NODES_PAD, INFO])
    same_d = dram("same_d", [GROUPS, EG])
    far_d = dram("far_d", [GROUPS, EG])
    prime_d = dram("prime_d", [16, 16])
    side_of = {"same": same_d, "far": far_d}

    def edge_rows(name):
        t = table[name]
        if name in STATES:
            t = t[NODES_PAD:NODES_PAD + EDGES_PAD, :]
        return t.rearrange("(g p j) d -> g p (j d)", p=P, j=ET)

    def node_rows(name):
        t = {"x": x, "out": out}.get(name)
        t = table[name][0:NODES_PAD, :] if t is None else t
        return t.rearrange("(g p j) d -> g p (j d)", p=P, j=NT)

    PHASES = [
        Phase("own", fwd="XH", fwd_idx="dst", after="root", out="XA", nodes=True, node_self="x", node_w="centre",
              node_after="ln", node_out="T1"),
        Phase("l0", fwd="XH", fwd_idx="src", scale="norm", side="far", agg=(ALU.add, ALU.max), w="centre",
              self_rows="XA", after="norm_ln", out="T1", nodes=True, node_self="T1", node_w="rot", node_bias="l1",
              node_after="ln", node_out="T2"),
        Phase("l1", fwd="T1", fwd_idx="src_own", side="same", agg=(ALU.mult, ALU.add), w="l1", self_rows="T1",
              bias="l1", after="ln", out="T2", nodes=True, node_self="T2", node_w="w1a", node_bias="b1",
              node_after="relu", node_out="H1"),
        Phase("l2a", fwd="T2", fwd_idx="src_own", scale="inv_out", side="same", agg=(ALU.mult, ALU.add), w="w1",
              self_rows="T2", bias="b1", after="relu", out="H1"),
        Phase("sum1", rev="H1", rev_scale="inv_in", rev_sum="S1"),
        Phase("l2b", fwd="S1", fwd_idx="dst", agg="pass", w="w2", self_rows="H1", bias="b2", after="relu", out="H2",
              nodes=True, node_self="H1", node_q="S1", node_w="w2", node_bias="b2", node_after="relu", node_out="H2"),
        Phase("sum2", fwd="H2", fwd_idx="src_own", scale="inv_all", side="same", agg=(ALU.mult, ALU.add), keep="F3",
              rev="H2", rev_scale="inv_all_dst", rev_sum="S2"),
        Phase("l2c", fwd="S2", fwd_idx="dst", side="F3", agg="add", w="w3", self_rows="H2", resid="T2", bias="b3",
              after="ln", out="T3", nodes=True, node_self="H2", node_q="S2", node_w="w3", node_bias="b3",
              node_resid="T2", node_after="ln", node_out="T3"),
    ]
    for n, (before, name) in enumerate((("T3", "G1"), ("G1", "G2"), ("G2", "FA"))):
        last = n == 2
        PHASES.append(Phase(
            "l3" + "abc"[n], fwd=before, fwd_idx="src_own", side="same", msg=n, agg=(ALU.mult, ALU.max), w=f"conv{n}",
            self_rows=before, resid="T3" if last else None, bias=f"bias{n}", after="ln" if last else "relu", out=name,
            nodes=True, node_self=before, node_w=f"self{n}", node_bias=f"bias{n}", node_resid="T3" if last else None,
            node_after="ln" if last else "relu", node_out="out" if last else name))
    PHASES.append(Phase("scatter", scatter=True))

    def which(test):
        return [p.name for p in PHASES if test(p)]

    with ctx:
        def sb(name, shape, dt=F32):
            return ctx.enter_context(nc.sbuf_tensor(name, shape, dt))

        def sem(name):
            return ctx.enter_context(nc.semaphore(name))

        bank = [ctx.enter_context(nc.psum_tensor(f"bank{n}", [P, 512], F32)) for n in range(8)]

        eye = sb("eye", [P, P])
        tri = sb("tri", [P, P])
        ones = sb("ones", [P, P])
        idx_all = {n: sb(f"idx_{n}", [P, COLS_BUF], U32) for n in ("dst", "src", "src_own", "dst_own", "sum", "out")}
        src_f = sb("src_f", [P, COLS_BUF])
        info_src = sb("info_src", [P, GROUPS, ET, INFO])
        info_dst = sb("info_dst", [P, GROUPS, ET, INFO])
        inv_in = sb("inv_in", [P, GROUPS, ET])
        spare = sb("spare", [P, ET])
        before = sb("before", [P, EG])
        eps = sb("eps", [P, 1])
        zero = sb("zero", [P, 1024])

        STACKS = {"l1": (w_lin, w_rot), "w1": (w1[D:2 * D, :], w1[0:D, :]), "w2": (w2[D:2 * D, :], w2[0:D, :]),
                  "w3": (w3[D:2 * D, :], w3[0:D, :])}
        for n in range(3):
            STACKS[f"conv{n}"] = (w_neigh[n], w_self[n])
        PAIRED = {"rot": w_rot, "w1a": w1[0:D, :]}
        for n in range(3):
            PAIRED[f"self{n}"] = w_self[n]
        stacked = {n: sb(f"stack_{n}", [P, D]) for n in [*STACKS, "centre"]}
        pair = {n: sb(f"pair_{n}", [P, P]) for n in [*PAIRED, "centre"]}
        pool_w = [sb(f"pool_w{n}", [D, D]) for n in range(3)]
        B_ROWS = {"l1": b_lin, "rot": b_rot, "b1": b1, "b2": b2, "b3": b3}
        for n in range(3):
            B_ROWS[f"bias{n}"] = bias[n:n + 1, :]
        brow = {n: sb(f"brow_{n}", [P, D]) for n in B_ROWS}
        row_mean = sb("row_mean", [P, 2])
        b_pool_col = sb("b_pool_col", [D, 3])

        two = range(2)
        ib = [sb(f"ib{b}", [P, ET], U32) for b in two]
        ib2 = [sb(f"ib2{b}", [P, ET], U32) for b in two]
        ib3 = [sb(f"ib3{b}", [P, ET], U32) for b in two]
        got = [sb(f"got{b}", [P, ET, XW]) for b in two]
        stack = [sb(f"stack{b}", [P, ET, 2 * D]) for b in two]
        got2 = [sb(f"got2{b}", [P, ET, D]) for b in two]
        scaled2 = [sb(f"scaled2{b}", [P, ET, D]) for b in two]
        src_row = [sb(f"src_row{b}", [P, EG], I32) for b in two]
        wide = sb("wide", [P, 2 * ET * EG])
        equal = [wide[:, b * ET * EG:(b + 1) * ET * EG].rearrange("p (k e) -> p k e", k=ET) for b in two]
        summed = [sb(f"summed{b}", [P, ET, D]) for b in two]
        side = [sb(f"side{b}", [D, EG]) for b in two]
        got_t = [sb(f"got_t{b}", [D, EG]) for b in two]
        msg_t = [sb(f"msg_t{b}", [D, EG]) for b in two]
        key = [sb(f"key{b}", [P, EG]) for b in two]
        resid = [sb(f"resid{b}", [P, ET, D]) for b in two]
        res = [sb(f"res{b}", [P, ET, D]) for b in two]
        nrows = [sb(f"nrows{b}", [P, NT, D]) for b in two]
        wide_n = sb("wide_n", [P, 4 * NT * P])
        nstack = [wide_n[:, b * NT * P:(b + 1) * NT * P].rearrange("p (j d) -> p j d", j=NT) for b in two]
        nresid = [sb(f"nresid{b}", [P, NT, D]) for b in two]
        nt = [wide_n[:, (2 + b) * NT * P:(3 + b) * NT * P] for b in two]
        nres = [sb(f"nres{b}", [P, NT, D]) for b in two]
        sq = [sb(f"sq{b}", [P, ET, D]) for b in two]
        nsq = [sb(f"nsq{b}", [P, NT, D]) for b in two]
        factor = [sb(f"factor{b}", [P, ET]) for b in two]
        stat = {k: sb(f"stat_{k}", [P, ET]) for k in ("var", "var2", "std", "rstd", "rstd2")}
        nstat = {k: sb(f"nstat_{k}", [P, NT]) for k in ("var", "std", "rstd")}

        fwd_ph = which(lambda p: p.fwd)
        rev_ph = which(lambda p: p.rev)
        scat_ph = which(lambda p: p.scatter)
        agg_ph = which(lambda p: p.agg)
        edge_ph = which(lambda p: p.w)
        out_ph = which(lambda p: p.out)
        node_ph = which(lambda p: p.nodes)
        msg_ph = which(lambda p: p.msg is not None)
        ln_ph = which(lambda p: p.after in ("ln", "norm_ln"))
        nln_ph = which(lambda p: p.node_after == "ln")
        steps = {}

        every = [p.name for p in PHASES]
        for name, phases in (
                ("idx_ready", fwd_ph + scat_ph), ("idx2_ready", rev_ph), ("idx3_ready", rev_ph),
                ("got_used", which(lambda p: p.scale or p.fwd == "XH")), ("root_ready", ["own"]),
                ("got2_used", rev_ph), ("equal_ready", which(lambda p: p.rev or p.name == "l2a")), ("dup_found", ["l2a"]),
                ("spare_off", ["l2a"]), ("dup_off", ["l2a"]),
                ("turned", agg_ph), ("nturned", node_ph), ("msg_summed", msg_ph), ("deduped", rev_ph),
                ("out_summed", edge_ph), ("nout_summed", node_ph),
                ("got_t_ready", agg_ph), ("own_t_ready", which(lambda p: p.w and p.agg != "pass")),
                ("nt_ready", node_ph), ("msg_ready", msg_ph), ("summed_ready", rev_ph),
                ("squared", ln_ph), ("nsquared", nln_ph), ("std_ready", ln_ph), ("nstd_ready", nln_ph),
                ("agg_ready", which(lambda p: p.agg and p.agg != "pass")),
                ("biased", which(lambda p: p.bias)), ("nbiased", which(lambda p: p.node_bias)),
                ("resid_added", which(lambda p: p.resid)), ("nresid_added", which(lambda p: p.node_resid)),
                ("var_ready", ln_ph), ("nvar_ready", nln_ph), ("var2_ready", ["l0"]),
                ("rstd_ready", ln_ph), ("nrstd_ready", nln_ph), ("rstd2_ready", ["l0"]),
                ("res_ready", out_ph), ("nres_ready", node_ph)):
            steps[name] = Step(sem(name), phases, 2 if name in ("idx_ready", "idx2_ready") else 0)
        s = steps

        def pairof(name):
            return [sem(f"{name}{b}") for b in two]

        early, late = every[:6], every[6:]
        gathered_1 = Arrivals(pairof("gathered_a"), [p for p in fwd_ph if p in early], ET)
        gathered_2 = Arrivals(pairof("gathered_b"), [p for p in fwd_ph if p in late], ET)

        def gathered(ph):
            return gathered_1 if ph in early else gathered_2

        gathered_rev = Arrivals(pairof("gathered_rev"), rev_ph, ET)
        scattered = Arrivals(pairof("scattered"), scat_ph, ET)
        side_in = Arrivals(pairof("side_in"), which(lambda p: p.side))
        srow_in = Arrivals(pairof("srow_in"), which(lambda p: p.rev or p.name == "l2a"))
        rows_in = Arrivals(pairof("rows_in"), which(lambda p: p.self_rows))
        resid_in = Arrivals(pairof("resid_in"), which(lambda p: p.resid or p.scatter))
        nrows_in = Arrivals(pairof("nrows_in"), node_ph)
        nq_in = Arrivals(pairof("nq_in"), which(lambda p: p.node_q))
        nresid_in = Arrivals(pairof("nresid_in"), which(lambda p: p.node_resid))
        stored = Arrivals(pairof("stored"), which(lambda p: p.out or p.keep), primed=True)
        nstored = Arrivals(pairof("nstored"), node_ph, primed=True)
        added = sem("added")
        consts_in, zeroed, prep_in = sem("consts_in"), sem("zeroed"), sem("prep_in")
        pool_built, dve_chain, act_chain, pe_chain = sem("pool_built"), sem("dve_chain"), sem("act_chain"), sem("pe_chain")
        hot_ready, hot_used = sem("hot_ready"), sem("hot_used")
        info_out, xh_in, xh_ready, xh_out = sem("info_out"), pairof("xh_in"), sem("xh_ready"), pairof("xh_out")
        masks_out, masks_ready, info_ready = sem("masks_out"), sem("masks_ready"), sem("info_ready")

        def barrier(eng, n):
            if n == 0:
                wait(eng, (xh_out[0], 16 * PAIRS), (xh_out[1], 16 * PAIRS), (masks_out, 32), (zeroed, 32 * (GROUPS + 1)))
                return
            before = PHASES[n - 1]
            if before.name in stored.at:
                wait(eng, *stored.all(before.name))
            if before.nodes:
                wait(eng, *nstored.all(before.name))
            if before.rev:
                wait(eng, (added, 16 * COLS * (rev_ph.index(before.name) + 1)))

        hot_lo = [[sb(f"hot_lo{k}{b}", [P, P], BF16) for b in two] for k in two]
        hot_hi = [[sb(f"hot_hi{k}{b}", [P, HI], BF16) for b in two] for k in two]
        count_up = sb("count_up", [P, HI], F16)
        count_i = sb("count_i", [P, HI], I32)
        node_i = sb("node_i", [P, HI], I32)
        edge_i = [sb(f"edge_i{k}", [P, COLS], I32) for k in range(3)]
        part_i = sb("part_i", [P, ET], I32)
        lo_f = [sb(f"lo_f{k}", [P, COLS]) for k in two]
        hi_f = [sb(f"hi_f{k}", [P, COLS]) for k in two]
        deg = [sb(f"deg{k}", [P, HI]) for k in two]
        field = [wide[:, k * HI:(k + 1) * HI] for k in range(INFO)]
        tmp = sb("tmp", [P, HI])
        info_t = wide_n[0:HT, 0:7 * P * INFO].rearrange("h (k l f) -> h k l f", k=7, f=INFO)
        xh = [sb(f"xh{b}", [P, NT, XW]) for b in two]
        xh_info = [sb(f"xh_info{b}", [P, NT * INFO]) for b in two]
        drow = sb("drow", [GROUPS, EG], I32)
        prow = sb("prow", [GROUPS, EG], I32)
        same = sb("same", [GROUPS, EG])
        far = sb("far", [GROUPS, EG])
        last_f = sb("last_f", [P, COLS])
        dst_f = sb("dst_f", [P, COLS])
        shifted = sb("shifted", [P, COLS], I32)
        prefix = sb("prefix", [P, HI])
        dup = sb("dup", [P, 3, ET])
        links, sp_pace, pool_pace, pe_pace = sem("links"), sem("sp_pace"), sem("pool_pace"), sem("pe_pace")

        block = ctx.enter_context(nc.Block())
        N_CONSTS = 2 * len(STACKS) + 2 * len(PAIRED) + 3 + len(B_ROWS) + 1

        def scale_of(p, kind, g):
            ap = {"norm": info_src[:, g, :, 0], "inv_out": info_src[:, g, :, 1], "inv_all": info_src[:, g, :, 2],
                  "inv_all_dst": info_dst[:, g, :, 2], "inv_in": inv_in[:, g, :]}[kind]
            return ap.unsqueeze(2).to_broadcast([P, ET, D])

        @block.sync
        def _(sp):
            for name in steps:
                sp.sem_inc(steps[name].sem, CREDIT)
            for k, a in enumerate((src_e, dst_e, next_e)):
                sp.dma_start(edge_i[k][:, :], a).then_inc(prep_in, 16)
            sp.dma_start(drow[:, :], dst_rows).then_inc(prep_in, 16)
            sp.dma_start(prow[:, :], prev_rows).then_inc(prep_in, 16)
            paced(sp, sp_pace, (pool_built, 2))
            for name, halves in STACKS.items():
                for k in two:
                    sp.dma_start(stacked[name][D * k:D * (k + 1), :], halves[k]).then_inc(consts_in, 16)
            for name, w in PAIRED.items():
                for k in two:
                    sp.dma_start(pair[name][D * k:D * (k + 1), D * k:D * (k + 1)], w).then_inc(consts_in, 16)
            for n in range(3):
                sp.dma_start(pool_w[n][:, :], w_pool[n]).then_inc(consts_in, 16)
            for name, v in B_ROWS.items():
                sp.dma_start(brow[name][:, :], v.to_broadcast([P, D])).then_inc(consts_in, 16)
            sp.dma_start(b_pool_col[:, :], b_pool).then_inc(consts_in, 16)
            for n, sm in enumerate(stored.sems + nstored.sems):
                sp.dma_start(prime_d[n:n + 1, :], zero[0:1, 0:16]).then_inc(sm, 16)
            with sp.Fori(0, GROUPS) as g:
                for name in ("S1", "S2"):
                    sp.dma_start(node_rows(name)[g], zero[:, 0:NT * D]).then_inc(zeroed, 16)
            for name in ("S1", "S2"):
                sp.dma_start(table[name][NODES_PAD:, :].rearrange("(p j) d -> p (j d)", p=P),
                             zero[:, 0:ET * D]).then_inc(zeroed, 16)
            paced(sp, sp_pace, (masks_ready, 1))
            sp.dma_start(same_d, same[:, :]).then_inc(masks_out, 16)
            sp.dma_start(far_d, far[:, :]).then_inc(masks_out, 16)
            paced(sp, sp_pace, (info_ready, 7))
            info_rows = info_d.rearrange("(k h l) f -> k h (l f)", k=7, l=P)
            for k in range(7):
                sp.dma_start(info_rows[k], info_t[:, k, :, :].rearrange("h l f -> h (l f)")).then_inc(info_out, 16)
            paced(sp, sp_pace, (info_out, 16 * 7))
            x_rows, xh_rows = node_rows("x"), node_rows("XH")
            info_in = info_d.rearrange("(g p j) f -> g p (j f)", p=P, j=NT)

            def load_xh(i, b):
                g = 2 * i + b
                if not isinstance(i, int) or i > 0:
                    paced(sp, sp_pace, (xh_out[b], 16 * i))
                sp.dma_start(xh[b][:, :, 0:D], x_rows[g].rearrange("p (j d) -> p j d", d=D)).then_inc(xh_in[b], 16)
                sp.dma_start(xh_info[b][:, :], info_in[g]).then_inc(xh_in[b], 16)

            def store_xh(i, b):
                g = 2 * i + b
                paced(sp, sp_pace, (xh_ready, g + 1))
                sp.dma_start(xh_rows[g], xh[b][:, :, :].rearrange("p j w -> p (j w)")).then_inc(xh_out[b], 16)

            load_xh(0, 0)
            load_xh(0, 1)
            store_xh(0, 0)
            with sp.Fori(1, PAIRS) as i:
                load_xh(i, 0)
                store_xh(i - 1, 1)
                load_xh(i, 1)
                store_xh(i, 0)
            store_xh(PAIRS - 1, 1)

            for n, p in enumerate(PHASES):
                ph = p.name
                barrier(sp, n)

                def load(i, b, p=p, ph=ph):
                    g = 2 * i + b
                    if p.rev or ph == "l2a":
                        paced(sp, sp_pace, s["equal_ready"].after(ph, g - 2))
                        sp.dma_start(src_row[b][:, :], src_tiles[g].to_broadcast([P, EG])).then_inc(srow_in.sems[b], 16)
                    if p.side:
                        paced(sp, sp_pace, s["agg_ready"].after(ph, g - 2))
                        a = F3[g] if p.side == "F3" else side_of[p.side][bass.ds(g, 1), :].to_broadcast([D, EG])
                        sp.dma_start(side[b][:, :], a).then_inc(side_in.sems[b], 16)
                    if p.self_rows:
                        paced(sp, sp_pace, s["turned"].after(ph, g - 2))
                        sp.dma_start(stack[b][:, :, D:2 * D], edge_rows(p.self_rows)[g].rearrange(
                            "p (j d) -> p j d", d=D)).then_inc(rows_in.sems[b], 16)
                    if p.nodes:
                        paced(sp, sp_pace, s["nturned"].after(ph, g - 2))
                        a = node_rows(p.node_self)[g].rearrange("p (j d) -> p j d", d=D)
                        if p.node_q:
                            sp.dma_start(nstack[b][:, :, D:2 * D], a).then_inc(nrows_in.sems[b], 16)
                            sp.dma_start(nstack[b][:, :, 0:D], node_rows(p.node_q)[g].rearrange(
                                "p (j d) -> p j d", d=D)).then_inc(nq_in.sems[b], 16)
                        else:
                            sp.dma_start(nrows[b][:, :, :], a).then_inc(nrows_in.sems[b], 16)
                    if p.resid:
                        paced(sp, sp_pace, s["resid_added"].after(ph, g - 2))
                        sp.dma_start(resid[b][:, :, :].rearrange("p j d -> p (j d)"),
                                     edge_rows(p.resid)[g]).then_inc(resid_in.sems[b], 16)
                    if p.node_resid:
                        paced(sp, sp_pace, s["nresid_added"].after(ph, g - 2))
                        sp.dma_start(nresid[b][:, :, :].rearrange("p j d -> p (j d)"),
                                     node_rows(p.node_resid)[g]).then_inc(nresid_in.sems[b], 16)

                def store(i, b, p=p, ph=ph):
                    g = 2 * i + b
                    if p.keep:
                        paced(sp, sp_pace, s["agg_ready"].after(ph, g))
                        sp.dma_start(F3[g], key[b][0:D, :]).then_inc(stored.sems[b], 16)
                    if p.out:
                        paced(sp, sp_pace, s["res_ready"].after(ph, g))
                        sp.dma_start(edge_rows(p.out)[g], res[b][:, :, :].rearrange("p j d -> p (j d)")).then_inc(
                            stored.sems[b], 16)
                    if p.nodes:
                        paced(sp, sp_pace, s["nres_ready"].after(ph, g))
                        sp.dma_start(node_rows(p.node_out)[g],
                                     nres[b][:, :, :].rearrange("p j d -> p (j d)")).then_inc(nstored.sems[b], 16)

                def load_res(i, b, ph=ph):
                    if not isinstance(i, int) or i > 0:
                        paced(sp, sp_pace, scattered.before(ph, i, b))
                    sp.dma_start(res[b][:, :, :].rearrange("p j d -> p (j d)"),
                                 edge_rows("FA")[2 * i + b]).then_inc(resid_in.sems[b], 16)

                if p.scatter:
                    for b in two:
                        load_res(0, b)
                    with sp.Fori(1, PAIRS) as i:
                        for b in two:
                            load_res(i, b)
                else:
                    for b in two:
                        load(0, b)
                    with sp.Fori(0, PAIRS - 1) as i:
                        for b in two:
                            load(i + 1, b)
                            store(i, b)
                    for b in two:
                        store(PAIRS - 1, b)
            paced(sp, sp_pace, *scattered.all("scatter"))

        @block.gpsimd
        def _(pool):
            nc.gpsimd.memset(zero[:, :], 0.0)
            nc.gpsimd.memset(ones[:, :], 1.0)
            for name in pair:
                nc.gpsimd.memset(pair[name][:, :], 0.0)
            nc.gpsimd.memset(eye[:, :], 0.0)
            for b in two:
                nc.gpsimd.memset(key[b][:, :], 0.0)
            nc.gpsimd.memset(before[:, 0:3 * P], 1.0)
            nc.gpsimd.memset(eps[:, :], EPS).then_inc(pool_built, 1)
            pool.wait_ge(pool_built, 1)
            nc.gpsimd.affine_select(out=eye[:, :], in_=eye[:, :], compare_op=ALU.not_equal, fill=1.0, base=0,
                                    pattern=[[-1, P]], channel_multiplier=1)
            nc.gpsimd.affine_select(out=tri[:, :], in_=ones[:, :], compare_op=ALU.is_ge, fill=0.0, base=0,
                                    pattern=[[1, P]], channel_multiplier=-1)
            nc.gpsimd.affine_select(out=before[:, 3 * P:EG], in_=ones[:, :], compare_op=ALU.is_gt, fill=0.0, base=0,
                                    pattern=[[-1, P]], channel_multiplier=1)
            nc.gpsimd.iota(count_i[:, :], pattern=[[1, HI]], base=0, channel_multiplier=0)
            nc.gpsimd.iota(node_i[:, :], pattern=[[P, HI]], base=0, channel_multiplier=1)
            nc.gpsimd.iota(part_i[:, :], pattern=[[P, ET]], base=NODES_PAD, channel_multiplier=1).then_inc(pool_built, 1)

            for n, p in enumerate(PHASES):
                ph = p.name
                barrier(pool, n)

                def gather(i, b, p=p, ph=ph):
                    g = 2 * i + b
                    if p.fwd:
                        wait(pool, s["idx_ready"].after(ph, g))
                        if ph in s["got_used"].at:
                            wait(pool, s["got_used"].after(ph, g - 2))
                        else:
                            wait(pool, s["turned"].after(ph, g - 2))
                    if p.rev:
                        wait(pool, s["idx2_ready"].after(ph, g), s["got2_used"].after(ph, g - 2))
                    settle(pool, pool_pace)
                    width = XW if p.fwd == "XH" else D
                    for j in range(ET):
                        if p.fwd:
                            to = got[b][:, j, 0:width] if ph in s["got_used"].at else stack[b][:, j, 0:D]
                            pool.indirect_dma_start(
                                to, None, table[p.fwd],
                                bass.IndirectOffsetOnAxis(ib[b][:, j:j + 1], 0)).then_inc(gathered(ph).sems[b], 16)
                        if p.rev:
                            pool.indirect_dma_start(
                                got2[b][:, j, :], None, table[p.rev],
                                bass.IndirectOffsetOnAxis(ib2[b][:, j:j + 1], 0)).then_inc(gathered_rev.sems[b], 16)

                def put(i, b, p=p, ph=ph):
                    g = 2 * i + b
                    if p.rev:
                        wait(pool, s["summed_ready"].after(ph, g), s["idx3_ready"].after(ph, g))
                        done = 16 * (COLS * rev_ph.index(ph) + ET * g)
                        if not isinstance(done, int) or done > 0:
                            pool.wait_ge(added, done)
                        settle(pool, pool_pace)
                        for j in range(ET):
                            pool.indirect_dma_start(
                                table[p.rev_sum], bass.IndirectOffsetOnAxis(ib3[b][:, j:j + 1], 0),
                                summed[b][:, j, :], None, compute_op=ALU.add).then_inc(added, 16)

                if p.scatter:
                    def scatter(i, b, ph=ph):
                        g = 2 * i + b
                        wait(pool, s["idx_ready"].after(ph, g), resid_in.after(ph, i, b))
                        settle(pool, pool_pace)
                        for j in range(ET):
                            pool.indirect_dma_start(
                                out, bass.IndirectOffsetOnAxis(ib[b][:, j:j + 1], 0),
                                res[b][:, j, :], None, bounds_check=NODES_PAD - 1,
                                oob_is_err=False).then_inc(scattered.sems[b], 16)
                    with pool.Fori(0, PAIRS) as i:
                        for b in two:
                            scatter(i, b)
                elif p.rev:
                    gather(0, 0)
                    gather(0, 1)
                    with pool.Fori(0, PAIRS - 1) as i:
                        for b in two:
                            put(i, b)
                            gather(i + 1, b)
                    put(PAIRS - 1, 0)
                    put(PAIRS - 1, 1)
                else:
                    with pool.Fori(0, PAIRS) as i:
                        for b in two:
                            gather(i, b)

        @block.tensor
        def _(pe):
            T = nc.tensor
            pe.wait_ge(pool_built, 2)
            wait(pe, (dve_chain, 1))
            for k in range(4):
                T.matmul(bank[k][:, 0:HALF], hot_lo[0][0][:, :], hot_hi[0][0][:, 0:HALF], start=True, stop=False,
                         skip_group_check=True)
            T.matmul(bank[4][:, 0:P], hot_lo[0][0][:, :], hot_lo[0][0][:, :], start=True,
                     stop=True).then_inc(hot_used, 2)
            with pe.Fori(0, COLS // 2) as i:
                for b in two:
                    pe.wait_ge(hot_ready, 2 * i + b + 1)
                    for k in two:
                        for h in two:
                            last = T.matmul(bank[2 * k + h][:, 0:HALF], hot_lo[k][b][:, :],
                                            hot_hi[k][b][:, h * HALF:(h + 1) * HALF], start=False, stop=False,
                                            skip_group_check=True)
                    last.then_inc(hot_used, 1)
            pe.wait_ge(hot_ready, COLS + 1)
            for k in range(4):
                last = T.matmul(bank[k][:, 0:HALF], hot_lo[0][0][:, :], hot_hi[0][0][:, 0:HALF], start=False, stop=True,
                                skip_group_check=True)
            last.then_inc(pe_chain, 1)
            pe.wait_ge(act_chain, 1)
            for h in two:
                T.matmul(bank[4 + h][:, 0:HALF], tri[:, :], deg[1][:, h * HALF:(h + 1) * HALF], start=True, stop=True)
            for h in two:
                last = T.matmul(bank[6 + h][:, 0:HALF], ones[:, :], deg[1][:, h * HALF:(h + 1) * HALF], start=True,
                                stop=True)
            last.then_inc(pe_chain, 1)
            pe.wait_ge(act_chain, 3)
            for k in range(7):
                if k >= 2:
                    pe.wait_ge(info_ready, k - 1)
                for f in range(INFO):
                    last = T.transpose(bank[k % 2][0:HT, f * P:(f + 1) * P], field[f][:, k * HT:(k + 1) * HT], eye[:, :])
                last.then_inc(pe_chain, 1)

            pe.wait_ge(consts_in, 16 * N_CONSTS)
            for n, p in enumerate(PHASES):
                ph = p.name

                def turn(i, b, p=p, ph=ph):
                    g = 2 * i + b
                    if p.agg:
                        wait(pe, s["got_used"].after(ph, g) if p.scale else gathered(ph).after(ph, i, b))
                        if p.self_rows:
                            wait(pe, rows_in.after(ph, i, b))
                        wait(pe, s["got_t_ready"].after(ph, g - 2))
                        if ph in s["own_t_ready"].at:
                            wait(pe, s["own_t_ready"].after(ph, g - 2))
                        settle(pe, pe_pace)
                        width = 2 * D if p.self_rows else D
                        for j in range(ET):
                            last = T.transpose(bank[b][0:width, j * P:(j + 1) * P], stack[b][:, j, 0:width], eye[:, :])
                        last.then_inc(s["turned"].sem, 1)
                    if p.nodes:
                        wait(pe, nrows_in.after(ph, i, b), s["nt_ready"].after(ph, g - 1))
                        if p.node_q:
                            wait(pe, nq_in.after(ph, i, b))
                        settle(pe, pe_pace)
                        for j in range(NT if p.node_q else NT // 2):
                            a = (nstack[b][:, j, :] if p.node_q
                                 else nrows[b][:, 2 * j:2 * j + 2, :].rearrange("p j d -> p (j d)"))
                            last = T.transpose(bank[5 + j // 4][:, j % 4 * P:(j % 4 + 1) * P], a, eye[:, :])
                        last.then_inc(s["nturned"].sem, 1)

                def combine(i, b, p=p, ph=ph):
                    g = 2 * i + b
                    if p.w:
                        if p.agg == "pass":
                            wait(pe, s["got_t_ready"].after(ph, g))
                        else:
                            wait(pe, s["agg_ready"].after(ph, g), s["own_t_ready"].after(ph, g))
                        wait(pe, s["biased" if p.bias else "res_ready"].after(ph, g - 2))
                        settle(pe, pe_pace)
                        a = key[b][:, :].rearrange("c (q j) -> c q j", j=ET)
                        for j in range(ET):
                            last = T.matmul(bank[3 + b][:, j * D:(j + 1) * D], a[:, :, j], stacked[p.w][:, :],
                                            start=True, stop=True)
                        last.then_inc(s["out_summed"].sem, 1)
                    if p.nodes:
                        wait(pe, s["nt_ready"].after(ph, g), s["nbiased" if p.node_bias else "nres_ready"].after(ph, g - 1))
                        settle(pe, pe_pace)
                        if p.node_q:
                            for j in range(NT):
                                last = T.matmul(bank[7][:, j * D:(j + 1) * D], nt[b][:, j * P:(j + 1) * P],
                                                stacked[p.node_w][:, :], start=True, stop=True)
                        else:
                            for j in range(NT // 2):
                                cols = slice(j * P, (j + 1) * P)
                                last = T.matmul(bank[7][:, cols], nt[b][:, cols], pair[p.node_w][:, :], start=True,
                                                stop=True)
                        last.then_inc(s["nout_summed"].sem, 1)

                def message(i, b, p=p, ph=ph):
                    g = 2 * i + b
                    if p.msg is not None:
                        wait(pe, s["got_t_ready"].after(ph, g), s["msg_ready"].after(ph, g - 1))
                        settle(pe, pe_pace)
                        T.matmul(bank[2][0:D, :], pool_w[p.msg][:, :], got_t[b][:, :], start=True,
                                 stop=True).then_inc(s["msg_summed"].sem, 1)
                    if p.rev:
                        wait(pe, s["equal_ready"].after(ph, g), s["got2_used"].after(ph, g),
                             s["summed_ready"].after(ph, g - 1))
                        settle(pe, pe_pace)
                        for j in range(ET):
                            for k in range(j, ET):
                                last = T.matmul(bank[2][:, j * D:(j + 1) * D], equal[b][:, k, j * P:(j + 1) * P],
                                                scaled2[b][:, k, :], start=k == j, stop=k == ET - 1)
                        last.then_inc(s["deduped"].sem, 1)

                if not p.scatter:
                    run_skewed(pe, ((0, combine), (1, turn), (1, message)))

        @block.scalar
        def _(act):
            A = nc.scalar
            act.wait_ge(pe_chain, 1)
            for k in two:
                for h in two:
                    last = A.copy(deg[k][:, h * HALF:(h + 1) * HALF], bank[2 * k + h][:, 0:HALF])
            last.then_inc(act_chain, 1)
            act.wait_ge(dve_chain, 2)
            act.wait_ge(pool_built, 2)
            A.activation(tmp[:, :], field[0][:, :], ACT.Sqrt).then_inc(act_chain, 1)
            act.wait_ge(dve_chain, 3)
            A.copy(eps[0:1, :], eps[0:1, :]).then_inc(act_chain, 1)
            for k in range(7):
                act.wait_ge(pe_chain, 3 + k)
                A.copy(info_t[:, k, :, :].rearrange("h l f -> h f l"),
                       bank[k % 2][0:HT, :].rearrange("h (f l) -> h f l", f=INFO)).then_inc(info_ready, 1)

            for n, p in enumerate(PHASES):
                ph = p.name

                def evacuate(i, b, p=p, ph=ph):
                    g = 2 * i + b
                    if p.agg:
                        whole = p.agg == "pass"
                        reader = "msg_summed" if p.msg is not None else "out_summed" if whole else "agg_ready"
                        wait(act, s["turned"].after(ph, g), s[reader].after(ph, g - 2))
                        to = key[b][:, :] if whole else got_t[b][:, :]
                        A.copy(to.rearrange("c (q j) -> c j q", j=ET),
                               bank[b][0:P if whole else D, :].rearrange("c (j q) -> c j q", j=ET)).then_inc(
                                   s["got_t_ready"].sem, 1)
                        if ph in s["own_t_ready"].at:
                            wait(act, s["out_summed"].after(ph, g - 2))
                            A.copy(key[b][D:P, :].rearrange("c (q j) -> c j q", j=ET),
                                   bank[b][D:P, :].rearrange("c (j q) -> c j q", j=ET)).then_inc(
                                       s["own_t_ready"].sem, 1)
                    if p.nodes:
                        wait(act, s["nturned"].after(ph, g), s["nout_summed"].after(ph, g - 2))
                        for k in range(2 if p.node_q else 1):
                            last = A.copy(nt[b][:, k * 512:(k + 1) * 512], bank[5 + k][:, :])
                        last.then_inc(s["nt_ready"].sem, 1)

                def message(i, b, p=p, ph=ph):
                    g = 2 * i + b
                    if p.msg is not None:
                        wait(act, s["msg_summed"].after(ph, g), s["agg_ready"].after(ph, g - 2))
                        A.activation(msg_t[b][:, :], bank[2][0:D, :], ACT.Relu,
                                     bias=b_pool_col[:, p.msg:p.msg + 1]).then_inc(s["msg_ready"].sem, 1)
                    if p.rev:
                        wait(act, s["deduped"].after(ph, g))
                        if not isinstance(i, int) or i > 0:
                            act.wait_ge(added, 16 * (COLS * rev_ph.index(ph) + ET * (g - 1)))
                        A.copy(summed[b][:, :, :].rearrange("p j d -> p (j d)"),
                               bank[2][:, 0:ET * D]).then_inc(s["summed_ready"].sem, 1)

                def squares(i, b, p=p, ph=ph):
                    g = 2 * i + b
                    if p.w:
                        if p.after == "relu":
                            wait(act, s["biased"].after(ph, g))
                            A.activation(res[b][:, :, :], res[b][:, :, :], ACT.Relu).then_inc(s["res_ready"].sem, 1)
                        else:
                            a = res[b][:, :, :]
                            if p.after == "norm_ln":
                                a = bank[3 + b][:, 0:ET * D].rearrange("p (j d) -> p j d", d=D)
                            wait(act, s["out_summed" if p.after == "norm_ln" else "resid_added" if p.resid
                                      else "biased"].after(ph, g), s["var_ready"].after(ph, g - 2))
                            A.activation(sq[b][:, :, :], a, ACT.Square).then_inc(s["squared"].sem, 1)
                    if p.nodes:
                        if p.node_after == "relu":
                            wait(act, s["nbiased"].after(ph, g))
                            A.activation(nres[b][:, :, :], nres[b][:, :, :], ACT.Relu).then_inc(s["nres_ready"].sem, 1)
                        else:
                            a = nres[b][:, :, :]
                            if not p.node_bias:
                                a = bank[7][:, :].rearrange("p (j d) -> p j d", d=D)
                            wait(act, s["nout_summed" if not p.node_bias else "nresid_added" if p.node_resid
                                      else "nbiased"].after(ph, g), s["nvar_ready"].after(ph, g - 2))
                            A.activation(nsq[b][:, :, :], a, ACT.Square).then_inc(s["nsquared"].sem, 1)

                def roots(i, b, p=p, ph=ph):
                    g = 2 * i + b
                    if ph in s["std_ready"].at:
                        v = "var2" if p.after == "norm_ln" else "var"
                        wait(act, s[v + "_ready"].after(ph, g), s["rstd_ready"].after(ph, g - 1))
                        A.activation(stat["std"][:, :], stat[v][:, :], ACT.Sqrt, bias=eps[:, 0:1],
                                     scale=1.0 / D).then_inc(s["std_ready"].sem, 1)
                    if ph in s["nstd_ready"].at:
                        wait(act, s["nvar_ready"].after(ph, g), s["nrstd_ready"].after(ph, g - 1))
                        A.activation(nstat["std"][:, :], nstat["var"][:, :], ACT.Sqrt, bias=eps[:, 0:1],
                                     scale=1.0 / D).then_inc(s["nstd_ready"].sem, 1)

                if not p.scatter:
                    run_skewed(act, ((1, evacuate), (0, squares), (1, message), (0, roots)))

        @block.vector
        def _(dve):
            V = nc.vector
            link_count = [0]

            def link(ins):
                link_count[0] += 1
                ins.then_inc(links, 1)
                dve.wait_ge(links, link_count[0])

            V.memset(hot_lo[0][0][:, :], 0.0)
            for name in idx_all:
                V.memset(idx_all[name][:, COLS:COLS_BUF], 0)
            V.memset(hot_hi[0][0][:, :], 0.0).then_inc(dve_chain, 1)
            wait(dve, (prep_in, 16 * 5), (pool_built, 2))
            link(V.tensor_copy(count_up[:, :], count_i[:, :]))
            for k in two:
                link(V.tensor_scalar(shifted[:, :], edge_i[k][:, :], P - 1, None, ALU.bitwise_and))
                link(V.tensor_copy(lo_f[k][:, :], shifted[:, :]))
                link(V.tensor_scalar(shifted[:, :], edge_i[k][:, :], 7, None, ALU.arith_shift_right))
                link(V.tensor_copy(hi_f[k][:, :], shifted[:, :]))
            with dve.Fori(0, COLS // 2) as i:
                for b in two:
                    c = 2 * i + b
                    dve.wait_ge(hot_used, c + 1)
                    for k in two:
                        V.tensor_scalar(hot_lo[k][b][:, :], count_up[:, 0:P], lo_f[k][:, bass.ds(c, 1)], None,
                                        ALU.is_equal)
                        last = V.tensor_scalar(hot_hi[k][b][:, :], count_up[:, :], hi_f[k][:, bass.ds(c, 1)], None,
                                               ALU.is_equal)
                    last.then_inc(hot_ready, 1)
            dve.wait_ge(hot_used, COLS + 2)
            V.memset(hot_lo[0][0][:, :], 0.0).then_inc(hot_ready, 1)

            link(V.tensor_copy(idx_all["src"][:, 0:COLS], edge_i[0][:, :]))
            link(V.tensor_copy(idx_all["dst"][:, 0:COLS], edge_i[1][:, :]))
            link(V.tensor_copy(src_f[:, 0:COLS], edge_i[0][:, :]))
            link(V.tensor_copy(dst_f[:, :], edge_i[1][:, :]))
            link(V.tensor_tensor(last_f[:, :], edge_i[1][:, :], edge_i[2][:, :], ALU.not_equal))
            link(V.tensor_scalar(dst_f[:, :], dst_f[:, :], float(NODES_PAD), None, ALU.subtract))
            link(V.tensor_tensor(dst_f[:, :], dst_f[:, :], last_f[:, :], ALU.mult))
            link(V.tensor_scalar(idx_all["out"][:, 0:COLS], dst_f[:, :], float(NODES_PAD), None, ALU.add))
            link(V.tensor_copy(spare[:, :], part_i[:, :]))
            link(V.tensor_tensor(same[:, :], drow[:, :], prow[:, :], ALU.is_equal))
            V.tensor_scalar(far[:, :], same[:, :], 1.0, -FAR, ALU.subtract, ALU.mult).then_inc(masks_ready, 1)

            dve.wait_ge(act_chain, 1)
            V.tensor_scalar(field[0][:, :], deg[1][:, :], 1.0, None, ALU.max).then_inc(dve_chain, 1)
            link(V.tensor_scalar(field[1][:, :], deg[0][:, :], 1.0, None, ALU.max))
            link(V.reciprocal(field[1][:, :], field[1][:, :]))
            link(V.tensor_tensor(field[2][:, :], deg[0][:, :], deg[1][:, :], ALU.add))
            link(V.tensor_scalar(field[2][:, :], field[2][:, :], 1.0, None, ALU.max))
            link(V.reciprocal(field[2][:, :], field[2][:, :]))
            dve.wait_ge(pe_chain, 2)
            for h in two:
                cols = slice(h * HALF, (h + 1) * HALF)
                link(V.tensor_copy(prefix[:, cols], bank[6 + h][:, 0:HALF]))
            link(V.tensor_tensor_scan(field[3][:, :], prefix[:, :], zero[:, 0:HI], 0.0, ALU.add, ALU.add))
            link(V.tensor_tensor(field[3][:, :], field[3][:, :], prefix[:, :], ALU.subtract))
            for h in two:
                cols = slice(h * HALF, (h + 1) * HALF)
                link(V.tensor_tensor(field[3][:, cols], field[3][:, cols], bank[4 + h][:, 0:HALF], ALU.add))
            link(V.tensor_copy(prefix[:, :], node_i[:, :]))
            link(V.tensor_scalar(field[3][:, :], field[3][:, :], float(NODES_PAD - 1), None, ALU.add))
            link(V.tensor_tensor(field[3][:, :], field[3][:, :], prefix[:, :], ALU.subtract))
            link(V.tensor_scalar(deg[1][:, :], deg[1][:, :], 1.0, None, ALU.min))
            link(V.tensor_tensor(field[3][:, :], field[3][:, :], deg[1][:, :], ALU.mult))
            link(V.tensor_tensor(field[3][:, :], field[3][:, :], prefix[:, :], ALU.add))
            dve.wait_ge(act_chain, 2)
            V.reciprocal(field[0][:, :], tmp[:, :]).then_inc(dve_chain, 1)
            dve.wait_ge(consts_in, 16 * N_CONSTS)
            link(V.tensor_tensor(brow["l1"][:, :], brow["l1"][:, :], brow["rot"][:, :], ALU.add))
            for k in two:
                half = slice(D * k, D * (k + 1))
                link(V.tensor_copy(stacked["centre"][half, :], eye[half, half]))
                link(V.tensor_copy(pair["centre"][half, half], eye[half, half]))
            link(V.tensor_tensor(stacked["l1"][D:P, :], stacked["l1"][D:P, :], eye[D:P, D:P], ALU.add))
            link(V.tensor_tensor(pair["rot"][:, :], pair["rot"][:, :], eye[:, :], ALU.add))
            for w, halves in ((stacked["centre"], 1), (stacked["l1"], 1), (stacked["w3"], 1), (stacked["conv2"], 1),
                              (pair["centre"], 2), (pair["rot"], 2), (pair["self2"], 2), (brow["l1"], 1),
                              (brow["b3"], 1), (brow["bias2"], 1)):
                a = w[:, :].rearrange("p (k d) -> p k d", d=D)
                m = row_mean[:, 0:halves]
                link(V.tensor_reduce(m, a, AX.X, ALU.add))
                link(V.tensor_scalar(m, m, -1.0 / D, None, ALU.mult))
                link(V.tensor_tensor(a, a, m.unsqueeze(2).to_broadcast([P, halves, D]), ALU.add))
            with dve.Fori(0, PAIRS) as i:
                for b in two:
                    dve.wait_ge(xh_in[b], 32 * (i + 1))
                    V.tensor_copy(xh[b][:, :, D:XW],
                                  xh_info[b][:, :].rearrange("p (j f) -> p j f", f=INFO)).then_inc(xh_ready, 1)

            def bc(ap, n):
                return ap.unsqueeze(2).to_broadcast([P, n, D])

            for n, p in enumerate(PHASES):
                ph = p.name

                def fetch_idx(g, b, p=p, ph=ph):
                    cols = bass.ds(g * ET, ET)
                    if p.fwd or p.scatter:
                        V.tensor_copy(ib[b][:, :], idx_all["out" if p.scatter else p.fwd_idx][:, cols]).then_inc(
                            s["idx_ready"].sem, 1)
                    if p.rev:
                        V.tensor_copy(ib2[b][:, :], idx_all["dst_own"][:, cols]).then_inc(s["idx2_ready"].sem, 1)

                def receive(i, b, p=p, ph=ph):
                    g = 2 * i + b
                    if p.scatter:
                        wait(dve, scattered.after(ph, i, b))
                        fetch_idx(g + 2, b)
                        return
                    if p.fwd:
                        wait(dve, gathered(ph).after(ph, i, b))
                    if p.rev:
                        wait(dve, gathered_rev.after(ph, i, b))
                    fetch_idx(g + 2, b)
                    cols = bass.ds(g * ET, ET)
                    if ph == "own":
                        V.reciprocal(factor[b][:, :], got[b][:, :, D]).then_inc(s["root_ready"].sem, 1)
                        wait(dve, s["root_ready"].after(ph, g), stored.before(ph, i, b))
                        V.tensor_tensor(res[b][:, :, :], got[b][:, :, 0:D], bc(factor[b][:, :], ET),
                                        ALU.mult).then_inc(s["res_ready"].sem, 1)
                    if p.scale:
                        wait(dve, s["turned"].after(ph, g - 2))
                        f = bc(got[b][:, :, D], ET) if p.scale == "norm" else scale_of(p, p.scale, g)
                        last = V.tensor_tensor(stack[b][:, :, 0:D], got[b][:, :, 0:D], f, ALU.mult)
                        if p.fwd != "XH":
                            last.then_inc(s["got_used"].sem, 1)
                    if p.fwd == "XH":
                        k = ph == "own"
                        V.tensor_copy((info_dst if k else info_src)[:, g, :, :], got[b][:, :, D:XW])
                        last = V.tensor_copy(idx_all["dst_own" if k else "src_own"][:, cols], got[b][:, :, XW - 1])
                        if k:
                            last = V.tensor_tensor(inv_in[:, g, :], got[b][:, :, D], got[b][:, :, D], ALU.mult)
                        last.then_inc(s["got_used"].sem, 1)
                    if p.rev:
                        wait(dve, s["deduped"].after(ph, g - 2))
                        V.tensor_tensor(scaled2[b][:, :, :], got2[b][:, :, :], scale_of(p, p.rev_scale, g),
                                        ALU.mult).then_inc(s["got2_used"].sem, 1)
                        wait(dve, srow_in.after(ph, i, b))
                        for k in range(ET):
                            last = V.tensor_scalar(equal[b][:, k, 0:(k + 1) * P], src_row[b][:, 0:(k + 1) * P],
                                                   src_f[:, bass.ds(g * ET + k, 1)], None, ALU.is_equal)
                        last.then_inc(s["equal_ready"].sem, 1)
                        if not isinstance(i, int) or i > 0:
                            dve.wait_ge(added, 16 * (COLS * rev_ph.index(ph) + ET * (g - 1)))
                        V.tensor_copy(ib3[b][:, :], idx_all["sum"][:, cols]).then_inc(s["idx3_ready"].sem, 1)

                def rank(i, b, p=p, ph=ph):
                    g = 2 * i + b
                    cols = bass.ds(g * ET, ET)
                    wait(dve, srow_in.after(ph, i, b))
                    for k in range(ET):
                        last = V.scalar_tensor_tensor(
                            out=equal[b][:, k, 0:(k + 1) * P], in0=src_row[b][:, 0:(k + 1) * P],
                            scalar=src_f[:, bass.ds(g * ET + k, 1)], in1=before[:, (ET - 1 - k) * P:EG],
                            op0=ALU.is_equal, op1=ALU.mult)
                    last.then_inc(s["equal_ready"].sem, 1)
                    V.tensor_tensor(dup[:, 1, :], spare[:, :], src_f[:, cols], ALU.subtract).then_inc(
                        s["spare_off"].sem, 1)
                    wait(dve, s["equal_ready"].after(ph, g))
                    for k in range(ET):
                        last = V.tensor_reduce(dup[:, 0, k:k + 1], equal[b][:, k, 0:(k + 1) * P], AX.X, ALU.max)
                    last.then_inc(s["dup_found"].sem, 1)
                    wait(dve, s["spare_off"].after(ph, g), s["dup_found"].after(ph, g))
                    V.tensor_tensor(dup[:, 2, :], dup[:, 0, :], dup[:, 1, :], ALU.mult).then_inc(s["dup_off"].sem, 1)
                    wait(dve, s["dup_off"].after(ph, g))
                    V.tensor_tensor(idx_all["sum"][:, cols], dup[:, 2, :], src_f[:, cols], ALU.add)

                def add_up(i, b, p=p, ph=ph):
                    g = 2 * i + b
                    if p.bias:
                        wait(dve, s["out_summed"].after(ph, g), stored.before(ph, i, b))
                        V.tensor_tensor(res[b][:, :, :], bank[3 + b][:, 0:ET * D].rearrange("p (j d) -> p j d", d=D),
                                        brow[p.bias][:, :].unsqueeze(1).to_broadcast([P, ET, D]),
                                        ALU.add).then_inc(s["biased"].sem, 1)
                    if p.node_bias:
                        wait(dve, s["nout_summed"].after(ph, g), nstored.before(ph, i, b))
                        V.tensor_tensor(nres[b][:, :, :], bank[7][:, :].rearrange("p (j d) -> p j d", d=D),
                                        brow[p.node_bias][:, :].unsqueeze(1).to_broadcast([P, NT, D]),
                                        ALU.add).then_inc(s["nbiased"].sem, 1)
                    if p.resid:
                        wait(dve, s["biased"].after(ph, g), resid_in.after(ph, i, b))
                        V.tensor_tensor(res[b][:, :, :], res[b][:, :, :], resid[b][:, :, :],
                                        ALU.add).then_inc(s["resid_added"].sem, 1)
                    if p.node_resid:
                        wait(dve, s["nbiased"].after(ph, g), nresid_in.after(ph, i, b))
                        V.tensor_tensor(nres[b][:, :, :], nres[b][:, :, :], nresid[b][:, :, :],
                                        ALU.add).then_inc(s["nresid_added"].sem, 1)

                def variance(i, b, p=p, ph=ph):
                    g = 2 * i + b
                    if ph in s["squared"].at:
                        wait(dve, s["squared"].after(ph, g), s["std_ready"].after(ph, g - 1))
                        V.tensor_reduce(stat["var"][:, :], sq[b][:, :, :], AX.X, ALU.add).then_inc(
                            s["var_ready"].sem, 1)
                        if p.after == "norm_ln":
                            wait(dve, s["var_ready"].after(ph, g))
                            V.tensor_tensor(stat["var2"][:, :], stat["var"][:, :], inv_in[:, g, :],
                                            ALU.mult).then_inc(s["var2_ready"].sem, 1)
                    if ph in s["nsquared"].at:
                        wait(dve, s["nsquared"].after(ph, g), s["nstd_ready"].after(ph, g - 1))
                        V.tensor_reduce(nstat["var"][:, :], nsq[b][:, :, :], AX.X, ALU.add).then_inc(
                            s["nvar_ready"].sem, 1)

                def normalise(i, b, p=p, ph=ph):
                    g = 2 * i + b
                    if ph in s["std_ready"].at:
                        wait(dve, s["std_ready"].after(ph, g))
                        V.reciprocal(stat["rstd"][:, :], stat["std"][:, :]).then_inc(s["rstd_ready"].sem, 1)
                        wait(dve, s["rstd_ready"].after(ph, g))
                        a, r = res[b][:, :, :], stat["rstd"]
                        if p.after == "norm_ln":
                            V.tensor_tensor(stat["rstd2"][:, :], stat["rstd"][:, :], info_dst[:, g, :, 0],
                                            ALU.mult).then_inc(s["rstd2_ready"].sem, 1)
                            wait(dve, s["rstd2_ready"].after(ph, g), stored.before(ph, i, b))
                            a, r = bank[3 + b][:, 0:ET * D].rearrange("p (j d) -> p j d", d=D), stat["rstd2"]
                        V.tensor_tensor(res[b][:, :, :], a, bc(r[:, :], ET), ALU.mult).then_inc(
                            s["res_ready"].sem, 1)
                    if ph in s["nstd_ready"].at:
                        wait(dve, s["nstd_ready"].after(ph, g))
                        V.reciprocal(nstat["rstd"][:, :], nstat["std"][:, :]).then_inc(s["nrstd_ready"].sem, 1)
                        wait(dve, s["nrstd_ready"].after(ph, g))
                        a = nres[b][:, :, :]
                        if not p.node_bias:
                            wait(dve, nstored.before(ph, i, b))
                            a = bank[7][:, :].rearrange("p (j d) -> p j d", d=D)
                        V.tensor_tensor(nres[b][:, :, :], a, bc(nstat["rstd"][:, :], NT), ALU.mult).then_inc(
                            s["nres_ready"].sem, 1)

                def scan(i, b, p=p, ph=ph):
                    g = 2 * i + b
                    if ph in s["agg_ready"].at:
                        a = got_t[b] if p.msg is None else msg_t[b]
                        wait(dve, s["got_t_ready" if p.msg is None else "msg_ready"].after(ph, g),
                             side_in.after(ph, i, b))
                        if p.keep:
                            wait(dve, stored.before(ph, i, b))
                        else:
                            wait(dve, s["out_summed"].after(ph, g - 2))
                        wait(dve, s["agg_ready"].after(ph, g - 1))
                        if p.agg == "add":
                            last = V.tensor_tensor(key[b][0:D, :], got_t[b][:, :], side[b][:, :], ALU.add)
                        else:
                            last = V.tensor_tensor_scan(key[b][0:D, :], side[b][:, :], a[:, :],
                                                        key[1 - b][0:D, EG - 1:EG], p.agg[0], p.agg[1])
                        last.then_inc(s["agg_ready"].sem, 1)

                if n:
                    barrier(dve, n)
                for b in two:
                    fetch_idx(b, b)
                if p.scatter:
                    with dve.Fori(0, PAIRS - 1) as i:
                        for b in two:
                            receive(i, b)
                else:
                    order = [(1, receive), (0, add_up), (0, variance), (1, scan), (0, normalise)]
                    if ph == "l2a":
                        order.insert(2, (1, rank))
                    run_skewed(dve, order)


def kernel(x, src, dst, L1_gnn_W_lin, L1_gnn_b_lin, L1_gnn_W_rot, L1_gnn_b_rot, L2_gnn_W1, L2_gnn_b1, L2_gnn_W2,
           L2_gnn_b2, L2_gnn_W3, L2_gnn_b3, L3_gnn_W_pool, L3_gnn_b_pool, L3_gnn_W_self, L3_gnn_W_neigh, L3_gnn_bias):
    import numpy as np
    import concourse.bacc as bacc
    from concourse.bass_utils import run_bass_kernel_spmd as run

    def edges(a, pad):
        return np.concatenate([np.asarray(a), np.full(pad, NODES, a.dtype)])

    def by_partition(e):
        return np.ascontiguousarray(e.reshape(GROUPS, P, ET).transpose(1, 0, 2).reshape(P, COLS))

    src, dst = np.asarray(src), np.asarray(dst)
    pad = EDGES_PAD - EDGES
    s, d = edges(src, pad), edges(dst, pad)
    nxt = np.concatenate([d[1:], np.full(1, -1, d.dtype)])
    prev = np.concatenate([np.full(1, -1, d.dtype), d[:-1]])
    xp = np.zeros((NODES_PAD, D), np.float32)
    xp[:NODES] = x
    row = lambda v: np.asarray(v).reshape(1, D)
    ins = {
        "x": xp, "src_e": by_partition(s), "dst_e": by_partition(d), "next_e": by_partition(nxt),
        "src_tiles": np.ascontiguousarray(s.reshape(GROUPS, P, ET).transpose(0, 2, 1).reshape(GROUPS, 1, EG)),
        "dst_rows": d.reshape(GROUPS, EG), "prev_rows": prev.reshape(GROUPS, EG),
        "w_lin": np.ascontiguousarray(np.asarray(L1_gnn_W_lin).T), "b_lin": row(L1_gnn_b_lin),
        "w_rot": np.ascontiguousarray(np.asarray(L1_gnn_W_rot).T), "b_rot": row(L1_gnn_b_rot),
        "w1": L2_gnn_W1, "b1": row(L2_gnn_b1), "w2": L2_gnn_W2, "b2": row(L2_gnn_b2), "w3": L2_gnn_W3,
        "b3": row(L2_gnn_b3), "w_pool": L3_gnn_W_pool, "b_pool": np.ascontiguousarray(np.asarray(L3_gnn_b_pool).T),
        "w_self": L3_gnn_W_self, "w_neigh": L3_gnn_W_neigh, "bias": L3_gnn_bias,
    }
    nc = bacc.Bacc("TRN2", target_bir_lowering=False, num_devices=1)
    arrays, args = {}, []
    for name, a in ins.items():
        a = np.ascontiguousarray(a)
        arrays[f"in_{name}"] = a
        args.append(nc.dram_tensor(f"in_{name}", a.shape, mybir.dt.from_np(a.dtype), kind="ExternalInput").ap())
    args.append(nc.dram_tensor("out_rows", (NODES_PAD, D), F32, kind="ExternalOutput").ap())
    graph_kernel(nc, *args)
    r = run(nc, [arrays], core_ids=[0])
    return r.results[0]["out_rows"][:NODES]
```

```python
import concourse.bass as bass
from concourse import mybir
from contextlib import ExitStack

P = 128
D = 64
NODES, EDGES = 100000, 50000
PAIRS = 49
GROUPS = 2 * PAIRS
ET, NT = 4, 8
EG, NG = ET * P, NT * P
EDGES_PAD = GROUPS * EG
NODES_PAD = GROUPS * NG
SPARES = EG
COLS = GROUPS * ET
COLS_BUF = COLS + 2 * ET
HI = NODES_PAD // P
HALF = HI // 2
HT = HI // 7
INFO = 4
XW = D + INFO
EPS = 1e-5
FAR = -3.0e38
CREDIT = 2

F32, I32, U32, BF16, F16 = (mybir.dt.float32, mybir.dt.int32, mybir.dt.uint32, mybir.dt.bfloat16, mybir.dt.float16)
ALU, ACT, AX = mybir.AluOpType, mybir.ActivationFunctionType, mybir.AxisListType


class Phase:

    def __init__(self, name, fwd=None, fwd_idx=None, scale=None, rev=None, rev_scale=None, rev_sum=None, side=None,
                 msg=None, agg=None, keep=None, w=None, bias=None, self_rows=None, resid=None,
                 after=None, out=None, nodes=False, node_self=None, node_q=None, node_w=None,
                 node_bias=None, node_resid=None, node_after=None, node_out=None, scatter=False, build=None):
        self.name = name
        self.fwd, self.fwd_idx, self.scale = fwd, fwd_idx, scale
        self.rev, self.rev_scale, self.rev_sum = rev, rev_scale, rev_sum
        self.side = side
        self.msg = msg
        self.agg = agg
        self.keep = keep
        self.w, self.bias = w, bias
        self.self_rows, self.resid, self.after, self.out = self_rows, resid, after, out
        self.nodes, self.node_self, self.node_q, self.node_w = nodes, node_self, node_q, node_w
        self.node_bias, self.node_resid, self.node_after, self.node_out = node_bias, node_resid, node_after, node_out
        self.scatter = scatter
        self.build = build


class Step:

    def __init__(self, sem, phases, more=0):
        self.sem, self.each, self.at = sem, GROUPS + more, {p: n for n, p in enumerate(phases)}

    def after(self, ph, g):
        return self.sem, CREDIT + self.at[ph] * self.each + g + 1


class Arrivals:

    def __init__(self, sems, phases, each=1, primed=False):
        self.sems, self.at, self.each, self.primed = sems, {p: n for n, p in enumerate(phases)}, each, primed

    def after(self, ph, i, b):
        return self.sems[b], 16 * self.each * (self.at[ph] * PAIRS + i + 1) + 16 * self.primed

    def before(self, ph, i, b):
        return self.sems[b], 16 * self.each * (self.at[ph] * PAIRS + i) + 16 * self.primed

    def all(self, ph):
        return [self.after(ph, PAIRS - 1, b) for b in range(2)]


def wait(eng, *pairs):
    for sem, value in pairs:
        eng.wait_ge(sem, value)


def settle(eng, pace):
    eng.sem_inc(pace, 1)


def paced(eng, pace, *pairs):
    for pair in pairs:
        wait(eng, pair)
        settle(eng, pace)


def run_skewed(eng, steps):
    most = max(ahead for ahead, _ in steps)
    fours = (GROUPS - most) // 4
    for g in range(-most, 0):
        for ahead, do in steps:
            if g + ahead >= 0:
                do(*divmod(g + ahead, 2))
    with eng.Fori(0, fours) as i:
        for b in range(4):
            for ahead, do in steps:
                do(2 * i + (b + ahead) // 2, (b + ahead) % 2)
    for g in range(4 * fours, GROUPS):
        for ahead, do in steps:
            if g + ahead < GROUPS:
                do(*divmod(g + ahead, 2))


def graph_kernel(nc, x, src_e, dst_e, next_e, src_tiles, dst_rows, prev_rows, w_lin, b_lin, w_rot, b_rot,
                 w1, b1, w2, b2, w3, b3, w_pool, b_pool, w_self, w_neigh, bias, out):
    ctx = ExitStack()

    def dram(name, shape, dt=F32):
        return nc.dram_tensor(name, shape, dt).ap()

    STATES = ["T1", "T2", "H1", "H2", "T3", "G1", "G2"]
    info_d = dram("info_d", [NODES_PAD, INFO])
    table = {n: dram(n, [NODES_PAD + EDGES_PAD, D]) for n in STATES}
    table["XH"] = dram("XH", [NODES_PAD, XW])
    table["info"] = info_d
    table["XA"] = dram("XA", [EDGES_PAD, D])
    table["FA"] = dram("FA", [EDGES_PAD, D])
    table["S1"] = dram("S1", [NODES_PAD + SPARES, D])
    table["S2"] = dram("S2", [NODES_PAD + SPARES, D])
    F3 = dram("F3", [GROUPS, D, EG])
    same_d = dram("same_d", [GROUPS, EG])
    far_d = dram("far_d", [GROUPS, EG])
    prime_d = dram("prime_d", [16, 16])
    side_of = {"same": same_d, "far": far_d}

    def edge_rows(name):
        t = table[name]
        if name in STATES:
            t = t[NODES_PAD:NODES_PAD + EDGES_PAD, :]
        return t.rearrange("(g p j) d -> g p (j d)", p=P, j=ET)

    def node_rows(name):
        t = {"x": x, "out": out}.get(name)
        t = table[name][0:NODES_PAD, :] if t is None else t
        return t.rearrange("(g p j) d -> g p (j d)", p=P, j=NT)

    PHASES = [
        Phase("own", fwd="info", fwd_idx="dst", build="XH", nodes=True, node_self="x", node_w="centre",
              node_after="ln", node_out="T1"),
        Phase("l0", fwd="XH", fwd_idx="src", scale="norm", side="far", agg=(ALU.add, ALU.max), w="centre",
              self_rows="XA", after="norm_ln", out="T1", nodes=True, node_self="T1", node_w="rot", node_bias="l1",
              node_after="ln", node_out="T2"),
        Phase("l1", fwd="T1", fwd_idx="src_own", side="same", agg=(ALU.mult, ALU.add), w="l1", self_rows="T1",
              bias="l1", after="ln", out="T2", nodes=True, node_self="T2", node_w="w1a", node_bias="b1",
              node_after="relu", node_out="H1"),
        Phase("l2a", fwd="T2", fwd_idx="src_own", scale="inv_out", side="same", agg=(ALU.mult, ALU.add), w="w1",
              self_rows="T2", bias="b1", after="relu", out="H1"),
        Phase("sum1", rev="H1", rev_scale="inv_in", rev_sum="S1"),
        Phase("l2b", fwd="S1", fwd_idx="dst", agg="pass", w="w2", self_rows="H1", bias="b2", after="relu", out="H2",
              nodes=True, node_self="H1", node_q="S1", node_w="w2", node_bias="b2", node_after="relu", node_out="H2"),
        Phase("sum2", fwd="H2", fwd_idx="src_own", scale="inv_all", side="same", agg=(ALU.mult, ALU.add), keep="F3",
              rev="H2", rev_scale="inv_all_dst", rev_sum="S2"),
        Phase("l2c", fwd="S2", fwd_idx="dst", side="F3", agg="add", w="w3", self_rows="H2", resid="T2", bias="b3",
              after="ln", out="T3", nodes=True, node_self="H2", node_q="S2", node_w="w3", node_bias="b3",
              node_resid="T2", node_after="ln", node_out="T3"),
    ]
    for n, (before, name) in enumerate((("T3", "G1"), ("G1", "G2"), ("G2", "FA"))):
        last = n == 2
        PHASES.append(Phase(
            "l3" + "abc"[n], fwd=before, fwd_idx="src_own", side="same", msg=n, agg=(ALU.mult, ALU.max), w=f"conv{n}",
            self_rows=before, resid="T3" if last else None, bias=f"bias{n}", after="ln" if last else "relu", out=name,
            nodes=True, node_self=before, node_w=f"self{n}", node_bias=f"bias{n}", node_resid="T3" if last else None,
            node_after="ln" if last else "relu", node_out="out" if last else name))
    PHASES.append(Phase("scatter", scatter=True))

    def which(test):
        return [p.name for p in PHASES if test(p)]

    def lead(p):
        if p.rev:
            return dict(load_rows=3, load_side=2, load_nodes=2, receive=2, turn=2, message=1, scan=1, combine=0,
                        post=0, turn_nodes=2, combine_nodes=0)
        scaled = 1 if p.scale else 0
        return dict(load_rows=4 + scaled, load_side=3, load_nodes=3 if p.build else 4,
                    receive=1 if p.build else 3 + scaled, turn=3, message=3, scan=2, combine=2, post=1,
                    turn_nodes=2 if p.build else 3, combine_nodes=1 if p.build else 2)

    with ctx:
        def sb(name, shape, dt=F32):
            return ctx.enter_context(nc.sbuf_tensor(name, shape, dt))

        def sem(name):
            return ctx.enter_context(nc.semaphore(name))

        bank = [ctx.enter_context(nc.psum_tensor(f"bank{n}", [P, 512], F32)) for n in range(8)]

        eye = sb("eye", [P, P])
        tri = sb("tri", [P, P])
        ones = sb("ones", [P, P])
        idx_all = {n: sb(f"idx_{n}", [P, COLS_BUF], U32) for n in ("dst", "src", "src_own", "dst_own", "sum", "out")}
        src_f = sb("src_f", [P, COLS_BUF])
        info_src = sb("info_src", [P, GROUPS, ET, INFO])
        info_dst = sb("info_dst", [P, GROUPS, ET, INFO])
        inv_in = sb("inv_in", [P, GROUPS, ET])
        spare = sb("spare", [P, ET])
        before = sb("before", [P, EG])
        eps = sb("eps", [P, 1])
        zero = sb("zero", [P, 1024])

        STACKS = {"l1": (w_lin, w_rot), "w1": (w1[D:2 * D, :], w1[0:D, :]), "w2": (w2[D:2 * D, :], w2[0:D, :]),
                  "w3": (w3[D:2 * D, :], w3[0:D, :])}
        for n in range(3):
            STACKS[f"conv{n}"] = (w_neigh[n], w_self[n])
        PAIRED = {"rot": w_rot, "w1a": w1[0:D, :]}
        for n in range(3):
            PAIRED[f"self{n}"] = w_self[n]
        stacked = {n: sb(f"stack_{n}", [P, D]) for n in [*STACKS, "centre"]}
        pair = {n: sb(f"pair_{n}", [P, P]) for n in [*PAIRED, "centre"]}
        pool_w = [sb(f"pool_w{n}", [D, D]) for n in range(3)]
        B_ROWS = {"l1": b_lin, "rot": b_rot, "b1": b1, "b2": b2, "b3": b3}
        for n in range(3):
            B_ROWS[f"bias{n}"] = bias[n:n + 1, :]
        brow = {n: sb(f"brow_{n}", [P, D]) for n in B_ROWS}
        row_mean = sb("row_mean", [P, 2])
        b_pool_col = sb("b_pool_col", [D, 3])

        two = range(2)
        ib = [sb(f"ib{b}", [P, ET], U32) for b in two]
        ib2 = [sb(f"ib2{b}", [P, ET], U32) for b in two]
        ib3 = [sb(f"ib3{b}", [P, ET], U32) for b in two]
        got = [sb(f"got{b}", [P, ET, XW]) for b in two]
        stack = [sb(f"stack{b}", [P, ET, 2 * D]) for b in two]
        got2 = [sb(f"got2{b}", [P, ET, D]) for b in two]
        scaled2 = [sb(f"scaled2{b}", [P, ET, D]) for b in two]
        src_row = [sb(f"src_row{b}", [P, EG], I32) for b in two]
        wide = sb("wide", [P, 2 * ET * EG])
        equal = [wide[:, b * ET * EG:(b + 1) * ET * EG].rearrange("p (k e) -> p k e", k=ET) for b in two]
        summed = [sb(f"summed{b}", [P, ET, D]) for b in two]
        side = [sb(f"side{b}", [D, EG]) for b in two]
        got_t = [sb(f"got_t{b}", [D, EG]) for b in two]
        msg_t = [sb(f"msg_t{b}", [D, EG]) for b in two]
        key = [sb(f"key{b}", [P, EG]) for b in two]
        resid = [sb(f"resid{b}", [P, ET, D]) for b in two]
        res = [sb(f"res{b}", [P, ET, D]) for b in two]
        nrows = [sb(f"nrows{b}", [P, NT, D]) for b in two]
        wide_n = sb("wide_n", [P, 4 * NT * P])
        nstack = [wide_n[:, b * NT * P:(b + 1) * NT * P].rearrange("p (j d) -> p j d", j=NT) for b in two]
        nresid = [sb(f"nresid{b}", [P, NT, D]) for b in two]
        nt = [wide_n[:, (2 + b) * NT * P:(3 + b) * NT * P] for b in two]
        nres = [sb(f"nres{b}", [P, NT, D]) for b in two]
        sq = [sb(f"sq{b}", [P, ET, D]) for b in two]
        nsq = [sb(f"nsq{b}", [P, NT, D]) for b in two]
        stat = {k: sb(f"stat_{k}", [P, ET]) for k in ("var", "var2", "std", "rstd", "rstd2")}
        nstat = {k: sb(f"nstat_{k}", [P, NT]) for k in ("var", "std", "rstd")}

        fwd_ph = which(lambda p: p.fwd)
        rev_ph = which(lambda p: p.rev)
        scat_ph = which(lambda p: p.scatter)
        agg_ph = which(lambda p: p.agg)
        edge_ph = which(lambda p: p.w)
        out_ph = which(lambda p: p.out)
        node_ph = which(lambda p: p.nodes)
        msg_ph = which(lambda p: p.msg is not None)
        ln_ph = which(lambda p: p.after in ("ln", "norm_ln"))
        nln_ph = which(lambda p: p.node_after == "ln")
        steps = {}

        every = [p.name for p in PHASES]
        for name, phases in (
                ("idx_ready", fwd_ph + scat_ph), ("idx2_ready", rev_ph), ("idx3_ready", rev_ph),
                ("got_used", which(lambda p: p.scale or p.build)), ("xh_info_put", ["own"]),
                ("got2_used", rev_ph), ("equal_ready", which(lambda p: p.rev or p.name == "l2a")), ("dup_found", ["l2a"]),
                ("spare_off", ["l2a"]), ("dup_off", ["l2a"]),
                ("turned", agg_ph), ("nturned", node_ph), ("msg_summed", msg_ph), ("deduped", rev_ph),
                ("out_summed", edge_ph), ("nout_summed", node_ph),
                ("xh_rows_put", ["own"]), ("got_t_ready", agg_ph), ("own_t_ready", which(lambda p: p.w and p.agg != "pass")),
                ("nt_ready", node_ph), ("msg_ready", msg_ph), ("summed_ready", rev_ph),
                ("squared", ln_ph), ("nsquared", nln_ph), ("std_ready", ln_ph), ("nstd_ready", nln_ph),
                ("agg_ready", which(lambda p: p.agg and p.agg != "pass")),
                ("biased", which(lambda p: p.bias)), ("nbiased", which(lambda p: p.node_bias)),
                ("resid_added", which(lambda p: p.resid)), ("nresid_added", which(lambda p: p.node_resid)),
                ("var_ready", ln_ph), ("nvar_ready", nln_ph), ("var2_ready", ["l0"]),
                ("rstd_ready", ln_ph), ("nrstd_ready", nln_ph), ("rstd2_ready", ["l0"]),
                ("res_ready", out_ph), ("nres_ready", node_ph)):
            steps[name] = Step(sem(name), phases, 2 if name in ("idx_ready", "idx2_ready") else 0)
        s = steps

        def pairof(name):
            return [sem(f"{name}{b}") for b in two]

        early, late = every[:6], every[6:]
        gathered_1 = Arrivals(pairof("gathered_a"), [p for p in fwd_ph if p in early], ET)
        gathered_2 = Arrivals(pairof("gathered_b"), [p for p in fwd_ph if p in late], ET)

        def gathered(ph):
            return gathered_1 if ph in early else gathered_2

        gathered_rev = Arrivals(pairof("gathered_rev"), rev_ph, ET)
        scattered = Arrivals(pairof("scattered"), scat_ph, ET)
        side_in = Arrivals(pairof("side_in"), which(lambda p: p.side))
        srow_in = Arrivals(pairof("srow_in"), which(lambda p: p.rev or p.name == "l2a"))
        rows_in = Arrivals(pairof("rows_in"), which(lambda p: p.self_rows))
        resid_in = Arrivals(pairof("resid_in"), which(lambda p: p.resid or p.scatter))
        nrows_in = Arrivals(pairof("nrows_in"), node_ph)
        nq_in = Arrivals(pairof("nq_in"), which(lambda p: p.node_q))
        nresid_in = Arrivals(pairof("nresid_in"), which(lambda p: p.node_resid))
        stored = Arrivals(pairof("stored"), which(lambda p: p.out or p.keep), primed=True)
        nstored = Arrivals(pairof("nstored"), node_ph, primed=True)
        added = sem("added")
        consts_in, zeroed, prep_in = sem("consts_in"), sem("zeroed"), sem("prep_in")
        pool_built, dve_chain, act_chain, pe_chain = sem("pool_built"), sem("dve_chain"), sem("act_chain"), sem("pe_chain")
        hot_ready, hot_used = sem("hot_ready"), sem("hot_used")
        info_out = sem("info_out")
        xh_in = Arrivals(pairof("xh_in"), ["own"])
        xh_out = Arrivals(pairof("xh_out"), ["own"], primed=True)
        xa_idx, xa_in, xa_out = sem("xa_idx"), pairof("xa_in"), pairof("xa_out")
        masks_out, masks_ready, info_ready = sem("masks_out"), sem("masks_ready"), sem("info_ready")

        def nbank(p, b):
            return bank[7 if p.node_q else 6 + b]

        def barrier(eng, n):
            if n == 0:
                wait(eng, (info_out, 16 * 7), (masks_out, 32), (zeroed, 32 * (GROUPS + 1)))
                return
            before = PHASES[n - 1]
            if before.name in stored.at:
                wait(eng, *stored.all(before.name))
            if before.nodes:
                wait(eng, *nstored.all(before.name))
            if before.build:
                wait(eng, *xh_out.all(before.name), (xa_out[0], 16 * PAIRS), (xa_out[1], 16 * PAIRS))
            if before.rev:
                wait(eng, (added, 16 * COLS * (rev_ph.index(before.name) + 1) + 16))

        hot_lo = [[sb(f"hot_lo{k}{b}", [P, P], BF16) for b in two] for k in two]
        hot_hi = [[sb(f"hot_hi{k}{b}", [P, HI], BF16) for b in two] for k in two]
        count_up = sb("count_up", [P, HI], F16)
        count_i = sb("count_i", [P, HI], I32)
        node_i = sb("node_i", [P, HI], I32)
        edge_i = [sb(f"edge_i{k}", [P, COLS], I32) for k in range(3)]
        part_i = sb("part_i", [P, ET], I32)
        lo_f = [sb(f"lo_f{k}", [P, COLS]) for k in two]
        hi_f = [sb(f"hi_f{k}", [P, COLS]) for k in two]
        root = lo_f[0][:, :].rearrange("p (g j) -> p g j", j=ET)
        deg = [sb(f"deg{k}", [P, HI]) for k in two]
        field = [wide[:, k * HI:(k + 1) * HI] for k in range(INFO)]
        tmp = sb("tmp", [P, HI])
        info_t = wide_n[0:HT, 0:7 * P * INFO].rearrange("h (k l f) -> h k l f", k=7, f=INFO)
        xh = [sb(f"xh{b}", [P, NT, XW]) for b in two]
        xh_info = [sb(f"xh_info{b}", [P, NT * INFO]) for b in two]
        drow = sb("drow", [GROUPS, EG], I32)
        prow = sb("prow", [GROUPS, EG], I32)
        same = sb("same", [GROUPS, EG])
        far = sb("far", [GROUPS, EG])
        last_f = sb("last_f", [P, COLS])
        dst_f = sb("dst_f", [P, COLS])
        shifted = sb("shifted", [P, COLS], I32)
        prefix = sb("prefix", [P, HI])
        dup = sb("dup", [P, 3, ET])
        links, sp_pace, pool_pace, pe_pace = sem("links"), sem("sp_pace"), sem("pool_pace"), sem("pe_pace")

        block = ctx.enter_context(nc.Block())
        N_CONSTS = 2 * len(STACKS) + 2 * len(PAIRED) + 3 + len(B_ROWS) + 1

        def scale_of(p, kind, g):
            ap = {"norm": info_src[:, g, :, 0], "inv_out": info_src[:, g, :, 1], "inv_all": info_src[:, g, :, 2],
                  "inv_all_dst": info_dst[:, g, :, 2], "inv_in": inv_in[:, g, :]}[kind]
            return ap.unsqueeze(2).to_broadcast([P, ET, D])

        @block.sync
        def _(sp):
            for name in steps:
                sp.sem_inc(steps[name].sem, CREDIT)
            for k, a in enumerate((src_e, dst_e, next_e)):
                sp.dma_start(edge_i[k][:, :], a).then_inc(prep_in, 16)
            sp.dma_start(drow[:, :], dst_rows).then_inc(prep_in, 16)
            sp.dma_start(prow[:, :], prev_rows).then_inc(prep_in, 16)
            paced(sp, sp_pace, (pool_built, 2))
            for name, halves in STACKS.items():
                for k in two:
                    sp.dma_start(stacked[name][D * k:D * (k + 1), :], halves[k]).then_inc(consts_in, 16)
            for name, w in PAIRED.items():
                for k in two:
                    sp.dma_start(pair[name][D * k:D * (k + 1), D * k:D * (k + 1)], w).then_inc(consts_in, 16)
            for n in range(3):
                sp.dma_start(pool_w[n][:, :], w_pool[n]).then_inc(consts_in, 16)
            for name, v in B_ROWS.items():
                sp.dma_start(brow[name][:, :], v.to_broadcast([P, D])).then_inc(consts_in, 16)
            sp.dma_start(b_pool_col[:, :], b_pool).then_inc(consts_in, 16)
            for n, sm in enumerate(stored.sems + nstored.sems + xh_out.sems):
                sp.dma_start(prime_d[n:n + 1, :], zero[0:1, 0:16]).then_inc(sm, 16)
            with sp.Fori(0, PAIRS) as i:
                for b in two:
                    g = 2 * i + b
                    for name in ("S1", "S2"):
                        sp.dma_start(node_rows(name)[g], zero[:, 0:NT * D]).then_inc(zeroed, 16)
                    paced(sp, sp_pace, (xa_in[b], 16 * ET * (i + 1)))
                    sp.dma_start(edge_rows("XA")[g], res[b][:, :, :].rearrange("p j d -> p (j d)")).then_inc(
                        xa_out[b], 16)
            for name in ("S1", "S2"):
                sp.dma_start(table[name][NODES_PAD:, :].rearrange("(p j) d -> p (j d)", p=P),
                             zero[:, 0:ET * D]).then_inc(zeroed, 16)
            paced(sp, sp_pace, (masks_ready, 1))
            sp.dma_start(same_d, same[:, :]).then_inc(masks_out, 16)
            sp.dma_start(far_d, far[:, :]).then_inc(masks_out, 16)
            paced(sp, sp_pace, (info_ready, 7))
            info_rows = info_d.rearrange("(k h l) f -> k h (l f)", k=7, l=P)
            for k in range(7):
                sp.dma_start(info_rows[k], info_t[:, k, :, :].rearrange("h l f -> h (l f)")).then_inc(info_out, 16)
            info_in = info_d.rearrange("(g p j) f -> g p (j f)", p=P, j=NT)

            for n, p in enumerate(PHASES):
                ph = p.name
                barrier(sp, n)

                def load_side(i, b, p=p, ph=ph):
                    g = 2 * i + b
                    if p.build:
                        paced(sp, sp_pace, s["xh_info_put"].after(ph, g - 2))
                        sp.dma_start(xh_info[b][:, :], info_in[g]).then_inc(xh_in.sems[b], 16)
                    if p.rev or ph == "l2a":
                        paced(sp, sp_pace, s["equal_ready"].after(ph, g - 2))
                        sp.dma_start(src_row[b][:, :], src_tiles[g].to_broadcast([P, EG])).then_inc(srow_in.sems[b], 16)
                    if p.side:
                        paced(sp, sp_pace, s["agg_ready"].after(ph, g - 2))
                        a = F3[g] if p.side == "F3" else side_of[p.side][bass.ds(g, 1), :].to_broadcast([D, EG])
                        sp.dma_start(side[b][:, :], a).then_inc(side_in.sems[b], 16)

                def load_resid(i, b, p=p, ph=ph):
                    g = 2 * i + b
                    if p.resid:
                        paced(sp, sp_pace, s["resid_added"].after(ph, g - 2))
                        sp.dma_start(resid[b][:, :, :].rearrange("p j d -> p (j d)"),
                                     edge_rows(p.resid)[g]).then_inc(resid_in.sems[b], 16)
                    if p.node_resid:
                        paced(sp, sp_pace, s["nresid_added"].after(ph, g - 2))
                        sp.dma_start(nresid[b][:, :, :].rearrange("p j d -> p (j d)"),
                                     node_rows(p.node_resid)[g]).then_inc(nresid_in.sems[b], 16)

                def load_rows(i, b, p=p, ph=ph):
                    g = 2 * i + b
                    if p.self_rows:
                        paced(sp, sp_pace, s["turned"].after(ph, g - 2))
                        sp.dma_start(stack[b][:, :, D:2 * D], edge_rows(p.self_rows)[g].rearrange(
                            "p (j d) -> p j d", d=D)).then_inc(rows_in.sems[b], 16)

                def load_nodes(i, b, p=p, ph=ph):
                    g = 2 * i + b
                    if p.nodes:
                        paced(sp, sp_pace, s["nturned"].after(ph, g - 2))
                        if p.build:
                            paced(sp, sp_pace, s["xh_rows_put"].after(ph, g - 2))
                        a = node_rows(p.node_self)[g].rearrange("p (j d) -> p j d", d=D)
                        if p.node_q:
                            sp.dma_start(nstack[b][:, :, D:2 * D], a).then_inc(nrows_in.sems[b], 16)
                            sp.dma_start(nstack[b][:, :, 0:D], node_rows(p.node_q)[g].rearrange(
                                "p (j d) -> p j d", d=D)).then_inc(nq_in.sems[b], 16)
                        else:
                            sp.dma_start(nrows[b][:, :, :], a).then_inc(nrows_in.sems[b], 16)

                def store(i, b, p=p, ph=ph):
                    g = 2 * i + b
                    if p.build:
                        paced(sp, sp_pace, s["xh_rows_put"].after(ph, g), s["xh_info_put"].after(ph, g))
                        sp.dma_start(node_rows(p.build)[g], xh[b][:, :, :].rearrange("p j w -> p (j w)")).then_inc(
                            xh_out.sems[b], 16)
                    if p.keep:
                        paced(sp, sp_pace, s["agg_ready"].after(ph, g))
                        sp.dma_start(F3[g], key[b][0:D, :]).then_inc(stored.sems[b], 16)
                    if p.out:
                        paced(sp, sp_pace, s["res_ready"].after(ph, g))
                        sp.dma_start(edge_rows(p.out)[g], res[b][:, :, :].rearrange("p j d -> p (j d)")).then_inc(
                            stored.sems[b], 16)
                    if p.nodes:
                        paced(sp, sp_pace, s["nres_ready"].after(ph, g))
                        sp.dma_start(node_rows(p.node_out)[g],
                                     nres[b][:, :, :].rearrange("p j d -> p (j d)")).then_inc(nstored.sems[b], 16)

                def load_res(i, b, ph=ph):
                    if not isinstance(i, int) or i > 0:
                        paced(sp, sp_pace, scattered.before(ph, i, b))
                    sp.dma_start(res[b][:, :, :].rearrange("p j d -> p (j d)"),
                                 edge_rows("FA")[2 * i + b]).then_inc(resid_in.sems[b], 16)

                if p.scatter:
                    for b in two:
                        load_res(0, b)
                    with sp.Fori(1, PAIRS) as i:
                        for b in two:
                            load_res(i, b)
                else:
                    a = lead(p)
                    run_skewed(sp, ((a["load_rows"], load_rows), (a["load_side"], load_side), (0, store),
                                    (a["load_nodes"], load_nodes), (3, load_resid)))
            paced(sp, sp_pace, *scattered.all("scatter"))

        @block.gpsimd
        def _(pool):
            nc.gpsimd.memset(zero[:, :], 0.0)
            nc.gpsimd.memset(ones[:, :], 1.0)
            for name in pair:
                nc.gpsimd.memset(pair[name][:, :], 0.0)
            nc.gpsimd.memset(eye[:, :], 0.0)
            for b in two:
                nc.gpsimd.memset(key[b][:, :], 0.0)
            nc.gpsimd.memset(before[:, 0:3 * P], 1.0)
            nc.gpsimd.memset(eps[:, :], EPS).then_inc(pool_built, 1)
            pool.wait_ge(pool_built, 1)
            nc.gpsimd.affine_select(out=eye[:, :], in_=eye[:, :], compare_op=ALU.not_equal, fill=1.0, base=0,
                                    pattern=[[-1, P]], channel_multiplier=1)
            nc.gpsimd.affine_select(out=tri[:, :], in_=ones[:, :], compare_op=ALU.is_ge, fill=0.0, base=0,
                                    pattern=[[1, P]], channel_multiplier=-1)
            nc.gpsimd.affine_select(out=before[:, 3 * P:EG], in_=ones[:, :], compare_op=ALU.is_gt, fill=0.0, base=0,
                                    pattern=[[-1, P]], channel_multiplier=1)
            nc.gpsimd.iota(count_i[:, :], pattern=[[1, HI]], base=0, channel_multiplier=0)
            nc.gpsimd.iota(node_i[:, :], pattern=[[P, HI]], base=0, channel_multiplier=1)
            nc.gpsimd.iota(part_i[:, :], pattern=[[P, ET]], base=NODES_PAD, channel_multiplier=1).then_inc(pool_built, 1)

            pool.dma_start(prime_d[8:9, :], zero[0:1, 0:16]).then_inc(added, 16)

            def gather_x(i, b):
                g = 2 * i + b
                wait(pool, (xa_idx, g + 1))
                if not isinstance(i, int):
                    wait(pool, (xa_out[b], 16 * i))
                settle(pool, pool_pace)
                for j in range(ET):
                    pool.indirect_dma_start(res[b][:, j, :], None, x,
                                            bass.IndirectOffsetOnAxis(ib[b][:, j:j + 1], 0)).then_inc(xa_in[b], 16)

            for b in two:
                gather_x(0, b)
            with pool.Fori(1, PAIRS) as i:
                for b in two:
                    gather_x(i, b)

            for n, p in enumerate(PHASES):
                ph = p.name
                barrier(pool, n)

                def gather(i, b, p=p, ph=ph):
                    g = 2 * i + b
                    if p.fwd:
                        wait(pool, s["idx_ready"].after(ph, g))
                        if ph in s["got_used"].at:
                            wait(pool, s["got_used"].after(ph, g - 2))
                        else:
                            wait(pool, s["turned"].after(ph, g - 2))
                    if p.rev:
                        wait(pool, s["idx2_ready"].after(ph, g), s["got2_used"].after(ph, g - 2))
                    settle(pool, pool_pace)
                    width = {"XH": XW, "info": INFO}.get(p.fwd, D)
                    for j in range(ET):
                        if p.fwd:
                            to = got[b][:, j, 0:width] if ph in s["got_used"].at else stack[b][:, j, 0:D]
                            pool.indirect_dma_start(
                                to, None, table[p.fwd],
                                bass.IndirectOffsetOnAxis(ib[b][:, j:j + 1], 0)).then_inc(gathered(ph).sems[b], 16)
                        if p.rev:
                            pool.indirect_dma_start(
                                got2[b][:, j, :], None, table[p.rev],
                                bass.IndirectOffsetOnAxis(ib2[b][:, j:j + 1], 0)).then_inc(gathered_rev.sems[b], 16)

                def put(i, b, p=p, ph=ph):
                    g = 2 * i + b
                    if p.rev:
                        wait(pool, s["summed_ready"].after(ph, g), s["idx3_ready"].after(ph, g))
                        pool.wait_ge(added, 16 * (COLS * rev_ph.index(ph) + ET * g) + 16)
                        settle(pool, pool_pace)
                        for j in range(ET):
                            pool.indirect_dma_start(
                                table[p.rev_sum], bass.IndirectOffsetOnAxis(ib3[b][:, j:j + 1], 0),
                                summed[b][:, j, :], None, compute_op=ALU.add).then_inc(added, 16)

                if p.scatter:
                    def scatter(i, b, ph=ph):
                        g = 2 * i + b
                        wait(pool, s["idx_ready"].after(ph, g), resid_in.after(ph, i, b))
                        settle(pool, pool_pace)
                        for j in range(ET):
                            pool.indirect_dma_start(
                                out, bass.IndirectOffsetOnAxis(ib[b][:, j:j + 1], 0),
                                res[b][:, j, :], None, bounds_check=NODES_PAD - 1,
                                oob_is_err=False).then_inc(scattered.sems[b], 16)
                    with pool.Fori(0, PAIRS) as i:
                        for b in two:
                            scatter(i, b)
                elif p.rev:
                    gather(0, 0)
                    gather(0, 1)
                    with pool.Fori(0, PAIRS - 1) as i:
                        for b in two:
                            put(i, b)
                            gather(i + 1, b)
                    put(PAIRS - 1, 0)
                    put(PAIRS - 1, 1)
                else:
                    with pool.Fori(0, PAIRS) as i:
                        for b in two:
                            gather(i, b)

        @block.tensor
        def _(pe):
            T = nc.tensor
            pe.wait_ge(pool_built, 2)
            wait(pe, (dve_chain, 1))
            for k in range(4):
                T.matmul(bank[k][:, 0:HALF], hot_lo[0][0][:, :], hot_hi[0][0][:, 0:HALF], start=True, stop=False,
                         skip_group_check=True)
            T.matmul(bank[4][:, 0:P], hot_lo[0][0][:, :], hot_lo[0][0][:, :], start=True,
                     stop=True).then_inc(hot_used, 2)
            with pe.Fori(0, COLS // 2) as i:
                for b in two:
                    pe.wait_ge(hot_ready, 2 * i + b + 1)
                    for k in two:
                        for h in two:
                            last = T.matmul(bank[2 * k + h][:, 0:HALF], hot_lo[k][b][:, :],
                                            hot_hi[k][b][:, h * HALF:(h + 1) * HALF], start=False, stop=False,
                                            skip_group_check=True)
                    last.then_inc(hot_used, 1)
            pe.wait_ge(hot_ready, COLS + 1)
            for k in range(4):
                last = T.matmul(bank[k][:, 0:HALF], hot_lo[0][0][:, :], hot_hi[0][0][:, 0:HALF], start=False, stop=True,
                                skip_group_check=True)
            last.then_inc(pe_chain, 1)
            pe.wait_ge(act_chain, 1)
            for h in two:
                T.matmul(bank[4 + h][:, 0:HALF], tri[:, :], deg[1][:, h * HALF:(h + 1) * HALF], start=True, stop=True)
            for h in two:
                last = T.matmul(bank[6 + h][:, 0:HALF], ones[:, :], deg[1][:, h * HALF:(h + 1) * HALF], start=True,
                                stop=True)
            last.then_inc(pe_chain, 1)
            pe.wait_ge(act_chain, 3)
            for k in range(7):
                if k >= 2:
                    pe.wait_ge(info_ready, k - 1)
                for f in range(INFO):
                    last = T.transpose(bank[k % 2][0:HT, f * P:(f + 1) * P], field[f][:, k * HT:(k + 1) * HT], eye[:, :])
                last.then_inc(pe_chain, 1)

            pe.wait_ge(consts_in, 16 * N_CONSTS)
            pe.wait_ge(dve_chain, 4)
            for n, p in enumerate(PHASES):
                ph = p.name

                def turn(i, b, p=p, ph=ph):
                    g = 2 * i + b
                    if p.agg:
                        wait(pe, s["got_used"].after(ph, g) if p.scale else gathered(ph).after(ph, i, b))
                        if p.self_rows:
                            wait(pe, rows_in.after(ph, i, b))
                        wait(pe, s["got_t_ready"].after(ph, g - 2))
                        if ph in s["own_t_ready"].at:
                            wait(pe, s["own_t_ready"].after(ph, g - 2))
                        settle(pe, pe_pace)
                        width = 2 * D if p.self_rows else D
                        for j in range(ET):
                            last = T.transpose(bank[b][0:width, j * P:(j + 1) * P], stack[b][:, j, 0:width], eye[:, :])
                        last.then_inc(s["turned"].sem, 1)

                def turn_nodes(i, b, p=p, ph=ph):
                    g = 2 * i + b
                    if p.nodes:
                        wait(pe, nrows_in.after(ph, i, b), s["nt_ready"].after(ph, g - 1))
                        if p.node_q:
                            wait(pe, nq_in.after(ph, i, b))
                        settle(pe, pe_pace)
                        for j in range(NT if p.node_q else NT // 2):
                            a = (nstack[b][:, j, :] if p.node_q
                                 else nrows[b][:, 2 * j:2 * j + 2, :].rearrange("p j d -> p (j d)"))
                            last = T.transpose(bank[5 + j // 4][:, j % 4 * P:(j % 4 + 1) * P], a, eye[:, :])
                        last.then_inc(s["nturned"].sem, 1)

                def combine(i, b, p=p, ph=ph):
                    g = 2 * i + b
                    if p.w:
                        if p.agg == "pass":
                            wait(pe, s["got_t_ready"].after(ph, g))
                        else:
                            wait(pe, s["agg_ready"].after(ph, g), s["own_t_ready"].after(ph, g))
                        wait(pe, s["biased" if p.bias else "res_ready"].after(ph, g - 2))
                        settle(pe, pe_pace)
                        a = key[b][:, :].rearrange("c (q j) -> c q j", j=ET)
                        for j in range(ET):
                            last = T.matmul(bank[3 + b][:, j * D:(j + 1) * D], a[:, :, j], stacked[p.w][:, :],
                                            start=True, stop=True)
                        last.then_inc(s["out_summed"].sem, 1)

                def combine_nodes(i, b, p=p, ph=ph):
                    g = 2 * i + b
                    if p.nodes:
                        wait(pe, s["nt_ready"].after(ph, g),
                             s["nbiased" if p.node_bias else "nres_ready"].after(ph, g - (1 if p.node_q else 2)))
                        settle(pe, pe_pace)
                        if p.node_q:
                            for j in range(NT):
                                last = T.matmul(nbank(p, b)[:, j * D:(j + 1) * D], nt[b][:, j * P:(j + 1) * P],
                                                stacked[p.node_w][:, :], start=True, stop=True)
                        else:
                            for j in range(NT // 2):
                                cols = slice(j * P, (j + 1) * P)
                                last = T.matmul(nbank(p, b)[:, cols], nt[b][:, cols], pair[p.node_w][:, :], start=True,
                                                stop=True)
                        last.then_inc(s["nout_summed"].sem, 1)

                def message(i, b, p=p, ph=ph):
                    g = 2 * i + b
                    if p.msg is not None:
                        wait(pe, s["got_t_ready"].after(ph, g), s["msg_ready"].after(ph, g - 1))
                        settle(pe, pe_pace)
                        T.matmul(bank[2][0:D, :], pool_w[p.msg][:, :], got_t[b][:, :], start=True,
                                 stop=True).then_inc(s["msg_summed"].sem, 1)
                    if p.rev:
                        wait(pe, s["equal_ready"].after(ph, g), s["got2_used"].after(ph, g),
                             s["summed_ready"].after(ph, g - 1))
                        settle(pe, pe_pace)
                        for j in range(ET):
                            for k in range(j, ET):
                                last = T.matmul(bank[2][:, j * D:(j + 1) * D], equal[b][:, k, j * P:(j + 1) * P],
                                                scaled2[b][:, k, :], start=k == j, stop=k == ET - 1)
                        last.then_inc(s["deduped"].sem, 1)

                if not p.scatter:
                    a = lead(p)
                    if p.rev:
                        run_skewed(pe, ((a["message"], message), (a["turn"], turn)))
                    elif not p.bias:
                        run_skewed(pe, ((a["turn"], turn), (a["combine_nodes"], combine_nodes),
                                        (a["turn_nodes"], turn_nodes), (a["combine"], combine)))
                    else:
                        run_skewed(pe, ((a["turn"], turn), (a["combine"], combine), (a["message"], message),
                                        (a["combine_nodes"], combine_nodes), (a["turn_nodes"], turn_nodes)))

        @block.scalar
        def _(act):
            A = nc.scalar
            act.wait_ge(pe_chain, 1)
            for k in two:
                for h in two:
                    last = A.copy(deg[k][:, h * HALF:(h + 1) * HALF], bank[2 * k + h][:, 0:HALF])
            last.then_inc(act_chain, 1)
            act.wait_ge(dve_chain, 2)
            act.wait_ge(pool_built, 2)
            A.activation(tmp[:, :], field[0][:, :], ACT.Sqrt).then_inc(act_chain, 1)
            act.wait_ge(dve_chain, 3)
            A.copy(eps[0:1, :], eps[0:1, :]).then_inc(act_chain, 1)
            for k in range(7):
                act.wait_ge(pe_chain, 3 + k)
                A.copy(info_t[:, k, :, :].rearrange("h l f -> h f l"),
                       bank[k % 2][0:HT, :].rearrange("h (f l) -> h f l", f=INFO)).then_inc(info_ready, 1)

            for n, p in enumerate(PHASES):
                ph = p.name

                def evacuate(i, b, p=p, ph=ph):
                    g = 2 * i + b
                    if p.agg:
                        whole = p.agg == "pass"
                        reader = "msg_summed" if p.msg is not None else "out_summed" if whole else "agg_ready"
                        wait(act, s["turned"].after(ph, g), s[reader].after(ph, g - 2))
                        to = key[b][:, :] if whole else got_t[b][:, :]
                        A.copy(to.rearrange("c (q j) -> c j q", j=ET),
                               bank[b][0:P if whole else D, :].rearrange("c (j q) -> c j q", j=ET)).then_inc(
                                   s["got_t_ready"].sem, 1)

                def evacuate_own(i, b, p=p, ph=ph):
                    g = 2 * i + b
                    if ph in s["own_t_ready"].at:
                        wait(act, s["turned"].after(ph, g), s["out_summed"].after(ph, g - 2))
                        A.copy(key[b][D:P, :].rearrange("c (q j) -> c j q", j=ET),
                               bank[b][D:P, :].rearrange("c (j q) -> c j q", j=ET)).then_inc(
                                   s["own_t_ready"].sem, 1)

                def evacuate_nodes(i, b, p=p, ph=ph):
                    g = 2 * i + b
                    if p.nodes:
                        wait(act, s["nturned"].after(ph, g), s["nout_summed"].after(ph, g - 2))
                        for k in range(2 if p.node_q else 1):
                            last = A.copy(nt[b][:, k * 512:(k + 1) * 512], bank[5 + k][:, :])
                        last.then_inc(s["nt_ready"].sem, 1)

                def put_rows(i, b, p=p, ph=ph):
                    if p.build:
                        wait(act, nrows_in.after(ph, i, b), xh_out.before(ph, i, b))
                        A.copy(xh[b][:, :, 0:D], nrows[b][:, :, :]).then_inc(s["xh_rows_put"].sem, 1)

                def message(i, b, p=p, ph=ph):
                    g = 2 * i + b
                    if p.msg is not None:
                        wait(act, s["msg_summed"].after(ph, g), s["agg_ready"].after(ph, g - 2))
                        A.activation(msg_t[b][:, :], bank[2][0:D, :], ACT.Relu,
                                     bias=b_pool_col[:, p.msg:p.msg + 1]).then_inc(s["msg_ready"].sem, 1)
                    if p.rev:
                        wait(act, s["deduped"].after(ph, g))
                        if not isinstance(i, int) or i > 0:
                            act.wait_ge(added, 16 * (COLS * rev_ph.index(ph) + ET * (g - 1)) + 16)
                        A.copy(summed[b][:, :, :].rearrange("p j d -> p (j d)"),
                               bank[2][:, 0:ET * D]).then_inc(s["summed_ready"].sem, 1)

                def squares(i, b, p=p, ph=ph):
                    g = 2 * i + b
                    if p.w:
                        if p.after == "relu":
                            wait(act, s["biased"].after(ph, g))
                            A.activation(res[b][:, :, :], res[b][:, :, :], ACT.Relu).then_inc(s["res_ready"].sem, 1)
                        else:
                            a = res[b][:, :, :]
                            if p.after == "norm_ln":
                                a = bank[3 + b][:, 0:ET * D].rearrange("p (j d) -> p j d", d=D)
                            wait(act, s["out_summed" if p.after == "norm_ln" else "resid_added" if p.resid
                                      else "biased"].after(ph, g), s["var_ready"].after(ph, g - 2))
                            A.activation(sq[b][:, :, :], a, ACT.Square).then_inc(s["squared"].sem, 1)

                def squares_nodes(i, b, p=p, ph=ph):
                    g = 2 * i + b
                    if p.nodes:
                        if p.node_after == "relu":
                            wait(act, s["nbiased"].after(ph, g))
                            A.activation(nres[b][:, :, :], nres[b][:, :, :], ACT.Relu).then_inc(s["nres_ready"].sem, 1)
                        else:
                            a = nres[b][:, :, :]
                            if not p.node_bias:
                                a = nbank(p, b)[:, :].rearrange("p (j d) -> p j d", d=D)
                            wait(act, s["nout_summed" if not p.node_bias else "nresid_added" if p.node_resid
                                      else "nbiased"].after(ph, g), s["nvar_ready"].after(ph, g - 2))
                            A.activation(nsq[b][:, :, :], a, ACT.Square).then_inc(s["nsquared"].sem, 1)

                def roots(i, b, p=p, ph=ph):
                    g = 2 * i + b
                    if ph in s["std_ready"].at:
                        v = "var2" if p.after == "norm_ln" else "var"
                        wait(act, s[v + "_ready"].after(ph, g), s["rstd_ready"].after(ph, g - 1))
                        A.activation(stat["std"][:, :], stat[v][:, :], ACT.Sqrt, bias=eps[:, 0:1],
                                     scale=1.0 / D).then_inc(s["std_ready"].sem, 1)

                def roots_nodes(i, b, p=p, ph=ph):
                    g = 2 * i + b
                    if ph in s["nstd_ready"].at:
                        wait(act, s["nvar_ready"].after(ph, g), s["nrstd_ready"].after(ph, g - 1))
                        A.activation(nstat["std"][:, :], nstat["var"][:, :], ACT.Sqrt, bias=eps[:, 0:1],
                                     scale=1.0 / D).then_inc(s["nstd_ready"].sem, 1)

                if not p.scatter:
                    a = lead(p)
                    if p.rev:
                        run_skewed(act, ((a["message"], message), (a["turn"], evacuate)))
                    else:
                        run_skewed(act, ((0, roots), (a["turn"], evacuate), (0, roots_nodes),
                                         (a["turn"], evacuate_own), (a["post"], squares), (a["message"], message),
                                         (a["post"], squares_nodes), (a["turn_nodes"], evacuate_nodes),
                                         (1, put_rows)))

        @block.vector
        def _(dve):
            V = nc.vector
            link_count = [0]

            def link(ins):
                link_count[0] += 1
                ins.then_inc(links, 1)
                dve.wait_ge(links, link_count[0])

            V.memset(hot_lo[0][0][:, :], 0.0)
            for name in idx_all:
                V.memset(idx_all[name][:, COLS:COLS_BUF], 0)
            V.memset(hot_hi[0][0][:, :], 0.0).then_inc(dve_chain, 1)
            wait(dve, (prep_in, 16 * 5), (pool_built, 2))
            link(V.tensor_copy(count_up[:, :], count_i[:, :]))
            for k in two:
                link(V.tensor_scalar(shifted[:, :], edge_i[k][:, :], P - 1, None, ALU.bitwise_and))
                link(V.tensor_copy(lo_f[k][:, :], shifted[:, :]))
                link(V.tensor_scalar(shifted[:, :], edge_i[k][:, :], 7, None, ALU.arith_shift_right))
                link(V.tensor_copy(hi_f[k][:, :], shifted[:, :]))
            link(V.tensor_copy(idx_all["dst"][:, 0:COLS], edge_i[1][:, :]))
            for b in two:
                V.tensor_copy(ib[b][:, :], idx_all["dst"][:, b * ET:(b + 1) * ET]).then_inc(xa_idx, 1)
            with dve.Fori(0, PAIRS) as i:
                for b in two:
                    g = 2 * i + b
                    for j in range(ET):
                        c = g * ET + j
                        dve.wait_ge(hot_used, c + 1)
                        for k in two:
                            V.tensor_scalar(hot_lo[k][j % 2][:, :], count_up[:, 0:P], lo_f[k][:, bass.ds(c, 1)], None,
                                            ALU.is_equal)
                            last = V.tensor_scalar(hot_hi[k][j % 2][:, :], count_up[:, :], hi_f[k][:, bass.ds(c, 1)],
                                                   None, ALU.is_equal)
                        last.then_inc(hot_ready, 1)
                    dve.wait_ge(xa_in[b], 16 * ET * (i + 1))
                    V.tensor_copy(ib[b][:, :], idx_all["dst"][:, bass.ds((g + 2) * ET, ET)]).then_inc(xa_idx, 1)
            dve.wait_ge(hot_used, COLS + 2)
            V.memset(hot_lo[0][0][:, :], 0.0).then_inc(hot_ready, 1)

            link(V.tensor_copy(idx_all["src"][:, 0:COLS], edge_i[0][:, :]))
            link(V.tensor_copy(src_f[:, 0:COLS], edge_i[0][:, :]))
            link(V.tensor_copy(dst_f[:, :], edge_i[1][:, :]))
            link(V.tensor_tensor(last_f[:, :], edge_i[1][:, :], edge_i[2][:, :], ALU.not_equal))
            link(V.tensor_scalar(dst_f[:, :], dst_f[:, :], float(NODES_PAD), None, ALU.subtract))
            link(V.tensor_tensor(dst_f[:, :], dst_f[:, :], last_f[:, :], ALU.mult))
            link(V.tensor_scalar(idx_all["out"][:, 0:COLS], dst_f[:, :], float(NODES_PAD), None, ALU.add))
            link(V.tensor_copy(spare[:, :], part_i[:, :]))
            link(V.tensor_tensor(same[:, :], drow[:, :], prow[:, :], ALU.is_equal))
            V.tensor_scalar(far[:, :], same[:, :], 1.0, -FAR, ALU.subtract, ALU.mult).then_inc(masks_ready, 1)

            dve.wait_ge(act_chain, 1)
            V.tensor_scalar(field[0][:, :], deg[1][:, :], 1.0, None, ALU.max).then_inc(dve_chain, 1)
            link(V.tensor_scalar(field[1][:, :], deg[0][:, :], 1.0, None, ALU.max))
            link(V.reciprocal(field[1][:, :], field[1][:, :]))
            link(V.tensor_tensor(field[2][:, :], deg[0][:, :], deg[1][:, :], ALU.add))
            link(V.tensor_scalar(field[2][:, :], field[2][:, :], 1.0, None, ALU.max))
            link(V.reciprocal(field[2][:, :], field[2][:, :]))
            dve.wait_ge(pe_chain, 2)
            for h in two:
                cols = slice(h * HALF, (h + 1) * HALF)
                link(V.tensor_copy(prefix[:, cols], bank[6 + h][:, 0:HALF]))
            link(V.tensor_tensor_scan(field[3][:, :], prefix[:, :], zero[:, 0:HI], 0.0, ALU.add, ALU.add))
            link(V.tensor_tensor(field[3][:, :], field[3][:, :], prefix[:, :], ALU.subtract))
            for h in two:
                cols = slice(h * HALF, (h + 1) * HALF)
                link(V.tensor_tensor(field[3][:, cols], field[3][:, cols], bank[4 + h][:, 0:HALF], ALU.add))
            link(V.tensor_copy(prefix[:, :], node_i[:, :]))
            link(V.tensor_scalar(field[3][:, :], field[3][:, :], float(NODES_PAD - 1), None, ALU.add))
            link(V.tensor_tensor(field[3][:, :], field[3][:, :], prefix[:, :], ALU.subtract))
            link(V.tensor_scalar(deg[1][:, :], deg[1][:, :], 1.0, None, ALU.min))
            link(V.tensor_tensor(field[3][:, :], field[3][:, :], deg[1][:, :], ALU.mult))
            link(V.tensor_tensor(field[3][:, :], field[3][:, :], prefix[:, :], ALU.add))
            dve.wait_ge(act_chain, 2)
            V.reciprocal(field[0][:, :], tmp[:, :]).then_inc(dve_chain, 1)
            dve.wait_ge(consts_in, 16 * N_CONSTS)
            link(V.tensor_tensor(brow["l1"][:, :], brow["l1"][:, :], brow["rot"][:, :], ALU.add))
            for k in two:
                half = slice(D * k, D * (k + 1))
                link(V.tensor_copy(stacked["centre"][half, :], eye[half, half]))
                link(V.tensor_copy(pair["centre"][half, half], eye[half, half]))
            link(V.tensor_tensor(stacked["l1"][D:P, :], stacked["l1"][D:P, :], eye[D:P, D:P], ALU.add))
            link(V.tensor_tensor(pair["rot"][:, :], pair["rot"][:, :], eye[:, :], ALU.add))
            for w, halves in ((stacked["centre"], 1), (stacked["l1"], 1), (stacked["w3"], 1), (stacked["conv2"], 1),
                              (pair["centre"], 2), (pair["rot"], 2), (pair["self2"], 2), (brow["l1"], 1),
                              (brow["b3"], 1), (brow["bias2"], 1)):
                a = w[:, :].rearrange("p (k d) -> p k d", d=D)
                m = row_mean[:, 0:halves]
                link(V.tensor_reduce(m, a, AX.X, ALU.add))
                link(V.tensor_scalar(m, m, -1.0 / D, None, ALU.mult))
                link(V.tensor_tensor(a, a, m.unsqueeze(2).to_broadcast([P, halves, D]), ALU.add))
            dve.sem_inc(dve_chain, 1)

            def bc(ap, n):
                return ap.unsqueeze(2).to_broadcast([P, n, D])

            for n, p in enumerate(PHASES):
                ph = p.name

                def fetch_idx(g, b, p=p, ph=ph):
                    cols = bass.ds(g * ET, ET)
                    if p.fwd or p.scatter:
                        V.tensor_copy(ib[b][:, :], idx_all["out" if p.scatter else p.fwd_idx][:, cols]).then_inc(
                            s["idx_ready"].sem, 1)
                    if p.rev:
                        V.tensor_copy(ib2[b][:, :], idx_all["dst_own"][:, cols]).then_inc(s["idx2_ready"].sem, 1)

                def receive(i, b, p=p, ph=ph):
                    g = 2 * i + b
                    if p.scatter:
                        wait(dve, scattered.after(ph, i, b))
                        fetch_idx(g + 2, b)
                        return
                    if p.fwd:
                        wait(dve, gathered(ph).after(ph, i, b))
                    if p.rev:
                        wait(dve, gathered_rev.after(ph, i, b))
                    fetch_idx(g + 2, b)
                    cols = bass.ds(g * ET, ET)
                    if p.build:
                        wait(dve, xh_in.after(ph, i, b), xh_out.before(ph, i, b))
                        V.tensor_copy(xh[b][:, :, D:XW], xh_info[b][:, :].rearrange(
                            "p (j f) -> p j f", f=INFO)).then_inc(s["xh_info_put"].sem, 1)
                        V.tensor_copy(info_dst[:, g, :, :], got[b][:, :, 0:INFO])
                        V.tensor_copy(idx_all["dst_own"][:, cols], got[b][:, :, INFO - 1])
                        V.reciprocal(root[:, g, :], got[b][:, :, 0])
                        V.tensor_tensor(inv_in[:, g, :], got[b][:, :, 0], got[b][:, :, 0], ALU.mult).then_inc(
                            s["got_used"].sem, 1)
                    if p.scale:
                        wait(dve, s["turned"].after(ph, g - 2))
                        if p.after == "norm_ln":
                            wait(dve, rows_in.after(ph, i, b))
                            V.tensor_tensor(stack[b][:, :, D:2 * D], stack[b][:, :, D:2 * D], bc(root[:, g, :], ET),
                                            ALU.mult)
                        f = bc(got[b][:, :, D], ET) if p.scale == "norm" else scale_of(p, p.scale, g)
                        last = V.tensor_tensor(stack[b][:, :, 0:D], got[b][:, :, 0:D], f, ALU.mult)
                        if p.fwd != "XH":
                            last.then_inc(s["got_used"].sem, 1)
                    if p.fwd == "XH":
                        V.tensor_copy(info_src[:, g, :, :], got[b][:, :, D:XW])
                        V.tensor_copy(idx_all["src_own"][:, cols], got[b][:, :, XW - 1]).then_inc(
                            s["got_used"].sem, 1)
                    if p.rev:
                        wait(dve, s["deduped"].after(ph, g - 2))
                        V.tensor_tensor(scaled2[b][:, :, :], got2[b][:, :, :], scale_of(p, p.rev_scale, g),
                                        ALU.mult).then_inc(s["got2_used"].sem, 1)
                        wait(dve, srow_in.after(ph, i, b))
                        for k in range(ET):
                            last = V.tensor_scalar(equal[b][:, k, 0:(k + 1) * P], src_row[b][:, 0:(k + 1) * P],
                                                   src_f[:, bass.ds(g * ET + k, 1)], None, ALU.is_equal)
                        last.then_inc(s["equal_ready"].sem, 1)
                        if not isinstance(i, int) or i > 0:
                            dve.wait_ge(added, 16 * (COLS * rev_ph.index(ph) + ET * (g - 1)) + 16)
                        V.tensor_copy(ib3[b][:, :], idx_all["sum"][:, cols]).then_inc(s["idx3_ready"].sem, 1)

                def rank(i, b, p=p, ph=ph):
                    g = 2 * i + b
                    cols = bass.ds(g * ET, ET)
                    wait(dve, srow_in.after(ph, i, b))
                    for k in range(ET):
                        last = V.scalar_tensor_tensor(
                            out=equal[b][:, k, 0:(k + 1) * P], in0=src_row[b][:, 0:(k + 1) * P],
                            scalar=src_f[:, bass.ds(g * ET + k, 1)], in1=before[:, (ET - 1 - k) * P:EG],
                            op0=ALU.is_equal, op1=ALU.mult)
                    last.then_inc(s["equal_ready"].sem, 1)
                    V.tensor_tensor(dup[:, 1, :], spare[:, :], src_f[:, cols], ALU.subtract).then_inc(
                        s["spare_off"].sem, 1)
                    wait(dve, s["equal_ready"].after(ph, g))
                    for k in range(ET):
                        last = V.tensor_reduce(dup[:, 0, k:k + 1], equal[b][:, k, 0:(k + 1) * P], AX.X, ALU.max)
                    last.then_inc(s["dup_found"].sem, 1)
                    wait(dve, s["spare_off"].after(ph, g), s["dup_found"].after(ph, g))
                    V.tensor_tensor(dup[:, 2, :], dup[:, 0, :], dup[:, 1, :], ALU.mult).then_inc(s["dup_off"].sem, 1)
                    wait(dve, s["dup_off"].after(ph, g))
                    V.tensor_tensor(idx_all["sum"][:, cols], dup[:, 2, :], src_f[:, cols], ALU.add)

                def add_up(i, b, p=p, ph=ph):
                    g = 2 * i + b
                    if p.bias:
                        wait(dve, s["out_summed"].after(ph, g), stored.before(ph, i, b))
                        V.tensor_tensor(res[b][:, :, :], bank[3 + b][:, 0:ET * D].rearrange("p (j d) -> p j d", d=D),
                                        brow[p.bias][:, :].unsqueeze(1).to_broadcast([P, ET, D]),
                                        ALU.add).then_inc(s["biased"].sem, 1)
                    if p.resid:
                        wait(dve, s["biased"].after(ph, g), resid_in.after(ph, i, b))
                        V.tensor_tensor(res[b][:, :, :], res[b][:, :, :], resid[b][:, :, :],
                                        ALU.add).then_inc(s["resid_added"].sem, 1)

                def add_up_nodes(i, b, p=p, ph=ph):
                    g = 2 * i + b
                    if p.node_bias:
                        wait(dve, s["nout_summed"].after(ph, g), nstored.before(ph, i, b))
                        V.tensor_tensor(nres[b][:, :, :], nbank(p, b)[:, :].rearrange("p (j d) -> p j d", d=D),
                                        brow[p.node_bias][:, :].unsqueeze(1).to_broadcast([P, NT, D]),
                                        ALU.add).then_inc(s["nbiased"].sem, 1)
                    if p.node_resid:
                        wait(dve, s["nbiased"].after(ph, g), nresid_in.after(ph, i, b))
                        V.tensor_tensor(nres[b][:, :, :], nres[b][:, :, :], nresid[b][:, :, :],
                                        ALU.add).then_inc(s["nresid_added"].sem, 1)

                def variance(i, b, p=p, ph=ph):
                    g = 2 * i + b
                    if ph in s["squared"].at:
                        wait(dve, s["squared"].after(ph, g), s["std_ready"].after(ph, g - 1))
                        V.tensor_reduce(stat["var"][:, :], sq[b][:, :, :], AX.X, ALU.add).then_inc(
                            s["var_ready"].sem, 1)
                        if p.after == "norm_ln":
                            wait(dve, s["var_ready"].after(ph, g))
                            V.tensor_tensor(stat["var2"][:, :], stat["var"][:, :], inv_in[:, g, :],
                                            ALU.mult).then_inc(s["var2_ready"].sem, 1)

                def variance_nodes(i, b, p=p, ph=ph):
                    g = 2 * i + b
                    if ph in s["nsquared"].at:
                        wait(dve, s["nsquared"].after(ph, g), s["nstd_ready"].after(ph, g - 1))
                        V.tensor_reduce(nstat["var"][:, :], nsq[b][:, :, :], AX.X, ALU.add).then_inc(
                            s["nvar_ready"].sem, 1)

                def normalise(i, b, p=p, ph=ph):
                    g = 2 * i + b
                    if ph in s["std_ready"].at:
                        wait(dve, s["std_ready"].after(ph, g))
                        V.reciprocal(stat["rstd"][:, :], stat["std"][:, :]).then_inc(s["rstd_ready"].sem, 1)
                        wait(dve, s["rstd_ready"].after(ph, g))
                        a, r = res[b][:, :, :], stat["rstd"]
                        if p.after == "norm_ln":
                            V.tensor_tensor(stat["rstd2"][:, :], stat["rstd"][:, :], info_dst[:, g, :, 0],
                                            ALU.mult).then_inc(s["rstd2_ready"].sem, 1)
                            wait(dve, s["rstd2_ready"].after(ph, g), stored.before(ph, i, b))
                            a, r = bank[3 + b][:, 0:ET * D].rearrange("p (j d) -> p j d", d=D), stat["rstd2"]
                        V.tensor_tensor(res[b][:, :, :], a, bc(r[:, :], ET), ALU.mult).then_inc(
                            s["res_ready"].sem, 1)

                def normalise_nodes(i, b, p=p, ph=ph):
                    g = 2 * i + b
                    if ph in s["nstd_ready"].at:
                        wait(dve, s["nstd_ready"].after(ph, g))
                        V.reciprocal(nstat["rstd"][:, :], nstat["std"][:, :]).then_inc(s["nrstd_ready"].sem, 1)
                        wait(dve, s["nrstd_ready"].after(ph, g))
                        a = nres[b][:, :, :]
                        if not p.node_bias:
                            wait(dve, nstored.before(ph, i, b))
                            a = nbank(p, b)[:, :].rearrange("p (j d) -> p j d", d=D)
                        V.tensor_tensor(nres[b][:, :, :], a, bc(nstat["rstd"][:, :], NT), ALU.mult).then_inc(
                            s["nres_ready"].sem, 1)

                def scan(i, b, p=p, ph=ph):
                    g = 2 * i + b
                    if ph in s["agg_ready"].at:
                        a = got_t[b] if p.msg is None else msg_t[b]
                        wait(dve, s["got_t_ready" if p.msg is None else "msg_ready"].after(ph, g),
                             side_in.after(ph, i, b))
                        if p.keep:
                            wait(dve, stored.before(ph, i, b))
                        else:
                            wait(dve, s["out_summed"].after(ph, g - 2))
                        wait(dve, s["agg_ready"].after(ph, g - 1))
                        if p.agg == "add":
                            last = V.tensor_tensor(key[b][0:D, :], got_t[b][:, :], side[b][:, :], ALU.add)
                        else:
                            last = V.tensor_tensor_scan(key[b][0:D, :], side[b][:, :], a[:, :],
                                                        key[1 - b][0:D, EG - 1:EG], p.agg[0], p.agg[1])
                        last.then_inc(s["agg_ready"].sem, 1)

                if n:
                    barrier(dve, n)
                for b in two:
                    fetch_idx(b, b)
                if p.scatter:
                    with dve.Fori(0, PAIRS - 1) as i:
                        for b in two:
                            receive(i, b)
                else:
                    a = lead(p)
                    if p.rev:
                        order = [(a["scan"], scan), (a["receive"], receive)]
                    elif p.build:
                        order = [(0, variance_nodes), (a["receive"], receive), (0, normalise_nodes)]
                    else:
                        order = [(a["scan"], scan), (0, variance), (0, variance_nodes), (a["post"], add_up),
                                 (0, normalise), (a["post"], add_up_nodes), (0, normalise_nodes),
                                 (a["receive"], receive)]
                    if ph == "l2a":
                        order.append((2, rank))
                    run_skewed(dve, order)


def kernel(x, src, dst, L1_gnn_W_lin, L1_gnn_b_lin, L1_gnn_W_rot, L1_gnn_b_rot, L2_gnn_W1, L2_gnn_b1, L2_gnn_W2,
           L2_gnn_b2, L2_gnn_W3, L2_gnn_b3, L3_gnn_W_pool, L3_gnn_b_pool, L3_gnn_W_self, L3_gnn_W_neigh, L3_gnn_bias):
    import numpy as np
    import concourse.bacc as bacc
    from concourse.bass_utils import run_bass_kernel_spmd as run

    def edges(a, pad):
        return np.concatenate([np.asarray(a), np.full(pad, NODES, a.dtype)])

    def by_partition(e):
        return np.ascontiguousarray(e.reshape(GROUPS, P, ET).transpose(1, 0, 2).reshape(P, COLS))

    src, dst = np.asarray(src), np.asarray(dst)
    pad = EDGES_PAD - EDGES
    s, d = edges(src, pad), edges(dst, pad)
    nxt = np.concatenate([d[1:], np.full(1, -1, d.dtype)])
    prev = np.concatenate([np.full(1, -1, d.dtype), d[:-1]])
    xp = np.zeros((NODES_PAD, D), np.float32)
    xp[:NODES] = x
    row = lambda v: np.asarray(v).reshape(1, D)
    ins = {
        "x": xp, "src_e": by_partition(s), "dst_e": by_partition(d), "next_e": by_partition(nxt),
        "src_tiles": np.ascontiguousarray(s.reshape(GROUPS, P, ET).transpose(0, 2, 1).reshape(GROUPS, 1, EG)),
        "dst_rows": d.reshape(GROUPS, EG), "prev_rows": prev.reshape(GROUPS, EG),
        "w_lin": np.ascontiguousarray(np.asarray(L1_gnn_W_lin).T), "b_lin": row(L1_gnn_b_lin),
        "w_rot": np.ascontiguousarray(np.asarray(L1_gnn_W_rot).T), "b_rot": row(L1_gnn_b_rot),
        "w1": L2_gnn_W1, "b1": row(L2_gnn_b1), "w2": L2_gnn_W2, "b2": row(L2_gnn_b2), "w3": L2_gnn_W3,
        "b3": row(L2_gnn_b3), "w_pool": L3_gnn_W_pool, "b_pool": np.ascontiguousarray(np.asarray(L3_gnn_b_pool).T),
        "w_self": L3_gnn_W_self, "w_neigh": L3_gnn_W_neigh, "bias": L3_gnn_bias,
    }
    nc = bacc.Bacc("TRN2", target_bir_lowering=False, num_devices=1)
    arrays, args = {}, []
    for name, a in ins.items():
        a = np.ascontiguousarray(a)
        arrays[f"in_{name}"] = a
        args.append(nc.dram_tensor(f"in_{name}", a.shape, mybir.dt.from_np(a.dtype), kind="ExternalInput").ap())
    args.append(nc.dram_tensor("out_rows", (NODES_PAD, D), F32, kind="ExternalOutput").ap())
    graph_kernel(nc, *args)
    r = run(nc, [arrays], core_ids=[0])
    return r.results[0]["out_rows"][:NODES]
```
